# Optimizing a Trainium2 kernel written in Bass

```python
import numpy as np
import jax
import jax.numpy as jnp

def _softmax(x, axis=-1):
    return jax.nn.softmax(x, axis=axis)

def _gelu(x):
    return jax.nn.gelu(x, approximate=True)

def _silu(x):
    return jax.nn.silu(x)

def _sigmoid(x):
    return jax.nn.sigmoid(x)

def _layernorm(x, axis=-1, eps=1e-05):
    m = jnp.mean(x, axis=axis, keepdims=True)
    v = jnp.var(x, axis=axis, keepdims=True)
    return (x - m) / jnp.sqrt(v + eps)

def _scatter_add(tgt, idx, src, axis=0):
    return tgt.at[idx].add(src)

def _segment_sum(src, seg, n):
    return jax.ops.segment_sum(src, seg, n)
kernel_name = 'mk_flamingo_gated_d4_seqx_r8_fcdc11'

def setup_inputs(seed: int=0):
    np.random.seed(seed)
    _w = jnp.asarray

    def _rec_inputs():
        import jax
        import jax.numpy as jnp
        _rk = jax.random.key(seed)
        x = 7.22e-05 + 1 * jax.random.normal(jax.random.fold_in(_rk, 1), (2, 512, 128), jnp.float32)
        _lenS = 512 - jax.random.randint(jax.random.fold_in(_rk, 7), (2,), 0, max(1, 512 // 4) + 1, jnp.int32)
        _lenS2 = 154 - jax.random.randint(jax.random.fold_in(_rk, 8), (2,), 0, max(1, 154 // 4) + 1, jnp.int32)
        _ctx_1024P = jax.random.normal(jax.random.fold_in(_rk, 11), (2, 16, 128), jnp.float32)
        _ctx_1024c = jax.random.dirichlet(jax.random.fold_in(_rk, 511), 0.3 * jnp.ones((16,), jnp.float32), (2, 154))
        _ctx_1024t = jnp.einsum('bsk,bkd->bsd', _ctx_1024c, _ctx_1024P)
        _ctx_1024t = _ctx_1024t * jax.lax.rsqrt(jnp.mean(jnp.square(_ctx_1024t)) + 1e-12) * 0.953939
        ctx_1024 = 4.13588e-05 + 0.999923 * (_ctx_1024t + 0.3 * jax.random.normal(jax.random.fold_in(_rk, 611), (2, 154, 128), jnp.float32))
        fside_Bx16xSxS2_0 = 1.50688e-05 + 0.100006 * jax.random.normal(jax.random.fold_in(_rk, 12), (2, 16, 512, 154), jnp.float32)
        fside_BxSxS2_0 = -1.47943e-05 + 1.00017 * jax.random.normal(jax.random.fold_in(_rk, 14), (2, 512, 154), jnp.float32)
        _validS = jnp.arange(512)[None, :] < _lenS[:, None]
        _validS2 = jnp.arange(154)[None, :] < _lenS2[:, None]
        _causal = jnp.tril(jnp.ones((512, 512), dtype=bool))
        mask_BxS2_bk0 = jnp.logical_not(jnp.broadcast_to(_validS2[:, :], (2, 154)))
        mask_BxS2_ik0 = jnp.where(jnp.broadcast_to(_validS2[:, :], (2, 154)), 0, 1).astype(jnp.int32)
        _g = jax.random.normal(jax.random.fold_in(_rk, 9001), (2, 4), jnp.float32)
        _g = jnp.sign(_g) * jnp.maximum(jnp.abs(_g), 1.0) + (_g == 0) * 1.0
        g_xattn = _g[0]
        g_ffn = _g[1]
        return (x, ctx_1024, fside_Bx16xSxS2_0, fside_BxSxS2_0, mask_BxS2_bk0, mask_BxS2_ik0, g_xattn, g_ffn)
    x, ctx_1024, fside_Bx16xSxS2_0, fside_BxSxS2_0, mask_BxS2_bk0, mask_BxS2_ik0, g_xattn, g_ffn = _rec_inputs()

    def _L0_xattn_setup():
        import jax, jax.numpy as jnp
        import numpy as np
        HEADS = 8
        DIM_HEAD = 64
        SCALE = DIM_HEAD ** (-0.5)
        QUERY_DIM = 128
        COND_DIM = 128
        INNER_DIM = DIM_HEAD * HEADS * 2
        key = jax.random.key(seed)
        ks = jax.random.split(key, 7)
        B, Nq, Nk = (4, 256, 256)
        x = jax.random.normal(ks[0], (B, Nq, QUERY_DIM), dtype=jnp.float32)
        cond = jax.random.normal(ks[1], (B, Nk, COND_DIM), dtype=jnp.float32)
        s = 0.02
        Wq = jax.random.normal(ks[2], (QUERY_DIM, INNER_DIM), dtype=jnp.float32) * s
        Wk = jax.random.normal(ks[3], (COND_DIM, INNER_DIM), dtype=jnp.float32) * s
        Wv = jax.random.normal(ks[4], (COND_DIM, INNER_DIM), dtype=jnp.float32) * s
        Wo = jax.random.normal(ks[5], (INNER_DIM, QUERY_DIM), dtype=jnp.float32) * s
        bo = jax.random.normal(ks[6], (QUERY_DIM,), dtype=jnp.float32) * s
        return {'x': x, 'cond': cond, 'Wq': Wq, 'Wk': Wk, 'Wv': Wv, 'Wo': Wo, 'bo': bo}
    _L0_xattn_all = _L0_xattn_setup()
    _L0_xattn_in = {k: v for k, v in _L0_xattn_all.items() if k in ('Wq', 'Wk', 'Wv', 'Wo', 'bo')}
    del _L0_xattn_all

    def _L0_ffn_setup():
        import jax, jax.numpy as jnp
        import numpy as np
        TOP_K = 2
        key = jax.random.key(seed)
        k1, k2, k3 = jax.random.split(key, 3)
        B, S, H, E, D = (4, 128, 128, 32, 128)
        x = jax.random.normal(k1, (B, S, H), dtype=jnp.float32)
        router_w = jax.random.normal(k2, (E, H), dtype=jnp.float32) * (1.0 / np.sqrt(H))
        bound = float(np.sqrt(6.0 / ((1.0 + 0.01 ** 2) * H)))
        expert_weights = jax.random.uniform(k3, (E, H, D), dtype=jnp.float32, minval=-bound, maxval=bound)
        return {'x': x, 'router_w': router_w, 'expert_weights': expert_weights}
    _L0_ffn_all = _L0_ffn_setup()
    _L0_ffn_in = {k: v for k, v in _L0_ffn_all.items() if k in ('router_w', 'expert_weights')}
    del _L0_ffn_all

    def _L1_xattn_setup():
        import jax, jax.numpy as jnp
        import numpy as np
        B, NQ, NK, D, H = (2, 128, 256, 128, 16)
        HD = D // H
        SCALE = HD ** (-0.5)
        key = jax.random.key(seed)
        ks = jax.random.split(key, 14)
        inp = {'query': jax.random.normal(ks[0], (B, NQ, D), jnp.float32), 'key': jax.random.normal(ks[1], (B, NK, D), jnp.float32), 'value': jax.random.normal(ks[2], (B, NK, D), jnp.float32), 'attn_bias': jax.random.normal(ks[3], (B, H, NQ, NK), jnp.float32) * 0.1, 'key_padding_mask': jax.random.bernoulli(ks[4], 0.1, (B, NK))}
        s = D ** (-0.5)
        inp['Wq'] = jax.random.normal(ks[5], (D, D), jnp.float32) * s
        inp['bq'] = jnp.zeros((D,), jnp.float32)
        inp['Wk'] = jax.random.normal(ks[6], (D, D), jnp.float32) * s
        inp['bk'] = jnp.zeros((D,), jnp.float32)
        inp['Wv'] = jax.random.normal(ks[7], (D, D), jnp.float32) * s
        inp['bv'] = jnp.zeros((D,), jnp.float32)
        inp['Wo'] = jax.random.normal(ks[8], (D, D), jnp.float32) * s
        inp['bo'] = jnp.zeros((D,), jnp.float32)
        return inp
    _L1_xattn_all = _L1_xattn_setup()
    _L1_xattn_in = {k: v for k, v in _L1_xattn_all.items() if k in ('Wq', 'bq', 'Wk', 'bk', 'Wv', 'bv', 'Wo', 'bo')}
    del _L1_xattn_all

    def _L1_ffn_setup():
        import jax, jax.numpy as jnp
        import numpy as np
        D_MODEL, D_FF, RANK = (128, 512, 32)
        B, S = (4, 512)
        key = jax.random.key(seed)
        ks = jax.random.split(key, 7)
        return {'x': jax.random.normal(ks[0], (B, S, D_MODEL), dtype=jnp.float32), 'U1': jax.random.normal(ks[1], (D_MODEL, RANK), dtype=jnp.float32) * 0.02, 'V1': jax.random.normal(ks[2], (RANK, D_FF), dtype=jnp.float32) * 0.02, 'b1': jnp.zeros((D_FF,), dtype=jnp.float32), 'U2': jax.random.normal(ks[3], (D_FF, RANK), dtype=jnp.float32) * 0.02, 'V2': jax.random.normal(ks[4], (RANK, D_MODEL), dtype=jnp.float32) * 0.02, 'b2': jnp.zeros((D_MODEL,), dtype=jnp.float32)}
    _L1_ffn_all = _L1_ffn_setup()
    _L1_ffn_in = {k: v for k, v in _L1_ffn_all.items() if k in ('U1', 'V1', 'b1', 'U2', 'V2', 'b2')}
    del _L1_ffn_all

    def _L2_xattn_setup():
        import jax, jax.numpy as jnp
        import numpy as np
        D = 128
        key = jax.random.key(seed)
        ks = jax.random.split(key, 13)
        B, S, d = (4, 256, D)
        inp = {'q_in': jax.random.normal(ks[0], (B, S, d), jnp.float32), 'k_in': jax.random.normal(ks[1], (B, S, d), jnp.float32), 'v_in': jax.random.normal(ks[2], (B, S, d), jnp.float32), 'phi_risk': jax.random.normal(ks[3], (B, S, S), jnp.float32), 'phi_prio': jax.random.normal(ks[4], (B, S, S), jnp.float32), 'phi_impl': jax.random.normal(ks[5], (B, S, S), jnp.float32), 'Wq': jax.random.normal(ks[6], (d, d), jnp.float32) / np.sqrt(d), 'bq': jax.random.normal(ks[7], (d,), jnp.float32) * 0.01, 'Wk': jax.random.normal(ks[8], (d, d), jnp.float32) / np.sqrt(d), 'bk': jax.random.normal(ks[9], (d,), jnp.float32) * 0.01, 'Wv': jax.random.normal(ks[10], (d, d), jnp.float32) / np.sqrt(d), 'bv': jax.random.normal(ks[11], (d,), jnp.float32) * 0.01, 'beta_risk': jnp.float32(0.1), 'beta_prio': jnp.float32(0.1), 'beta_impl': jnp.float32(0.1)}
        return inp
    _L2_xattn_all = _L2_xattn_setup()
    _L2_xattn_in = {k: v for k, v in _L2_xattn_all.items() if k in ('Wq', 'bq', 'Wk', 'bk', 'Wv', 'bv', 'beta_risk', 'beta_prio', 'beta_impl')}
    del _L2_xattn_all

    def _L2_ffn_setup():
        import jax, jax.numpy as jnp
        import numpy as np
        FP8_E4M3_MAX = 448.0

        def fake_quant_fp8(t):
            amax = jnp.max(jnp.abs(t))
            scale = FP8_E4M3_MAX / jnp.maximum(amax, 1e-12)
            q = (t * scale).astype(jnp.float8_e4m3fn).astype(jnp.float32)
            return q / scale
        key = jax.random.key(seed)
        k1, k2, k3 = jax.random.split(key, 3)
        d_in, d_out = (128, 128)
        x = jax.random.normal(k1, (4, 1024, d_in), dtype=jnp.float32)
        weight = jax.random.normal(k2, (d_out, d_in), dtype=jnp.float32) * (1.0 / np.sqrt(d_in))
        bias = jax.random.normal(k3, (d_out,), dtype=jnp.float32) * 0.01
        return {'x': x, 'weight': weight, 'bias': bias}
    _L2_ffn_all = _L2_ffn_setup()
    _L2_ffn_in = {k: v for k, v in _L2_ffn_all.items() if k in ('weight', 'bias')}
    del _L2_ffn_all

    def _L3_xattn_setup():
        import jax, jax.numpy as jnp
        import numpy as np
        B, LQ, LK, D = (4, 256, 256, 128)
        H = 16
        HD = D // H

        def _split_heads(x):
            b, l, _ = x.shape
            return x.reshape(b, l, H, HD).transpose(0, 2, 1, 3)
        key = jax.random.key(seed)
        ks = jax.random.split(key, 10)
        s = 0.02
        return {'hidden_states': jax.random.normal(ks[0], (B, LQ, D), jnp.float32), 'context': jax.random.normal(ks[1], (B, LK, D), jnp.float32), 'attention_mask': jax.random.randint(ks[2], (B, LK), 0, 2, jnp.int32), 'q_w': jax.random.normal(ks[3], (D, D), jnp.float32) * s, 'q_b': jnp.zeros((D,), jnp.float32), 'k_w': jax.random.normal(ks[4], (D, D), jnp.float32) * s, 'k_b': jnp.zeros((D,), jnp.float32), 'v_w': jax.random.normal(ks[5], (D, D), jnp.float32) * s, 'v_b': jnp.zeros((D,), jnp.float32)}
    _L3_xattn_all = _L3_xattn_setup()
    _L3_xattn_in = {k: v for k, v in _L3_xattn_all.items() if k in ('q_w', 'q_b', 'k_w', 'k_b', 'v_w', 'v_b')}
    del _L3_xattn_all

    def _L3_ffn_setup():
        import jax, jax.numpy as jnp
        import numpy as np
        B, S, D = (4, 256, 128)
        DFF = 64
        E = 16
        TOP_K = 2
        N_SHARED = 2
        FUSED_DFF = DFF * N_SHARED
        key = jax.random.key(seed)
        ks = jax.random.split(key, 16)
        sc_d = 1.0 / np.sqrt(D)
        sc_f = 1.0 / np.sqrt(DFF)
        sc_sf = 1.0 / np.sqrt(FUSED_DFF)
        inp = {'x': jax.random.normal(ks[0], (B, S, D), dtype=jnp.float32), 'gate_w': jax.random.uniform(ks[1], (E, D), dtype=jnp.float32, minval=-sc_d, maxval=sc_d), 'expert_bias': jnp.zeros((E,), dtype=jnp.float32), 'w1': jax.random.uniform(ks[2], (E, DFF, D), dtype=jnp.float32, minval=-sc_d, maxval=sc_d), 'b1': jax.random.uniform(ks[3], (E, DFF), dtype=jnp.float32, minval=-sc_d, maxval=sc_d), 'w3': jax.random.uniform(ks[4], (E, DFF, D), dtype=jnp.float32, minval=-sc_d, maxval=sc_d), 'b3': jax.random.uniform(ks[5], (E, DFF), dtype=jnp.float32, minval=-sc_d, maxval=sc_d), 'w2': jax.random.uniform(ks[6], (E, D, DFF), dtype=jnp.float32, minval=-sc_f, maxval=sc_f), 'b2': jax.random.uniform(ks[7], (E, D), dtype=jnp.float32, minval=-sc_f, maxval=sc_f), 'sw1': jax.random.uniform(ks[8], (FUSED_DFF, D), dtype=jnp.float32, minval=-sc_d, maxval=sc_d), 'sb1': jax.random.uniform(ks[9], (FUSED_DFF,), dtype=jnp.float32, minval=-sc_d, maxval=sc_d), 'sw3': jax.random.uniform(ks[10], (FUSED_DFF, D), dtype=jnp.float32, minval=-sc_d, maxval=sc_d), 'sb3': jax.random.uniform(ks[11], (FUSED_DFF,), dtype=jnp.float32, minval=-sc_d, maxval=sc_d), 'sw2': jax.random.uniform(ks[12], (D, FUSED_DFF), dtype=jnp.float32, minval=-sc_sf, maxval=sc_sf), 'sb2': jax.random.uniform(ks[13], (D,), dtype=jnp.float32, minval=-sc_sf, maxval=sc_sf)}
        return inp
    _L3_ffn_all = _L3_ffn_setup()
    _L3_ffn_in = {k: v for k, v in _L3_ffn_all.items() if k in ('gate_w', 'expert_bias', 'w1', 'b1', 'w2', 'b2', 'w3', 'b3', 'sw1', 'sb1', 'sw2', 'sb2', 'sw3', 'sb3')}
    del _L3_ffn_all
    return {'x': x, 'ctx_1024': ctx_1024, 'fside_Bx16xSxS2_0': fside_Bx16xSxS2_0, 'fside_BxSxS2_0': fside_BxSxS2_0, 'mask_BxS2_bk0': mask_BxS2_bk0, 'mask_BxS2_ik0': mask_BxS2_ik0, 'g_xattn': g_xattn, 'g_ffn': g_ffn, 'L0_xattn_Wq': _L0_xattn_in['Wq'], 'L0_xattn_Wk': _L0_xattn_in['Wk'], 'L0_xattn_Wv': _L0_xattn_in['Wv'], 'L0_xattn_Wo': _L0_xattn_in['Wo'], 'L0_xattn_bo': _L0_xattn_in['bo'], 'L0_ffn_router_w': _L0_ffn_in['router_w'], 'L0_ffn_expert_weights': _L0_ffn_in['expert_weights'], 'L1_xattn_Wq': _L1_xattn_in['Wq'], 'L1_xattn_bq': _L1_xattn_in['bq'], 'L1_xattn_Wk': _L1_xattn_in['Wk'], 'L1_xattn_bk': _L1_xattn_in['bk'], 'L1_xattn_Wv': _L1_xattn_in['Wv'], 'L1_xattn_bv': _L1_xattn_in['bv'], 'L1_xattn_Wo': _L1_xattn_in['Wo'], 'L1_xattn_bo': _L1_xattn_in['bo'], 'L1_ffn_U1': _L1_ffn_in['U1'], 'L1_ffn_V1': _L1_ffn_in['V1'], 'L1_ffn_b1': _L1_ffn_in['b1'], 'L1_ffn_U2': _L1_ffn_in['U2'], 'L1_ffn_V2': _L1_ffn_in['V2'], 'L1_ffn_b2': _L1_ffn_in['b2'], 'L2_xattn_Wq': _L2_xattn_in['Wq'], 'L2_xattn_bq': _L2_xattn_in['bq'], 'L2_xattn_Wk': _L2_xattn_in['Wk'], 'L2_xattn_bk': _L2_xattn_in['bk'], 'L2_xattn_Wv': _L2_xattn_in['Wv'], 'L2_xattn_bv': _L2_xattn_in['bv'], 'L2_xattn_beta_risk': _L2_xattn_in['beta_risk'], 'L2_xattn_beta_prio': _L2_xattn_in['beta_prio'], 'L2_xattn_beta_impl': _L2_xattn_in['beta_impl'], 'L2_ffn_weight': _L2_ffn_in['weight'], 'L2_ffn_bias': _L2_ffn_in['bias'], 'L3_xattn_q_w': _L3_xattn_in['q_w'], 'L3_xattn_q_b': _L3_xattn_in['q_b'], 'L3_xattn_k_w': _L3_xattn_in['k_w'], 'L3_xattn_k_b': _L3_xattn_in['k_b'], 'L3_xattn_v_w': _L3_xattn_in['v_w'], 'L3_xattn_v_b': _L3_xattn_in['v_b'], 'L3_ffn_gate_w': _L3_ffn_in['gate_w'], 'L3_ffn_expert_bias': _L3_ffn_in['expert_bias'], 'L3_ffn_w1': _L3_ffn_in['w1'], 'L3_ffn_b1': _L3_ffn_in['b1'], 'L3_ffn_w2': _L3_ffn_in['w2'], 'L3_ffn_b2': _L3_ffn_in['b2'], 'L3_ffn_w3': _L3_ffn_in['w3'], 'L3_ffn_b3': _L3_ffn_in['b3'], 'L3_ffn_sw1': _L3_ffn_in['sw1'], 'L3_ffn_sb1': _L3_ffn_in['sb1'], 'L3_ffn_sw2': _L3_ffn_in['sw2'], 'L3_ffn_sb2': _L3_ffn_in['sb2'], 'L3_ffn_sw3': _L3_ffn_in['sw3'], 'L3_ffn_sb3': _L3_ffn_in['sb3']}

def reference(x, ctx_1024, fside_Bx16xSxS2_0, fside_BxSxS2_0, mask_BxS2_bk0, mask_BxS2_ik0, g_xattn, g_ffn, L0_xattn_Wq, L0_xattn_Wk, L0_xattn_Wv, L0_xattn_Wo, L0_xattn_bo, L0_ffn_router_w, L0_ffn_expert_weights, L1_xattn_Wq, L1_xattn_bq, L1_xattn_Wk, L1_xattn_bk, L1_xattn_Wv, L1_xattn_bv, L1_xattn_Wo, L1_xattn_bo, L1_ffn_U1, L1_ffn_V1, L1_ffn_b1, L1_ffn_U2, L1_ffn_V2, L1_ffn_b2, L2_xattn_Wq, L2_xattn_bq, L2_xattn_Wk, L2_xattn_bk, L2_xattn_Wv, L2_xattn_bv, L2_xattn_beta_risk, L2_xattn_beta_prio, L2_xattn_beta_impl, L2_ffn_weight, L2_ffn_bias, L3_xattn_q_w, L3_xattn_q_b, L3_xattn_k_w, L3_xattn_k_b, L3_xattn_v_w, L3_xattn_v_b, L3_ffn_gate_w, L3_ffn_expert_bias, L3_ffn_w1, L3_ffn_b1, L3_ffn_w2, L3_ffn_b2, L3_ffn_w3, L3_ffn_b3, L3_ffn_sw1, L3_ffn_sb1, L3_ffn_sw2, L3_ffn_sb2, L3_ffn_sw3, L3_ffn_sb3):
    import jax
    import jax.numpy as jnp

    def _L0_xattn_ref(x, cond, Wq, Wk, Wv, Wo, bo):
        import jax, jax.numpy as jnp
        import numpy as np
        HEADS = 8
        DIM_HEAD = 64
        SCALE = DIM_HEAD ** (-0.5)
        QUERY_DIM = 128
        COND_DIM = 128
        INNER_DIM = DIM_HEAD * HEADS * 2
        B, Nq, _ = x.shape
        Nk = cond.shape[1]
        h = HEADS
        d = INNER_DIM // h
        q = (x @ Wq).reshape(B, Nq, h, d).transpose(0, 2, 1, 3)
        k = (cond @ Wk).reshape(B, Nk, h, d).transpose(0, 2, 1, 3)
        v = (cond @ Wv).reshape(B, Nk, h, d).transpose(0, 2, 1, 3)
        sim = jnp.einsum('bhid,bhjd->bhij', q, k) * SCALE
        attn = jax.nn.softmax(sim, axis=-1)
        out = jnp.einsum('bhij,bhjd->bhid', attn, v)
        out = out.transpose(0, 2, 1, 3).reshape(B, Nq, INNER_DIM)
        return out @ Wo + bo

    def _L0_ffn_ref(x, router_w, expert_weights):
        import jax, jax.numpy as jnp
        import numpy as np
        TOP_K = 2
        B, S, H = x.shape
        E = router_w.shape[0]
        T = B * S
        logits = jnp.einsum('bsh,eh->bse', x, router_w)
        rw = jax.nn.softmax(logits, axis=-1).reshape(T, E)
        x_flat = x.reshape(T, H)
        vals, idx = jax.lax.top_k(rw, TOP_K)
        w_masked = jnp.zeros_like(rw).at[jnp.arange(T)[:, None], idx].set(vals)

        def body(acc, we):
            w_e, W_e = we
            return (acc + x_flat * w_e[:, None] @ W_e, None)
        out_flat, _ = jax.lax.scan(body, jnp.zeros((T, H), dtype=x.dtype), (w_masked.T, expert_weights))
        return out_flat.reshape(B, S, H)

    def _L1_xattn_ref(query, key, value, attn_bias, key_padding_mask, Wq, bq, Wk, bk, Wv, bv, Wo, bo):
        import jax, jax.numpy as jnp
        import numpy as np
        B, NQ, NK, D, H = (2, 128, 256, 128, 16)
        HD = D // H
        SCALE = HD ** (-0.5)
        b, nq, d = query.shape
        nk = key.shape[1]
        q = (query @ Wq + bq).reshape(b, nq, H, HD).transpose(0, 2, 1, 3)
        k = (key @ Wk + bk).reshape(b, nk, H, HD).transpose(0, 2, 1, 3)
        v = (value @ Wv + bv).reshape(b, nk, H, HD).transpose(0, 2, 1, 3)
        logits = jnp.einsum('bhqd,bhkd->bhqk', q, k) * SCALE + attn_bias
        all_masked = jnp.all(key_padding_mask, axis=1)
        safe_mask = key_padding_mask.at[:, 0].set(jnp.where(all_masked, False, key_padding_mask[:, 0]))
        logits = jnp.where(safe_mask[:, None, None, :], -jnp.inf, logits)
        attn = jax.nn.softmax(logits, axis=-1)
        out = jnp.einsum('bhqk,bhkd->bhqd', attn, v)
        out = out.transpose(0, 2, 1, 3).reshape(b, nq, d)
        return out @ Wo + bo

    def _L1_ffn_ref(x, U1, V1, b1, U2, V2, b2):
        import jax, jax.numpy as jnp
        import numpy as np
        D_MODEL, D_FF, RANK = (128, 512, 32)
        B, S = (4, 512)
        P = jnp.einsum('bsd,dr->bsr', x, U1)
        H = jax.nn.gelu(jnp.einsum('bsr,rf->bsf', P, V1) + b1)
        Q = jnp.einsum('bsf,fr->bsr', H, U2)
        return jnp.einsum('bsr,rd->bsd', Q, V2) + b2

    def _L2_xattn_ref(q_in, k_in, v_in, phi_risk, phi_prio, phi_impl, Wq, bq, Wk, bk, Wv, bv, beta_risk, beta_prio, beta_impl):
        import jax, jax.numpy as jnp
        import numpy as np
        D = 128
        d = q_in.shape[-1]
        scale = jnp.asarray(d, q_in.dtype) ** (-0.5)
        Q = q_in @ Wq.T + bq
        K = k_in @ Wk.T + bk
        V = v_in @ Wv.T + bv
        att = jnp.einsum('bsd,btd->bst', Q, K) * scale
        att = att + beta_risk * phi_risk + beta_prio * phi_prio - beta_impl * phi_impl
        w = jax.nn.softmax(att, axis=-1)
        return jnp.einsum('bst,btd->bsd', w, V)

    def _L2_ffn_ref(x, weight, bias):
        import jax, jax.numpy as jnp
        import numpy as np
        FP8_E4M3_MAX = 448.0

        def fake_quant_fp8(t):
            amax = jnp.max(jnp.abs(t))
            scale = FP8_E4M3_MAX / jnp.maximum(amax, 1e-12)
            q = (t * scale).astype(jnp.float8_e4m3fn).astype(jnp.float32)
            return q / scale
        xq = fake_quant_fp8(x)
        wq = fake_quant_fp8(weight)
        return jnp.einsum('bsd,od->bso', xq, wq) + bias

    def _L3_xattn_ref(hidden_states, context, attention_mask, q_w, q_b, k_w, k_b, v_w, v_b):
        import jax, jax.numpy as jnp
        import numpy as np
        B, LQ, LK, D = (4, 256, 256, 128)
        H = 16
        HD = D // H

        def _split_heads(x):
            b, l, _ = x.shape
            return x.reshape(b, l, H, HD).transpose(0, 2, 1, 3)
        q = _split_heads(hidden_states @ q_w.T + q_b)
        k = _split_heads(context @ k_w.T + k_b)
        v = _split_heads(context @ v_w.T + v_b)
        scores = jnp.einsum('bhqd,bhkd->bhqk', q, k) / jnp.sqrt(jnp.float32(HD))
        mask = (attention_mask > 0)[:, None, None, :]
        scores = jnp.where(mask, -jnp.inf, scores)
        probs = jax.nn.softmax(scores, axis=-1)
        ctx = jnp.einsum('bhqk,bhkd->bhqd', probs, v)
        ctx = ctx.transpose(0, 2, 1, 3).reshape(ctx.shape[0], ctx.shape[2], H * HD)
        return ctx

    def _L3_ffn_ref(x, gate_w, expert_bias, w1, b1, w2, b2, w3, b3, sw1, sb1, sw2, sb2, sw3, sb3):
        import jax, jax.numpy as jnp
        import numpy as np
        B, S, D = (4, 256, 128)
        DFF = 64
        E = 16
        TOP_K = 2
        N_SHARED = 2
        FUSED_DFF = DFF * N_SHARED
        Bv, Sv, Dv = x.shape
        xf = x.reshape(-1, Dv)
        logits = xf @ gate_w.T
        scores = jax.nn.sigmoid(logits)
        biased = logits + expert_bias.astype(logits.dtype)[None, :]
        _, topk_idx = jax.lax.top_k(biased, TOP_K)
        topk_w = jnp.take_along_axis(scores, topk_idx, axis=-1)
        topk_w = topk_w / (topk_w.sum(-1, keepdims=True) + 1e-10)
        gatew = (jax.nn.one_hot(topk_idx, E, dtype=xf.dtype) * topk_w[..., None]).sum(1)
        y = jnp.zeros_like(xf)
        for e in range(E):
            h = jax.nn.silu(xf @ w1[e].T + b1[e]) * (xf @ w3[e].T + b3[e])
            y = y + gatew[:, e:e + 1] * (h @ w2[e].T + b2[e])
        hs = jax.nn.silu(xf @ sw1.T + sb1) * (xf @ sw3.T + sb3)
        y = y + hs @ sw2.T + sb2
        return y.reshape(Bv, Sv, Dv)
    x = x + jnp.tanh(g_xattn[0]) * _L0_xattn_ref(_layernorm(x, axis=-1), ctx_1024, L0_xattn_Wq, L0_xattn_Wk, L0_xattn_Wv, L0_xattn_Wo, L0_xattn_bo)
    x = x + jnp.tanh(g_ffn[0]) * _L0_ffn_ref(_layernorm(x, axis=-1), L0_ffn_router_w, L0_ffn_expert_weights)
    x = x + jnp.tanh(g_xattn[1]) * _L1_xattn_ref(_layernorm(x, axis=-1), ctx_1024, ctx_1024, fside_Bx16xSxS2_0, mask_BxS2_bk0, L1_xattn_Wq, L1_xattn_bq, L1_xattn_Wk, L1_xattn_bk, L1_xattn_Wv, L1_xattn_bv, L1_xattn_Wo, L1_xattn_bo)
    x = x + jnp.tanh(g_ffn[1]) * _L1_ffn_ref(_layernorm(x, axis=-1), L1_ffn_U1, L1_ffn_V1, L1_ffn_b1, L1_ffn_U2, L1_ffn_V2, L1_ffn_b2)
    x = x + jnp.tanh(g_xattn[2]) * _L2_xattn_ref(_layernorm(x, axis=-1), ctx_1024, ctx_1024, fside_BxSxS2_0, fside_BxSxS2_0, fside_BxSxS2_0, L2_xattn_Wq, L2_xattn_bq, L2_xattn_Wk, L2_xattn_bk, L2_xattn_Wv, L2_xattn_bv, L2_xattn_beta_risk, L2_xattn_beta_prio, L2_xattn_beta_impl)
    x = x + jnp.tanh(g_ffn[2]) * _L2_ffn_ref(_layernorm(x, axis=-1), L2_ffn_weight, L2_ffn_bias)
    x = x + jnp.tanh(g_xattn[3]) * _L3_xattn_ref(_layernorm(x, axis=-1), ctx_1024, mask_BxS2_ik0, L3_xattn_q_w, L3_xattn_q_b, L3_xattn_k_w, L3_xattn_k_b, L3_xattn_v_w, L3_xattn_v_b)
    x = x + jnp.tanh(g_ffn[3]) * _L3_ffn_ref(_layernorm(x, axis=-1), L3_ffn_gate_w, L3_ffn_expert_bias, L3_ffn_w1, L3_ffn_b1, L3_ffn_w2, L3_ffn_b2, L3_ffn_w3, L3_ffn_b3, L3_ffn_sw1, L3_ffn_sb1, L3_ffn_sw2, L3_ffn_sb2, L3_ffn_sw3, L3_ffn_sb3)
    return x

_drawn_inputs = setup_inputs


def setup_inputs(seed=0):
    import zlib

    import numpy as np

    out = dict(_drawn_inputs(seed))
    spreads = {'L1_xattn_bq': (0.0, 0.351),
     'L1_xattn_bk': (0.0, 2.0),
     'L1_xattn_bv': (0.0, 0.1),
     'L1_xattn_bo': (0.0, 0.1),
     'L1_ffn_b1': (0.0, 0.8),
     'L1_ffn_b2': (0.0, 0.3),
     'L3_xattn_q_b': (0.0, 2.0),
     'L3_xattn_k_b': (0.0, 2.0),
     'L3_xattn_v_b': (0.0, 0.431),
     'L3_ffn_expert_bias': (0.0, 1.059)}
    factors = {'fside_Bx16xSxS2_0': 4.185,
     'fside_BxSxS2_0': 22.295,
     'g_ffn': 7.065,
     'L0_xattn_Wq': 7.047,
     'L0_xattn_Wk': 7.721,
     'L1_ffn_U1': 8.0,
     'L1_ffn_V1': 8.0,
     'L1_ffn_U2': 8.0,
     'L1_ffn_V2': 8.0,
     'L2_xattn_bq': 64.0,
     'L2_xattn_bk': 64.0,
     'L2_xattn_bv': 25.361,
     'L2_ffn_bias': 24.333,
     'L3_xattn_q_w': 8.0,
     'L3_xattn_k_w': 8.0,
     'L3_ffn_b1': 24.728,
     'L3_ffn_b3': 24.46,
     'L3_ffn_sb1': 24.22,
     'L3_ffn_sb3': 8.0,
     'L3_ffn_b2': 4.683,
     'L3_ffn_sb2': 4.842}
    for name, (base, spread) in spreads.items():
        noise = np.random.default_rng([zlib.crc32(name.encode()), seed]).standard_normal(out[name].shape)
        drawn = base * np.exp(spread * noise) if base else spread * noise
        out[name] = jnp.asarray(drawn.astype(out[name].dtype))
    for name, factor in factors.items():
        out[name] = (out[name] * factor).astype(out[name].dtype)
    return out
```

```python
from contextlib import ExitStack

import concourse.bass as bass
from concourse import mybir

F32 = mybir.dt.float32
BF16 = mybir.dt.bfloat16
I32 = mybir.dt.int32
U32 = mybir.dt.uint32
U8 = mybir.dt.uint8
ALU = mybir.AluOpType
ACT = mybir.ActivationFunctionType
AX = mybir.AxisListType

B, S, D, SK = 2, 512, 128, 154
KM, KR = 128, SK - 128
RR = 4 * KR
KP = 160
TILES = S // 128
HALVES = 16
HT = S
LAG = 3
BR = 3
NP = 6
E0, E3 = 32, 16
F3N = 1 + E3 // 2
NEG = -1.0e30
KINDS = ["attn", "moe0", "attn", "lowrank", "attn2", "fp8", "attn", "moe3"]
UNITS = {0: 8, 2: 16, 6: 16}


def kind(q):
    return KINDS[q // 2]


def layer(q):
    return q // 4


def steps(q, first, last):
    n_units = UNITS[q // 2]
    pair0 = n_units // 2 - 1
    for k in range(first, last):
        if k < n_units:
            yield "scores", k
        if 2 <= k <= n_units + 1:
            yield "normalise", k - 2
        if k >= LAG:
            yield "transpose", k - LAG
        if k == pair0 + 5:
            yield "values", 0
        if k == pair0 + 7:
            yield "finish", 0
    if last == n_units + LAG:
        yield "values", 1
        yield "finish", 1


def head_steps(q):
    return steps(q, 0, 2)


def rest_steps(q):
    return steps(q, 2, UNITS[q // 2])


def tail_steps(q):
    return steps(q, UNITS[q // 2], UNITS[q // 2] + LAG)


def walk(head, tail, norm, rest):
    norm(0)
    for q in range(HALVES):
        head(q)
        if q > 0:
            tail(q - 1)
        if q + 1 < HALVES:
            norm(q + 1)
        rest(q)
    tail(HALVES - 1)


PREP = [("k", 1), ("v", 1, 0), ("v", 1, 1), ("k", 3), ("v", 3, 0), ("v", 3, 1), ("k", 2), ("v", 2, 0), ("v", 2, 1)]


def t_uses():
    keys = []
    for h in range(8):
        keys += [("k0", h), ("v0", h)]
    keys += [("a0", h) for h in range(8)]
    keys += [("vo", b, i) for b in range(B) for i in range(2)] + [("vr", b) for b in range(B)]

    def of_steps(q, events):
        for what, n in events:
            if what == "transpose":
                keys.append(("t", q, n))
            if what == "finish":
                keys.append(("fin", q, n))

    def head(q):
        if kind(q) == "attn":
            if layer(q) > 0:
                keys.append(("q", q))
            of_steps(q, head_steps(q))
        elif kind(q) in ("moe0", "moe3"):
            keys.append(("logits", q))
        elif kind(q) == "lowrank":
            keys.append(("p1", q))
        elif kind(q) == "attn2":
            keys.append(("q", q))

    def tail(q):
        if kind(q) == "attn":
            of_steps(q, tail_steps(q))
        elif kind(q) == "lowrank":
            keys.append(("fin", q))
        elif kind(q) == "attn2":
            keys.append(("fin", q))
        elif kind(q) == "fp8":
            keys.append(("fin", q))
        elif kind(q) == "moe3":
            keys.append(("fin", q))

    def norm(q):
        keys.append(("ln", q))

    def rest(q):
        if kind(q) == "attn":
            of_steps(q, rest_steps(q))
        elif q == 2:
            keys.extend(PREP)
        elif kind(q) == "lowrank":
            keys.append(("q1", q))
        elif kind(q) == "attn2":
            keys.extend([("main", q), ("rem", q)])
        elif q == 10:
            keys.extend([("amax_t", q), ("amax_b", q)])
        elif kind(q) == "moe3":
            keys.append(("gates", q))
            keys.extend([("gb", q, n) for n in range(1, F3N)])

    walk(head, tail, norm, rest)
    return keys


def s_uses():
    keys = []
    for q in range(HALVES):
        n = {"attn": UNITS.get(q // 2), "moe0": 16, "lowrank": 2, "attn2": 1, "fp8": 0, "moe3": F3N}[kind(q)]
        keys += [(q, i) for i in range(n)]
    return keys


def build(nc, t, out):
    T_USE = {key: (i % 2, i // 2) for i, key in enumerate(t_uses())}
    S_USE = {key: (i % 2, i // 2) for i, key in enumerate(s_uses())}
    P_KEYS = [(q, n) for q in range(HALVES) for n in range(UNITS[q // 2] if kind(q) == "attn" else
                                                           1 if kind(q) == "attn2" else 0)]
    P_USE = {key: i for i, key in enumerate(P_KEYS)}
    M_USE = {key: i for i, key in enumerate((q, tt) for q in range(HALVES) if kind(q) == "attn" for tt in range(TILES))}
    O_KEYS = [(q, p) for q in range(HALVES) if kind(q) == "attn" for p in range(2)] + [(q, 0) for q in (14, 15)]
    O_USE = {key: i for i, key in enumerate(O_KEYS)}
    BIAS_USE = {key: i for i, key in enumerate((q, n) for q in (4, 5) for n in range(16))}

    with ExitStack() as ctx:
        def sb(name, shape, dt=F32):
            return ctx.enter_context(nc.sbuf_tensor(name, shape, dt))

        def ps(name, cols):
            return ctx.enter_context(nc.psum_tensor(name, [128, cols], F32))

        def sem(name):
            return ctx.enter_context(nc.semaphore(name))

        const = sb("const", [128, 456])
        rmask = const[:, 452:456]
        ident, dmask, iota32, iota16, ones = (const[:, 0:128], const[:, 128:132], const[:, 132:260],
                                              const[:, 260:324], const[:, 324:452])
        x = sb("x", [128, 8, D])
        ctxT = sb("ctxT", [128, B, KP])
        ctx_all = ctxT[:, :, :].rearrange("p b k -> p (b k)")
        cols = sb("cols", [128, 30])
        (bo0, bq1, bk1, bq2, bk2, bq3, bk3, sb1, sb3, sb2) = (cols[:, i:i + 1] for i in range(10))
        fb1 = cols[:, 10:14]
        eb1, eb3 = cols[:, 14:22], cols[:, 22:30]
        rows = sb("rows", [1, 4 * 128])
        bv1, bo1, bv2, bv3 = (rows[0:1, 128 * i:128 * i + 128] for i in range(4))
        wide = sb("wide", [128, 155])
        b_fp8, ebias, gates_in, betas = wide[:, 0:128], wide[:, 128:144], wide[:, 144:152], wide[:, 152:155]
        mask1_u8 = sb("mask1_u8", [128, B * SK], U8)
        mask3_i32 = sb("mask3_i32", [128, B * SK], I32)
        early = sb("early", [128, 4, 8, 128])
        wq0T, wk0, wv0, wo0 = (early[:, i] for i in range(4))
        routerT = sb("routerT", [128, E0])
        experts = sb("experts", [128, E0 * D])
        w_exp0 = experts[:, :].rearrange("p (e d) -> p e d", e=E0)
        w1T, w3T, w2T = (experts[:, 1152 * i:1152 * i + 1152].rearrange("p (n c) -> p n c", n=F3N) for i in range(3))
        gT = experts[0:E3, 3456:3456 + HT]
        sq = sb("sq", [128, 12, D])
        wq1, wk1, wv1, wo1, wq2, wk2, wv2, w_fp8, wq3, wk3, wv3 = (sq[:, i, :] for i in range(11))
        u1 = sb("u1", [128, 32])
        v1 = sb("v1", [32, 512])
        u2 = sb("u2", [128, 4, 32])
        v2b = sb("v2b", [33, D])
        gate3T = sb("gate3T", [128, E3])
        b2_exp = sb("b2_exp", [E3, D])
        bias1 = sb("bias1", [128, BR, 16, SK])
        phi = sb("phi", [128, 8, SK])
        phi_flat = phi[:, :, :].rearrange("p t k -> p (t k)")
        pair_sel = phi_flat[0:E3, 0:E3 // 2 * 128].rearrange("p (n c) -> p n c", n=E3 // 2)

        keyed = sb("keyed", [128, 4 * 8 * KP])
        a0 = keyed[:, 0:2560].rearrange("p (h b k) -> p h b k", h=8, b=B)
        vo_main = keyed[:, 2560:4608].rearrange("p (b h d) -> p b h d", b=B, h=8)
        vo_rem = keyed[:, 4608:5120].rearrange("p (b u d) -> p b u d", b=B, u=2)
        kb = {i: keyed[:, 640 * (i - 1):640 * (i - 1) + 1280].rearrange("p (u b k) -> p u b k", u=4, b=B)
              for i in (1, 3)}
        vm = {i: keyed[:, 2560 + 640 * (i - 1):2560 + 640 * (i - 1) + 1280].rearrange(
            "p (b g c) -> p b g c", b=B, g=4) for i in (1, 3)}
        vr = {i: sb(f"vr{i}", [RR, B, 128]) for i in (1, 3)}
        ctx_rem = sb("ctx_rem", [128, B, RR])
        kT2 = sb("kT2", [128, B, KP])
        v2m = sb("v2m", [128, B, D])
        v2r = sb("v2r", [KR, B, D])
        bk_masked = {i: sb(f"bk_masked{i}", [128, 4]) for i in (1, 3)}
        tg = sb("tg", [128, 8])
        tg_bias = sb("tg_bias", [128, D])
        coef = sb("coef", [128, 2])
        mask1 = sb("mask1", [128, B, SK])
        all_masked = sb("all_masked", [128, 2])
        mask3f = sb("mask3f", [128, B * SK])
        mask3 = sb("mask3", [128, B, SK], BF16)
        ones_b = sb("ones_b", [128, 128], BF16)
        expo = sb("expo", [128, 4])

        xnT = [sb(f"xnT{b}", [128, HT]) for b in range(B)]
        qT = [sb(f"qT{b}", [128, HT]) for b in range(B)]
        xn = sb("xn", [128, TILES, D])
        stats = sb("stats", [128, TILES, 6])
        meanvar = sb("meanvar", [128, TILES, 2])
        vareps = sb("vareps", [128, TILES])
        rstd = sb("rstd", [128, TILES])
        scores_sb = sb("scores_sb", [128, 2, 4, SK])
        probs = sb("probs", [128, NP, SK, 4])
        negmax = sb("negmax", [128, NP, 4])
        sums = sb("sums", [128, NP, 4])
        rsums = sb("rsums", [128, NP, 4])
        pT = sb("pT", [128, 2, 20, 256])
        oT = sb("oT", [128, 2, 256])
        spare = sb("spare", [128, 4])
        kT0 = pT[:, 0, 0:10, :].rearrange("p a c -> p (a c)").rearrange("p (h k) -> p h k", h=8)
        vT0 = pT[:, 0, 10:20, :].rearrange("p a c -> p (a c)").rearrange("p (h b k) -> p h b k", h=8, b=B)
        vT0_rem = pT[:, 1, 0:8, 0:B * RR].rearrange("p h (b c) -> p h b c", b=B)
        mult0, acc0 = (early[:, 2 * i:2 * i + 2].rearrange("p i h c -> p i (h c)") for i in range(2))
        red0 = sb("red0", [128, D])
        lg = sb("lg", [128, TILES, 32])
        lsel = sb("lsel", [128, TILES, 32])
        ex = sb("ex", [128, TILES, 32])
        hit = sb("hit", [128, 2, TILES, 32])
        gate = sb("gate", [128, 2, TILES, 32])
        top8 = sb("top8", [128, TILES, 8])
        idx8 = sb("idx8", [128, TILES, 8], U32)
        idxf = sb("idxf", [128, TILES, 2])
        gsum = sb("gsum", [128, 2, TILES])
        work = bias1[:, :, :, :].rearrange("p i h k -> p (i h k)")
        hidden = work[:, 0:2048].rearrange("p (n c) -> p n c", n=4)
        fq = work[:, 2048:3072].rearrange("p (n c) -> p n c", n=2)
        p1 = fq[0:32, 0, :]
        q1 = fq[0:33, 1, :]
        a1, h3, hg = (work[:, c:c + 1024].rearrange("p (n c) -> p n c", n=2) for c in (3072, 4096, 5120))
        oT3 = work[:, 6144:6656]
        am = sb("am", [128, 2])
        am2 = sb("am2", [2, 4])
        fsc = sb("fsc", [128, 8])
        x8 = sb("x8", [128, B, HT], BF16)
        w8 = sb("w8", [128, 128], BF16)

        psS = ps("psS", 2048)
        slot_view = psS[:, :].rearrange("p (s g c) -> p s g c", s=2, g=4)
        psT = [ps("psT0", 512), ps("psT1", 512)]
        psO = ps("psO", 512)
        psM = ps("psM", 512)

        LOADS = ["const", "ctxT", "x", "wk0", "wv0", "wq0T", "wo0", "cols", "wide", "rows", "routerT", "w_exp0",
                 "masks1", "masks3", "sq", "phi", "u1", "v1", "u2", "v2b", "pair_sel", "gate3T", "w1T", "w3T",
                 "w2T", "b2_exp"]
        loaded = {n: sem(f"loaded_{n}") for n in LOADS}
        bias_loaded = [sem(f"bias_loaded{i}") for i in range(8)]
        t_full, t_free = ([sem(f"t_{w}{i}") for i in range(2)] for w in ("full", "free"))
        s_full, s_free = ([sem(f"s_{w}{i}") for i in range(2)] for w in ("full", "free"))
        m_full, m_free, o_full, o_free = (sem(n) for n in ("m_full", "m_free", "o_full", "o_free"))
        dve_done = sem("dve_done")
        pool_done = sem("pool_done")
        zeroed = sem("zeroed")
        consts_ready = sem("consts_ready")
        tanh_ready = sem("tanh_ready")
        eps_added = sem("eps_added")
        rstd_ready = sem("rstd_ready")
        xn_ready = sem("xn_ready")
        xnT_ready = sem("xnT_ready")
        max_ready = sem("max_ready")
        bias_exp_done = sem("bias_exp_done")
        rsum_ready = sem("rsum_ready")
        probs_ready = sem("probs_ready")
        oT_ready = sem("oT_ready")
        bias_masked = sem("bias_masked")
        exp_in = sem("exp_in")
        exp_out = sem("exp_out")
        gate_ready = sem("gate_ready")
        acc_first = sem("acc_first")
        mult_ready = sem("mult_ready")
        acc_added = sem("acc_added")
        acc_read = sem("acc_read")
        hidden_ready = sem("hidden_ready")
        q1_ready = sem("q1_ready")
        silu_ready = sem("silu_ready")
        y_done = sem("y_done")
        am_ready = sem("am_ready")
        quant_ready = sem("quant_ready")
        x_final = sem("x_final")
        stored = sem("stored")

        def t_bank(key):
            return psT[T_USE[key][0]]

        def wait_t_free(eng, key):
            i, n = T_USE[key]
            if n > 0:
                eng.wait_ge(t_free[i], n)

        def wait_t_full(eng, key):
            i, n = T_USE[key]
            eng.wait_ge(t_full[i], n + 1)

        def wait_t_read(eng, key):
            i, n = T_USE[key]
            eng.wait_ge(t_free[i], n + 1)

        def slot(q, n):
            return slot_view[:, S_USE[q, n][0]]

        def wait_s_free(eng, q, n):
            i, k = S_USE[q, n]
            if k > 0:
                eng.wait_ge(s_free[i], k)

        def wait_s_full(eng, q, n):
            i, k = S_USE[q, n]
            eng.wait_ge(s_full[i], k + 1)

        def wait_s_read(eng, q, n):
            i, k = S_USE[q, n]
            eng.wait_ge(s_free[i], k + 1)

        def wait_exp_done(eng, q, n):
            if layer(q) == 1:
                eng.wait_ge(bias_exp_done, BIAS_USE[q, n] + 1)
            elif kind(q) == "attn2":
                eng.wait_ge(exp_out, EXP_OUT[q])
            else:
                wait_s_read(eng, q, n)

        EXP_IN = {2: 1, 3: 2, 14: 3, 15: 4}
        EXP_OUT = {2: 1, 3: 2, 8: 3, 9: 4, 14: 5, 15: 6}
        X_SCALE = {0: 0, 1: 4, 2: 1, 3: 5, 4: 2, 5: 6, 6: 3, 7: 7}

        def turned_by(q, n):
            if layer(q) == 3:
                return "scalar" if n % 4 == 0 else "vector"
            return "scalar" if n % 2 == 0 else "vector"

        def rem_turned_by(q):
            return "vector" if layer(q) == 3 else "scalar"

        def tile_of(q, n):
            return n // (UNITS[q // 2] // TILES), n % (UNITS[q // 2] // TILES)

        def copy_turned(eng, copy, q, n):
            tt, u = tile_of(q, n)
            nu = UNITS[q // 2] // TILES
            p, cols_of = tt // 2, slice(tt % 2 * 128, tt % 2 * 128 + 128)
            me = "scalar" if eng is nc.scalar else "vector"
            use = O_USE[q, p]
            if turned_by(q, n) == me:
                if use >= 2:
                    eng.wait_ge(o_full, use - 1)
                wait_t_full(eng, ("t", q, n))
                copy(pT[:, use % 2, 4 * u:4 * u + 4, cols_of],
                     t_bank(("t", q, n))[:, :].rearrange("p (g c) -> p g c", g=4)).then_inc(
                    t_free[T_USE["t", q, n][0]], 1)
            if u == nu - 1 and rem_turned_by(q) == me:
                if use >= 2:
                    eng.wait_ge(o_full, use - 1)
                eng.wait_ge(m_full, M_USE[q, tt] + 1)
                copy(pT[0:RR, use % 2, 4 * nu:5 * nu, cols_of],
                     psM[0:RR, 0:128 * nu].rearrange("p (u c) -> p u c", u=nu)).then_inc(m_free, 1)

        block = ctx.enter_context(nc.Block())

        @block.sync
        def _(sp):
            def load(name, dst, src):
                sp.dma_start(dst, src).then_inc(loaded[name], 16)

            load("const", const[:, :], t["const"])
            load("ctxT", ctxT[:, :, :], t["ctxT"])
            load("wk0", wk0[:, :, :], t["wk0"])
            load("wv0", wv0[:, :, :], t["wv0"])
            load("wq0T", wq0T[:, :, :], t["wq0T"])
            load("wo0", wo0[:, :, :], t["wo0"])
            load("routerT", routerT[:, :], t["routerT"])
            load("w_exp0", w_exp0[:, :, :], t["w_exp0"])
            load("sq", sq[:, 0:11, :], t["sq"])

            def load_bias(i):
                b, tt = i // TILES, i % TILES
                src = t["fside4"][b, :, 128 * tt:128 * tt + 128, :].rearrange("h p k -> p h k")
                sp.dma_start(bias1[:, i % BR, :, :], src).then_inc(bias_loaded[i], 16)

            for i in range(BR):
                load_bias(i)
            load("phi", phi[:, :, :], t["phi"].rearrange("(t p) k -> p t k", p=128))
            for name, dst in (("u1", u1), ("v1", v1), ("u2", u2), ("v2b", v2b), ("gate3T", gate3T),
                              ("b2_exp", b2_exp)):
                load(name, dst[:], t[name])
            wait_s_full(sp, 3, 15)
            for name, dst in (("w1T", w1T), ("w3T", w3T), ("w2T", w2T)):
                load(name, dst, t[name])
            for i in range(BR, 8):
                old = i - BR
                wait_s_read(sp, 4 + old // TILES, 4 * (old % TILES) + 3)
                load_bias(i)
            sp.wait_ge(am_ready, 1)
            load("pair_sel", pair_sel, t["pair_sel"])
            for b in range(B):
                sp.wait_ge(x_final, b + 1)
                sp.dma_start(out[b].rearrange("(t p) d -> p t d", p=128),
                             x[:, TILES * b:TILES * b + TILES, :]).then_inc(stored, 16)
            sp.wait_ge(stored, 32)

        @block.tensor
        def _(pe):
            mm = nc.tensor.matmul

            def begin_t(key):
                wait_t_free(pe, key)
                return t_bank(key)

            def end_t(ins, key):
                ins.then_inc(t_full[T_USE[key][0]], 1)

            def prepare0():
                pe.wait_ge(loaded["const"], 16)
                pe.wait_ge(loaded["ctxT"], 16)
                pe.wait_ge(loaded["wk0"], 16)
                pe.wait_ge(loaded["wv0"], 16)
                for h in range(8):
                    for key, w in ((("k0", h), wk0), (("v0", h), wv0)):
                        bank = begin_t(key)
                        end_t(mm(bank[:, 0:B * KP], w[:, h, :], ctx_all, start=True, stop=True), key)
                pe.wait_ge(loaded["wq0T"], 16)
                for h in range(8):
                    key = ("a0", h)
                    bank = begin_t(key)
                    wait_t_read(pe, ("k0", h))
                    end_t(mm(bank[:, 0:B * KP], wq0T[:, h, :], kT0[:, h, :], start=True, stop=True), key)
                pe.wait_ge(loaded["wo0"], 16)
                for b in range(B):
                    for i in range(2):
                        key = ("vo", b, i)
                        bank = begin_t(key)
                        for g in range(4):
                            h = 4 * i + g
                            wait_t_read(pe, ("v0", h))
                            last = mm(bank[:, 128 * g:128 * g + 128], vT0[:, h, b, 0:KM], wo0[:, h, :],
                                      start=True, stop=True)
                        end_t(last, key)
                for b in range(B):
                    key = ("vr", b)
                    bank = begin_t(key)
                    for u in range(2):
                        for g in range(4):
                            h = 4 * u + g
                            last = mm(bank[0:RR, 128 * u:128 * u + 128], vT0_rem[:, h, b, :], wo0[:, h, :],
                                      start=g == 0, stop=g == 3)
                    end_t(last, key)

            def prepare(key):
                bank = begin_t(key)
                i = key[1]
                wk, wv, bv = {1: (wk1, wv1, bv1), 2: (wk2, wv2, bv2), 3: (wk3, wv3, bv3)}[i]
                if key[0] == "k":
                    last = mm(bank[:, 0:B * KP], wk, ctx_all, start=True, stop=True)
                else:
                    b = key[2]
                    mm(bank[:, 0:128], ctxT[:, b, 0:KM], wv, start=True, stop=False)
                    mm(bank[:, 0:128], ones[0:1, :], bv, start=False, stop=True)
                    lhs = ctxT[:, b, KM:SK] if i == 2 else ctx_rem[:, b, :]
                    o = bank[0:lhs.shape[1], 128:256]
                    mm(o, lhs, wv, start=True, stop=False)
                    last = mm(o, ones[0:1, 0:lhs.shape[1]], bv, start=False, stop=True)
                end_t(last, key)

            def scores(q, n):
                b, i = q % 2, layer(q)
                tt, u = tile_of(q, n)
                wait_s_free(pe, q, n)
                sl = slot(q, n)
                tok = slice(128 * tt, 128 * tt + 128)
                for g in range(4):
                    if i == 0:
                        last = mm(sl[:, g, 0:SK], xnT[b][:, tok], a0[:, 4 * u + g, b, 0:SK], start=True, stop=True)
                        continue
                    r = slice(32 * u, 32 * u + 32)
                    last = mm(sl[:, g, 0:SK], qT[b][r, tok], kb[i][r, g, b, 0:SK], start=True, stop=i == 1)
                    if i == 3:
                        last = mm(sl[:, g, 0:SK], ones_b[32 * u:32 * u + 1, :], mask3[32 * u:32 * u + 1, b, :],
                                  start=False, stop=True)
                last.then_inc(s_full[S_USE[q, n][0]], 1)

            def turn(q, n):
                tt, u = tile_of(q, n)
                key = ("t", q, n)
                pe.wait_ge(probs_ready, P_USE[q, n] + 1)
                if u == 0 and M_USE[q, tt] > 0:
                    pe.wait_ge(m_free, M_USE[q, tt])
                p = probs[:, P_USE[q, n] % NP]
                last = nc.tensor.transpose(psM[0:RR, 128 * u:128 * u + 128],
                                           p[:, KM:SK, :].rearrange("p k g -> p (k g)"), ident)
                if u == UNITS[q // 2] // TILES - 1:
                    last.then_inc(m_full, 1)
                bank = begin_t(key)
                for g in range(4):
                    last = nc.tensor.transpose(bank[:, 128 * g:128 * g + 128], p[:, 0:KM, g], ident)
                end_t(last, key)

            def values(q, p):
                b, i, nu = q % 2, layer(q), UNITS[q // 2] // TILES
                use = O_USE[q, p]
                for n in range(p * 2 * nu, (p + 1) * 2 * nu):
                    if n >= (p + 1) * 2 * nu - 4:
                        wait_t_read(pe, ("t", q, n))
                pe.wait_ge(m_free, M_USE[q, 2 * p + 1] + 1)
                if use > 0:
                    pe.wait_ge(o_free, use)
                src = pT[:, use % 2]
                if i == 0:
                    for c in range(8):
                        mm(psO[:, 0:256], vo_main[:, b, c, :], src[:, c, :], start=c == 0, stop=False)
                    for u in range(2):
                        last = mm(psO[:, 0:256], vo_rem[0:RR, b, u, :], src[0:RR, 8 + u, :], start=False, stop=u == 1)
                else:
                    for g in range(4):
                        for u in range(nu):
                            mm(psO[32 * u:32 * u + 32, 0:256], vm[i][:, b, u, 32 * g:32 * g + 32],
                               src[:, 4 * u + g, :], start=g == 0, stop=False, skip_group_check=True)
                    for u in range(nu):
                        last = mm(psO[32 * u:32 * u + 32, 0:256], vr[i][:, b, 32 * u:32 * u + 32],
                                  src[0:RR, 4 * nu + u, :], start=False, stop=True, skip_group_check=True)
                last.then_inc(o_full, 1)

            def finish(q, p):
                key = ("fin", q, p)
                use = O_USE[q, p]
                bank = begin_t(key)
                pe.wait_ge(oT_ready, use + 1)
                for c in range(2):
                    part = oT[:, use % 2, 128 * c:128 * c + 128]
                    o = bank[:, 128 * c:128 * c + 128]
                    if layer(q) == 1:
                        mm(o, part, wo1, start=True, stop=False)
                        last = mm(o, ones[0:1, :], bo1, start=False, stop=True)
                    else:
                        last = nc.tensor.transpose(o, part, ident)
                end_t(last, key)

            def run_steps(q, events):
                for what, n in events:
                    if what == "scores":
                        scores(q, n)
                    elif what == "transpose":
                        turn(q, n)
                    elif what == "values":
                        values(q, n)
                    elif what == "finish":
                        finish(q, n)

            def tokens_major(key, lhs_of, rhs):
                bank = begin_t(key)
                w = rhs.shape[1]
                for tt in range(TILES):
                    last = mm(bank[:, w * tt:w * tt + w], lhs_of(tt), rhs, start=True, stop=True)
                end_t(last, key)

            def expert_unit(q, n):
                tt, part = n // 4, n % 4
                wait_s_free(pe, q, n)
                sl = slot(q, n)
                for g in range(2):
                    e = 8 * part + 4 * g
                    last = mm(sl[:, 2 * g:2 * g + 2, :].rearrange("p g c -> p (g c)"),
                              xnT[q % 2][:, 128 * tt:128 * tt + 128],
                              w_exp0[:, e:e + 4, :].rearrange("p e d -> p (e d)"), start=True, stop=True)
                last.then_inc(s_full[S_USE[q, n][0]], 1)

            def lowrank_unit(q, n):
                wait_s_free(pe, q, n)
                sl = slot(q, n)
                for g in range(2):
                    c = 2 * n + g
                    last = mm(sl[:, 2 * g:2 * g + 2, :].rearrange("p g c -> p (g c)"), v1[:, 128 * c:128 * c + 128],
                              p1, start=True, stop=True)
                last.then_inc(s_full[S_USE[q, n][0]], 1)

            def moe3_unit(q, n):
                wait_s_free(pe, q, n)
                sl = slot(q, n)
                for g, w in enumerate((w1T, w3T)):
                    last = mm(sl[:, 2 * g:2 * g + 2, :].rearrange("p g c -> p (g c)"), w[:, n, :], xnT[q % 2][:, :],
                              start=True, stop=True)
                last.then_inc(s_full[S_USE[q, n][0]], 1)

            def gate_spread(q, n):
                key = ("gb", q, n)
                bank = begin_t(key)
                end_t(mm(bank[:, :], pair_sel[:, n - 1, :], gT[:, :], start=True, stop=True), key)

            def moe3_out(q, n):
                if n == 0:
                    wait_s_read(pe, q, 0)
                    pe.wait_ge(o_free, O_USE[q, 0])
                else:
                    wait_t_read(pe, ("gb", q, n))
                src = h3[:, 0, :] if n == 0 else hg[:, n % 2, :]
                last = mm(psO[:, :], w2T[:, n, :], src, start=n == 0, stop=n == F3N - 1)
                last.then_inc(o_full if n == F3N - 1 else y_done, 1)

            def head(q):
                b = q % 2
                pe.wait_ge(xnT_ready, q + 1)
                k = kind(q)
                if k == "attn":
                    if layer(q) > 0:
                        key = ("q", q)
                        bank = begin_t(key)
                        end_t(mm(bank[:, :], wq1 if layer(q) == 1 else wq3, xnT[b][:, :], start=True, stop=True), key)
                        wait_t_read(pe, key)
                    run_steps(q, head_steps(q))
                elif k == "moe0":
                    if q == 2:
                        pe.wait_ge(loaded["routerT"], 16)
                        pe.wait_ge(loaded["w_exp0"], 16)
                    tokens_major(("logits", q), lambda tt: xnT[b][:, 128 * tt:128 * tt + 128], routerT[:, :])
                    expert_unit(q, 0)
                    expert_unit(q, 1)
                elif k == "moe3":
                    if q == 14:
                        for n in ("gate3T", "w1T", "w3T", "w2T", "b2_exp", "pair_sel"):
                            pe.wait_ge(loaded[n], 16)
                    tokens_major(("logits", q), lambda tt: xnT[b][:, 128 * tt:128 * tt + 128], gate3T[:, :])
                    moe3_unit(q, 0)
                    moe3_unit(q, 1)
                elif k == "lowrank":
                    if q == 6:
                        for n in ("u1", "v1", "u2", "v2b"):
                            pe.wait_ge(loaded[n], 16)
                    key = ("p1", q)
                    bank = begin_t(key)
                    end_t(mm(bank[0:32, :], u1[:, :], xnT[b][:, :], start=True, stop=True), key)
                    wait_t_read(pe, key)
                    lowrank_unit(q, 0)
                    lowrank_unit(q, 1)
                elif k == "attn2":
                    key = ("q", q)
                    bank = begin_t(key)
                    end_t(mm(bank[:, :], wq2, xnT[b][:, :], start=True, stop=True), key)
                    wait_t_read(pe, key)
                    wait_s_free(pe, q, 0)
                    for tt in range(TILES):
                        last = mm(slot(q, 0)[:, tt, 0:SK], qT[b][:, 128 * tt:128 * tt + 128], kT2[:, b, 0:SK],
                                  start=True, stop=True)
                    last.then_inc(s_full[S_USE[q, 0][0]], 1)

            def norm(q):
                key = ("ln", q)
                bank = begin_t(key)
                pe.wait_ge(xn_ready, q + 1)
                for tt in range(TILES):
                    last = nc.tensor.transpose(bank[:, 128 * tt:128 * tt + 128], xn[:, tt, :], ident)
                end_t(last, key)

            def rest(q):
                k = kind(q)
                if k == "attn":
                    run_steps(q, rest_steps(q))
                elif k == "moe0":
                    todo = list(PREP) if q == 2 else []
                    if todo:
                        pe.wait_ge(loaded["sq"], 16)
                        pe.wait_ge(loaded["rows"], 16)
                    for n in range(2, 16):
                        expert_unit(q, n)
                        if todo:
                            prepare(todo.pop(0))
                elif k == "lowrank":
                    key = ("q1", q)
                    bank = begin_t(key)
                    for c in range(4):
                        pe.wait_ge(hidden_ready, (q - 6) * 4 + c + 1)
                        last = mm(bank[0:32, :], u2[:, c, :], hidden[:, c, :], start=c == 0, stop=c == 3)
                    end_t(last, key)
                elif k == "attn2":
                    pe.wait_ge(probs_ready, P_USE[q, 0] + 1)
                    p = probs[:, P_USE[q, 0] % NP]
                    for key, ks in ((("main", q), slice(0, KM)), (("rem", q), slice(KM, SK))):
                        bank = begin_t(key)
                        for tt in range(TILES):
                            last = nc.tensor.transpose(bank[0:ks.stop - ks.start, 128 * tt:128 * tt + 128],
                                                       p[:, ks, tt], ident)
                        end_t(last, key)
                elif q == 10:
                    key = ("amax_t", q)
                    bank = begin_t(key)
                    pe.wait_ge(am_ready, 1)
                    end_t(nc.tensor.transpose(bank[0:2, 0:128], am[:, :], ident), key)
                    key = ("amax_b", q)
                    bank = begin_t(key)
                    pe.wait_ge(am_ready, 2)
                    end_t(mm(bank[:, 0:2], ones[0:2, :], am2[:, 2:4], start=True, stop=True), key)
                elif k == "moe3":
                    moe3_out(q, 0)
                    key = ("gates", q)
                    bank = begin_t(key)
                    pe.wait_ge(gate_ready, q - 14 + 3)
                    for tt in range(TILES):
                        last = nc.tensor.transpose(bank[0:E3, 128 * tt:128 * tt + 128], gate[:, 0, tt, 0:E3], ident)
                    end_t(last, key)
                    wait_t_read(pe, key)
                    mm(psO[:, :], b2_exp[:, :], gT[:, :], start=False, stop=False)
                    gate_spread(q, 1)
                    for n in range(1, F3N - 1):
                        moe3_unit(q, n + 1)
                        gate_spread(q, n + 1)
                        moe3_out(q, n)

            def tail(q):
                b, k = q % 2, kind(q)
                if k == "attn":
                    run_steps(q, tail_steps(q))
                elif k == "lowrank":
                    wait_t_read(pe, ("q1", q))
                    tokens_major(("fin", q), lambda tt: q1[:, 128 * tt:128 * tt + 128], v2b[:, :])
                elif k == "attn2":
                    wait_t_read(pe, ("main", q))
                    wait_t_read(pe, ("rem", q))
                    key = ("fin", q)
                    bank = begin_t(key)
                    for tt in range(TILES):
                        tok = slice(128 * tt, 128 * tt + 128)
                        mm(bank[:, tok], pT[:, 0, 0:2, :].rearrange("p a c -> p (a c)")[:, tok], v2m[:, b, :],
                           start=True, stop=False)
                        last = mm(bank[:, tok], pT[0:KR, 1, 0:2, :].rearrange("p a c -> p (a c)")[:, tok],
                                  v2r[:, b, :], start=False, stop=True)
                    end_t(last, key)
                elif k == "fp8":
                    pe.wait_ge(quant_ready, b + 2)
                    tokens_major(("fin", q), lambda tt: x8[:, b, 128 * tt:128 * tt + 128], w8[:, :])
                elif k == "moe3":
                    moe3_out(q, F3N - 1)
                    key = ("fin", q)
                    bank = begin_t(key)
                    pe.wait_ge(oT_ready, O_USE[q, 0] + 1)
                    for tt in range(TILES):
                        last = nc.tensor.transpose(bank[:, 128 * tt:128 * tt + 128], oT3[:, 128 * tt:128 * tt + 128],
                                                   ident)
                    end_t(last, key)

            prepare0()
            walk(head, tail, norm, rest)

        @block.vector
        def _(dve):
            v = nc.vector
            chain = [0]

            def tick(ins):
                chain[0] += 1
                ins.then_inc(dve_done, 1)

            def settle():
                dve.wait_ge(dve_done, chain[0])

            def link(ins):
                tick(ins)
                settle()

            def copy(dst, src):
                return v.tensor_copy(dst, src)

            def free_t(ins, key):
                ins.then_inc(t_free[T_USE[key][0]], 1)

            def constants():
                for n in ("const", "cols", "wide", "masks1", "masks3"):
                    dve.wait_ge(loaded[n], 16)
                for i, bk in ((1, bk1), (3, bk3)):
                    tick(v.tensor_scalar(bk_masked[i][:, :], dmask, bk, None, ALU.mult))
                tick(v.tensor_tensor(coef[:, 0:1], betas[:, 0:1], betas[:, 1:2], ALU.add))
                tick(v.tensor_copy(mask1[:, :, :].rearrange("p b k -> p (b k)"), mask1_u8[:, :]))
                tick(v.tensor_copy(mask3f[:, :], mask3_i32[:, :]))
                tick(v.memset(ones_b[:, :], 1.0))
                settle()
                tick(v.tensor_tensor(coef[:, 1:2], coef[:, 0:1], betas[:, 2:3], ALU.subtract))
                tick(v.tensor_reduce(all_masked[:, :], mask1[:, :, :], AX.X, ALU.min))
                tick(v.tensor_scalar(mask3[:, :, :].rearrange("p b k -> p (b k)"), mask3f[:, :], 0.0, NEG,
                                     ALU.is_gt, ALU.mult))
                settle()
                link(v.tensor_scalar(all_masked[:, :], all_masked[:, :], -1.0, 1.0, ALU.mult, ALU.add))
                link(v.tensor_tensor(mask1[:, :, 0], mask1[:, :, 0], all_masked[:, :], ALU.mult))
                link(v.tensor_scalar(mask1[:, :, :], mask1[:, :, :], NEG, None, ALU.mult))
                dve.wait_ge(tanh_ready, 1)
                v.tensor_scalar(tg_bias[:, :], b_fp8, tg[:, X_SCALE[5]:X_SCALE[5] + 1], None,
                                ALU.mult).then_inc(consts_ready, 1)
                dve.wait_ge(consts_ready, 1)

            def prepare0():
                dve.wait_ge(loaded["ctxT"], 16)
                dve.wait_ge(zeroed, 1)
                v.tensor_copy(ctx_rem[:, :, :].rearrange("p b (k g) -> p b k g", g=4),
                              ctxT[:, :, KM:SK].unsqueeze(3).broadcast_to([128, B, KR, 4]))
                for h in range(8):
                    key = ("v0", h)
                    wait_t_full(dve, key)
                    src = t_bank(key)[:, 0:B * KP].rearrange("p (b k) -> p b k", b=B)
                    v.tensor_copy(vT0[:, h, :, 0:KM], src[:, :, 0:KM])
                    free_t(v.tensor_copy(vT0_rem[:, h, :, :].rearrange("p b (k g) -> p b k g", g=4)[:, :, :, h % 4],
                                         src[:, :, KM:SK]), key)
                for h in range(0, 8, 2):
                    key = ("a0", h)
                    wait_t_full(dve, key)
                    free_t(v.tensor_scalar(a0[:, h, :, :], t_bank(key)[:, 0:B * KP].rearrange("p (b k) -> p b k", b=B),
                                           64.0 ** -0.5, None, ALU.mult), key)
                for b in range(B):
                    key = ("vo", b, 0)
                    wait_t_full(dve, key)
                    free_t(v.tensor_copy(vo_main[:, b, 0:4, :].rearrange("p h d -> p (h d)"), t_bank(key)[:, :]), key)

            def norm(q):
                b = q % 2
                if q < 2:
                    dve.wait_ge(loaded["x"], 16)
                settle()
                xs = x[:, TILES * b:TILES * b + TILES, :]
                for tt in range(TILES):
                    tick(v.bn_stats(stats[:, tt, :], xs[:, tt, :]))
                settle()
                for tt in range(TILES):
                    tick(v.bn_aggr(meanvar[:, tt, :], stats[:, tt, :]))
                settle()
                v.tensor_scalar(vareps[:, :], meanvar[:, :, 1], 1e-5, None, ALU.add).then_inc(eps_added, 1)
                dve.wait_ge(rstd_ready, q + 1)
                if q > 0:
                    wait_t_full(dve, ("ln", q - 1))
                for tt in range(TILES):
                    last = v.tensor_scalar(xn[:, tt, :], xs[:, tt, :], meanvar[:, tt, 0:1], rstd[:, tt:tt + 1],
                                           ALU.subtract, ALU.mult)
                last.then_inc(xn_ready, 1)

            def add_to_x(q, key, tiles, width):
                wait_t_full(dve, key)
                s = q // 2
                xs = x[:, tiles.start:tiles.stop, :].rearrange("p t d -> p (t d)")
                v.scalar_tensor_tensor(xs, t_bank(key)[:, 0:width], tg[:, X_SCALE[s]:X_SCALE[s] + 1], xs,
                                       ALU.mult, ALU.add).then_inc(t_free[T_USE[key][0]], 1)
                wait_t_read(dve, key)

            def maxima(q, n):
                b = q % 2
                ring = P_USE[q, n] % NP
                wait_s_full(dve, q, n)
                src = slot(q, n)[:, :, 0:SK]
                if layer(q) == 1:
                    tt, u = tile_of(q, n)
                    if u == 0:
                        dve.wait_ge(bias_masked, TILES * b + tt + 1)
                    use = BIAS_USE[q, n]
                    if use >= 2:
                        dve.wait_ge(bias_exp_done, use - 1)
                    part = bias1[:, (TILES * b + tt) % BR, 4 * u:4 * u + 4, :]
                    v.tensor_tensor(scores_sb[:, use % 2, :, :], src, part, ALU.add).then_inc(
                        s_free[S_USE[q, n][0]], 1)
                    src = scores_sb[:, use % 2, :, :]
                    wait_s_read(dve, q, n)
                v.tensor_reduce(negmax[:, ring, :], src, AX.X, ALU.max, negate=True).then_inc(max_ready, 1)

            def reciprocals(q, n):
                ring = P_USE[q, n] % NP
                wait_exp_done(dve, q, n)
                v.reciprocal(rsums[:, ring, :], sums[:, ring, :]).then_inc(rsum_ready, 1)

            def run_steps(q, events):
                for what, n in events:
                    if what == "scores":
                        maxima(q, n)
                    elif what == "normalise":
                        reciprocals(q, n)
                    elif what == "transpose":
                        copy_turned(nc.vector, copy, q, n)
                    elif what == "finish":
                        t0 = TILES * (q % 2) + 2 * n
                        add_to_x(q, ("fin", q, n), range(t0, t0 + 2), 256)

            def gating(q):
                first = kind(q) == "moe0"
                ne = E0 if first else E3
                io = (iota32 if first else iota16).rearrange("p (t e) -> p t e", t=TILES)
                key = ("logits", q)
                wait_t_full(dve, key)
                bank = t_bank(key)[:, 0:TILES * ne].rearrange("p (t e) -> p t e", t=TILES)
                l, sel, e = lg[:, :, 0:ne], lsel[:, :, 0:ne], ex[:, :, 0:ne]
                free_t(v.tensor_copy(l, bank), key)
                wait_t_read(dve, key)
                if not first:
                    v.tensor_copy(sel, l).then_inc(exp_in, 1)
                    dve.wait_ge(exp_in, EXP_IN[q])
                    link(v.tensor_tensor(sel, l, ebias.unsqueeze(1).broadcast_to([128, TILES, ne]), ALU.add))
                    l = sel
                for tt in range(TILES):
                    tick(v.max(top8[:, tt, :], l[:, tt, :]))
                settle()
                for tt in range(TILES):
                    tick(v.max_index(idx8[:, tt, :], top8[:, tt, :], l[:, tt, :]))
                if first:
                    v.tensor_tensor(sel, l, top8[:, :, 0:1].broadcast_to([128, TILES, ne]),
                                    ALU.subtract).then_inc(exp_in, 1)
                settle()
                link(v.tensor_copy(idxf[:, :, :], idx8[:, :, 0:2]))
                for i in range(2):
                    tick(v.tensor_tensor(hit[:, i, :, 0:ne], io, idxf[:, :, i:i + 1].broadcast_to([128, TILES, ne]),
                                         ALU.is_equal))
                settle()
                link(v.tensor_tensor(hit[:, 0, :, 0:ne], hit[:, 0, :, 0:ne], hit[:, 1, :, 0:ne], ALU.add))
                dve.wait_ge(exp_out, EXP_OUT[q])
                gb = q % 2 if first else 0
                g = gate[:, gb, :, 0:ne]
                if first:
                    link(v.tensor_reduce(gsum[:, 0, :], e, AX.X, ALU.add))
                else:
                    link(v.tensor_scalar(e, e, 1.0, None, ALU.add))
                    link(v.reciprocal(e, e))
                link(v.tensor_tensor(e, e, hit[:, 0, :, 0:ne], ALU.mult))
                if not first:
                    link(v.tensor_reduce(gsum[:, 0, :], e, AX.X, ALU.add))
                    link(v.tensor_scalar(gsum[:, 0, :], gsum[:, 0, :], 1e-10, None, ALU.add))
                link(v.reciprocal(gsum[:, 1, :], gsum[:, 0, :]))
                if q == 15:
                    wait_t_full(dve, ("gates", 14))
                v.tensor_tensor(g, e, gsum[:, 1, :].unsqueeze(2).broadcast_to([128, TILES, ne]),
                                ALU.mult).then_inc(gate_ready, 1)
                dve.wait_ge(gate_ready, {2: 1, 3: 2, 14: 3, 15: 4}[q])

            def weigh(q, n):
                tt, part = n // 4, n % 4
                tile = TILES * (q % 2) + tt
                wait_s_full(dve, q, n)
                w = gate[:, q % 2, tt, 8 * part:8 * part + 8].rearrange("p (g e) -> p g e", g=4)
                src = slot(q, n).rearrange("p g (e d) -> p g e d", e=2)
                w = w.unsqueeze(3).broadcast_to([128, 4, 2, 128])
                if part == 0:
                    if tile >= 2:
                        dve.wait_ge(acc_read, tile - 1)
                    dst, done = acc0[:, tile % 2, :], s_free[S_USE[q, n][0]]
                else:
                    m = 3 * tile + part - 1
                    if m >= 2:
                        dve.wait_ge(acc_added, m - 1)
                    dst, done = mult0[:, m % 2, :], s_free[S_USE[q, n][0]]
                v.tensor_tensor(dst.rearrange("p (g e d) -> p g e d", g=4, e=2), src, w, ALU.mult).then_inc(done, 1)

            def sum_experts(q, tt):
                tile = TILES * (q % 2) + tt
                dve.wait_ge(acc_added, 3 * tile + 3)
                settle()
                v.tensor_reduce(red0[:, :], acc0[:, tile % 2, :].rearrange("p (e d) -> p d e", e=8), AX.X,
                                ALU.add).then_inc(acc_read, 1)
                dve.wait_ge(acc_read, tile + 1)
                s = X_SCALE[q // 2]
                tick(v.scalar_tensor_tensor(x[:, tile, :], red0[:, :], tg[:, s:s + 1], x[:, tile, :],
                                            ALU.mult, ALU.add))

            def quantise(src, scale, tmp, dst, sig):
                link(v.tensor_scalar(tmp[0], src, scale, None, ALU.mult))
                link(v.tensor_scalar(tmp[1].bitcast(U32), tmp[0].bitcast(U32), 0x7F800000, None, ALU.bitwise_and))
                link(v.tensor_scalar(tmp[1], tmp[1], 2.0 ** -6, 1.5 * 2.0 ** 20, ALU.max, ALU.mult))
                link(v.tensor_tensor(tmp[0], tmp[0], tmp[1], ALU.add))
                v.tensor_tensor(dst, tmp[0], tmp[1], ALU.subtract).then_inc(sig, 1)

            def head(q):
                b, k = q % 2, kind(q)
                if k == "attn":
                    if layer(q) > 0:
                        key = ("q", q)
                        wait_t_full(dve, key)
                        free_t(v.tensor_scalar(qT[b][:, :], t_bank(key)[:, :], bq1 if layer(q) == 1 else bq3,
                                               8.0 ** -0.5, ALU.add, ALU.mult), key)
                    run_steps(q, head_steps(q))
                elif k == "moe0":
                    gating(q)
                    weigh(q, 0)
                    weigh(q, 1)
                elif k == "attn2":
                    key = ("q", q)
                    wait_t_full(dve, key)
                    free_t(v.tensor_scalar(qT[b][:, :], t_bank(key)[:, :], bq2, 128.0 ** -0.5, ALU.add, ALU.mult), key)
                    wait_s_full(dve, q, 0)
                    if q == 8:
                        dve.wait_ge(loaded["phi"], 16)
                    sc = scores_sb[:, q % 2, :, :]
                    v.scalar_tensor_tensor(sc, phi[:, TILES * b:TILES * b + TILES, :], coef[:, 1:2],
                                           slot(q, 0)[:, :, 0:SK], ALU.mult, ALU.add).then_inc(
                        s_free[S_USE[q, 0][0]], 1)
                    wait_s_read(dve, q, 0)
                    v.tensor_reduce(negmax[:, P_USE[q, 0] % NP, :], sc, AX.X, ALU.max,
                                    negate=True).then_inc(max_ready, 1)
                    reciprocals(q, 0)
                elif k == "moe3":
                    gating(q)

            def moe3_hidden(q, n):
                use = (q - 14) * F3N + n
                wait_s_full(dve, q, n)
                dve.wait_ge(silu_ready, use + 1)
                b3 = sb3 if n == 0 else eb3[:, n - 1:n]
                dst = h3[:, 0 if n == 0 else 1, :]
                if n == 0 and q == 15:
                    dve.wait_ge(y_done, F3N - 1)
                if n >= 2:
                    wait_t_read(dve, ("gb", q, n - 1))
                v.scalar_tensor_tensor(dst.rearrange("p (g c) -> p g c", g=2), slot(q, n)[:, 2:4, :], b3,
                                       a1[:, use % 2, :].rearrange("p (g c) -> p g c", g=2),
                                       ALU.add, ALU.mult).then_inc(s_free[S_USE[q, n][0]], 1)
                if n == 0:
                    return
                wait_s_read(dve, q, n)
                key = ("gb", q, n)
                wait_t_full(dve, key)
                if n >= 3:
                    dve.wait_ge(y_done, (q - 14) * (F3N - 1) + n - 1)
                elif n == 2 and q == 15:
                    dve.wait_ge(o_full, O_USE[14, 0] + 1)
                free_t(v.tensor_tensor(hg[:, n % 2, :], dst, t_bank(key)[:, :], ALU.mult), key)

            def rest(q):
                b, k = q % 2, kind(q)
                if k == "attn":
                    run_steps(q, rest_steps(q))
                elif k == "moe0":
                    for n in range(2, 16):
                        weigh(q, n)
                        if n % 4 == 2 and n > 4:
                            sum_experts(q, n // 4 - 1)
                elif k == "attn2":
                    key = ("main", q)
                    wait_t_full(dve, key)
                    free_t(v.tensor_copy(pT[:, 0, 0:2, :].rearrange("p a c -> p (a c)"), t_bank(key)[:, :]), key)
                elif q == 10:
                    dve.wait_ge(xnT_ready, 12)
                    for i in range(B):
                        tick(v.tensor_reduce(fsc[:, i:i + 1], xnT[i][:, :], AX.X, ALU.max, apply_absolute_value=True))
                    tick(v.tensor_reduce(am[:, 1:2], w_fp8, AX.X, ALU.max, apply_absolute_value=True))
                    settle()
                    v.tensor_tensor(am[:, 0:1], fsc[:, 0:1], fsc[:, 1:2], ALU.max).then_inc(am_ready, 1)
                    key = ("amax_t", q)
                    wait_t_full(dve, key)
                    free_t(v.tensor_reduce(am2[:, 0:1], t_bank(key)[0:2, 0:128], AX.X, ALU.max), key)
                    wait_t_read(dve, key)
                    v.tensor_scalar(am2[:, 2:4], ident[0:2, 0:2], am2[:, 0:1], None, ALU.mult).then_inc(am_ready, 1)
                    key = ("amax_b", q)
                    wait_t_full(dve, key)
                    free_t(v.tensor_scalar(fsc[:, 2:4], t_bank(key)[:, 0:2], 1e-12, None, ALU.max), key)
                    wait_t_read(dve, key)
                    link(v.reciprocal(fsc[:, 2:4], fsc[:, 2:4]))
                    link(v.tensor_scalar(fsc[:, 4:6], fsc[:, 2:4], 448.0, None, ALU.mult))
                    link(v.tensor_tensor(fsc[:, 6:7], fsc[:, 4:5], fsc[:, 5:6], ALU.mult))
                    link(v.reciprocal(fsc[:, 7:8], fsc[:, 6:7]))
                    s = X_SCALE[5]
                    link(v.tensor_tensor(fsc[:, 6:7], fsc[:, 7:8], tg[:, s:s + 1], ALU.mult))
                    quantise(w_fp8, fsc[:, 5:6], (fq[:, 0, 0:128], fq[:, 1, 0:128]), w8[:, :], quant_ready)
                    dve.wait_ge(quant_ready, 1)
                    for i in range(B):
                        quantise(xnT[i][:, :], fsc[:, 4:5], (fq[:, 0, :], fq[:, 1, :]), x8[:, i, :], quant_ready)
                        dve.wait_ge(quant_ready, i + 2)
                elif k == "moe3":
                    for n in range(F3N - 1):
                        moe3_hidden(q, n)

            def tail(q):
                b, k = q % 2, kind(q)
                half = range(TILES * b, TILES * b + TILES)
                if k == "attn":
                    run_steps(q, tail_steps(q))
                elif k == "moe0":
                    sum_experts(q, TILES - 1)
                elif k == "fp8":
                    key = ("fin", q)
                    wait_t_full(dve, key)
                    xs = x[:, half.start:half.stop, :]
                    free_t(v.scalar_tensor_tensor(xs.rearrange("p t d -> p (t d)"), t_bank(key)[:, :], fsc[:, 6:7],
                                                  xs.rearrange("p t d -> p (t d)"), ALU.mult, ALU.add), key)
                    wait_t_read(dve, key)
                    link(v.tensor_tensor(xs, xs, tg_bias[:, :].unsqueeze(1).broadcast_to([128, TILES, D]), ALU.add))
                elif k == "moe3":
                    moe3_hidden(q, F3N - 1)
                    key = ("fin", q)
                    wait_t_full(dve, key)
                    s = X_SCALE[7]
                    xs = x[:, half.start:half.stop, :].rearrange("p t d -> p (t d)")
                    v.scalar_tensor_tensor(xs, t_bank(key)[:, :], tg[:, s:s + 1], xs, ALU.mult,
                                           ALU.add).then_inc(x_final, 1)
                    if b == 0:
                        dve.wait_ge(x_final, 1)
                        free_t(v.memset(am2[0:1, 0:1], 0.0), key)
                else:
                    add_to_x(q, ("fin", q), half, 512)

            prepare0()
            constants()
            walk(head, tail, norm, rest)

        @block.scalar
        def _(act):
            a = nc.scalar.activation

            def copy(dst, src):
                return a(dst, src, ACT.Copy)

            def free_t(ins, key):
                ins.then_inc(t_free[T_USE[key][0]], 1)

            def load(name, dst, src):
                act.dma_start(dst, src).then_inc(loaded[name], 16)

            load("x", x[:, :, :], t["x"].rearrange("(t p) d -> p t d", p=128))
            load("wide", wide[:, :], t["wide"].broadcast_to([128, 155]))
            load("cols", cols[:, :], t["cols"])
            load("masks1", mask1_u8[:, :], t["mask1"].broadcast_to([128, B * SK]))
            load("masks3", mask3_i32[:, :], t["mask3"].broadcast_to([128, B * SK]))
            load("rows", rows[:, :], t["rows"])
            act.wait_ge(loaded["wide"], 16)
            a(tg[:, :], gates_in, ACT.Tanh).then_inc(tanh_ready, 1)

            def prepare0():
                for h in range(8):
                    key = ("k0", h)
                    wait_t_full(act, key)
                    free_t(copy(kT0[:, h, :], t_bank(key)[:, 0:B * KP]), key)
                for h in range(1, 8, 2):
                    key = ("a0", h)
                    wait_t_full(act, key)
                    free_t(a(a0[:, h, :, :].rearrange("p b k -> p (b k)"), t_bank(key)[:, 0:B * KP], ACT.Copy,
                             scale=64.0 ** -0.5), key)
                for b in range(B):
                    key = ("vo", b, 1)
                    wait_t_full(act, key)
                    free_t(copy(vo_main[:, b, 4:8, :].rearrange("p h d -> p (h d)"), t_bank(key)[:, :]), key)
                for b in range(B):
                    key = ("vr", b)
                    wait_t_full(act, key)
                    free_t(copy(vo_rem[0:RR, b, :, :].rearrange("p u d -> p (u d)"), t_bank(key)[0:RR, 0:256]), key)

            def prepare(key):
                wait_t_full(act, key)
                bank, i = t_bank(key), key[1]
                if key[0] == "k":
                    if i == 2:
                        last = a(kT2[:, :, :].rearrange("p b k -> p (b k)"), bank[:, 0:B * KP], ACT.Identity, bias=bk2)
                    else:
                        for u in range(4):
                            last = a(kb[i][:, u, :, :].rearrange("p b k -> p (b k)"), bank[:, 0:B * KP], ACT.Identity,
                                     scale=dmask[:, u:u + 1], bias=bk_masked[i][:, u:u + 1])
                else:
                    b = key[2]
                    if i == 2:
                        copy(v2m[:, b, :], bank[:, 0:128])
                        last = copy(v2r[:, b, :], bank[0:KR, 128:256])
                    else:
                        copy(vm[i][:, b, :, :].rearrange("p g (u c) -> p g u c", u=4)[:, :, :, 0:8],
                             bank[:, 0:128].rearrange("p (g u d) -> p g u d", g=4, u=4))
                        for g in range(4):
                            last = a(vr[i][:, b, :].rearrange("p (u c) -> p u c", u=4)[:, :, 8 * g:8 * g + 8],
                                     bank[0:RR, 128:256].rearrange("p (u c) -> p u c", u=4)[:, :, 8 * g:8 * g + 8],
                                     ACT.Copy, scale=rmask[0:RR, g:g + 1])
                free_t(last, key)

            def norm(q):
                key = ("ln", q)
                wait_t_full(act, key)
                copy(xnT[q % 2][:, :], t_bank(key)[:, :]).then_inc(xnT_ready, 1)
                act.wait_ge(xnT_ready, q + 1)
                free_t(copy(spare[:, 0:1], t_bank(key)[:, 0:1]), key)

            def exps(q, n):
                ring = P_USE[q, n] % NP
                if P_USE[q, n] >= NP:
                    old = P_KEYS[P_USE[q, n] - NP]
                    wait_t_full(act, ("t", *old) if kind(old[0]) == "attn" else ("rem", old[0]))
                act.wait_ge(max_ready, P_USE[q, n] + 1)
                if layer(q) == 1:
                    src = scores_sb[:, BIAS_USE[q, n] % 2, :, :]
                elif kind(q) == "attn2":
                    src = scores_sb[:, q % 2, :, :]
                else:
                    src = slot(q, n)
                for g in range(4):
                    last = a(probs[:, ring, :, g], src[:, g, 0:SK], ACT.Exp, bias=negmax[:, ring, g:g + 1],
                             accum_out=sums[:, ring, g:g + 1])
                if layer(q) == 1:
                    last.then_inc(bias_exp_done, 1)
                elif kind(q) == "attn2":
                    last.then_inc(exp_out, 1)
                else:
                    last.then_inc(s_free[S_USE[q, n][0]], 1)

            def run_steps(q, events):
                for what, n in events:
                    if what == "scores":
                        exps(q, n)
                    elif what == "transpose":
                        copy_turned(nc.scalar, copy, q, n)
                    elif what == "values":
                        use = O_USE[q, n]
                        act.wait_ge(o_full, use + 1)
                        if layer(q) == 0:
                            a(oT[:, use % 2, :], psO[:, 0:256], ACT.Identity, bias=bo0).then_inc(oT_ready, 1)
                        else:
                            copy(oT[:, use % 2, :], psO[:, 0:256]).then_inc(oT_ready, 1)
                        act.wait_ge(oT_ready, use + 1)
                        copy(spare[:, 1:2], psO[:, 0:1]).then_inc(o_free, 1)

            def gate_exp(q):
                act.wait_ge(exp_in, EXP_IN[q])
                ne = E0 if q < 4 else E3
                a(ex[:, :, 0:ne], lsel[:, :, 0:ne] if q < 4 else lg[:, :, 0:ne], ACT.Exp,
                  scale=1.0 if q < 4 else -1.0).then_inc(exp_out, 1)

            def silu(q, n):
                use = (q - 14) * F3N + n
                wait_s_full(act, q, n)
                if use >= 2:
                    wait_s_read(act, q if n >= 2 else q - 1, n - 2 if n >= 2 else n - 2 + F3N)
                b1 = sb1 if n == 0 else eb1[:, n - 1:n]
                a(a1[:, use % 2, :].rearrange("p (g c) -> p g c", g=2), slot(q, n)[:, 0:2, :], ACT.Silu,
                  bias=b1).then_inc(silu_ready, 1)

            def head(q):
                k = kind(q)
                if k == "attn":
                    run_steps(q, head_steps(q))
                elif k in ("moe0", "moe3"):
                    gate_exp(q)
                elif k == "lowrank":
                    key = ("p1", q)
                    wait_t_full(act, key)
                    if q == 6:
                        a(q1[32:33, :], xnT[0][32:33, :], ACT.Identity, scale=0.0, bias=1.0)
                    free_t(copy(p1, t_bank(key)[0:32, :]), key)
                elif k == "attn2":
                    exps(q, 0)

            def tail(q):
                k = kind(q)
                if k == "attn":
                    run_steps(q, tail_steps(q))
                elif k == "moe3":
                    silu(q, F3N - 1)
                    act.wait_ge(o_full, O_USE[q, 0] + 1)
                    a(oT3[:, :], psO[:, :], ACT.Identity, bias=sb2).then_inc(oT_ready, 1)
                    act.wait_ge(oT_ready, O_USE[q, 0] + 1)
                    copy(spare[:, 1:2], psO[:, 0:1]).then_inc(o_free, 1)

            def rest(q):
                k = kind(q)
                if k == "attn":
                    run_steps(q, rest_steps(q))
                elif q == 2:
                    act.wait_ge(consts_ready, 1)
                    act.wait_ge(zeroed, 2)
                    for key in PREP:
                        prepare(key)
                elif k == "lowrank":
                    for n in range(2):
                        wait_s_full(act, q, n)
                        for c in range(2):
                            ins = a(hidden[:, 2 * n + c, :].rearrange("p (g c) -> p g c", g=2),
                                    slot(q, n)[:, 2 * c:2 * c + 2, :], ACT.Gelu_apprx_tanh,
                                    bias=fb1[:, 2 * n + c:2 * n + c + 1])
                            ins.then_inc(hidden_ready, 1)
                        act.wait_ge(hidden_ready, (q - 6) * 4 + 2 * n + 2)
                        copy(spare[:, 2:3], slot(q, n)[:, 0, 0:1]).then_inc(s_free[S_USE[q, n][0]], 1)
                    key = ("q1", q)
                    wait_t_full(act, key)
                    free_t(copy(q1[0:32, :], t_bank(key)[0:32, :]), key)
                elif k == "attn2":
                    key = ("rem", q)
                    wait_t_full(act, key)
                    free_t(copy(pT[0:KR, 1, 0:2, :].rearrange("p a c -> p (a c)"), t_bank(key)[0:KR, :]), key)
                elif k == "moe3":
                    silu(q, 0)
                    key = ("gates", q)
                    silu(q, 1)
                    wait_t_full(act, key)
                    free_t(copy(gT[:, :], t_bank(key)[0:E3, :]), key)
                    for n in range(2, F3N - 1):
                        silu(q, n)

            prepare0()
            walk(head, tail, norm, rest)

        @block.gpsimd
        def _(pool):
            g = nc.gpsimd
            g.memset(expo[:, :], -0.5)
            g.memset(vT0_rem, 0.0).then_inc(zeroed, 1)

            def mask_bias(tile):
                if tile == 0:
                    pool.wait_ge(consts_ready, 1)
                pool.wait_ge(bias_loaded[tile], 16)
                g.tensor_tensor(bias1[:, tile % BR, :, :], bias1[:, tile % BR, :, :],
                                mask1[:, tile // TILES, :].unsqueeze(1).broadcast_to([128, 16, SK]),
                                ALU.add).then_inc(bias_masked, 1)

            def normalise(q, n):
                i = P_USE[q, n]
                pool.wait_ge(rsum_ready, i + 1)
                p = probs[:, i % NP, :, :]
                g.tensor_tensor(p, p, rsums[:, i % NP, :].unsqueeze(1).broadcast_to([128, SK, 4]),
                                ALU.mult).then_inc(probs_ready, 1)

            def run_steps(q, events):
                for what, n in events:
                    if what == "normalise":
                        normalise(q, n)
                        if q == 1 and n in (1, 3):
                            mask_bias(n // 2)
                        if layer(q) == 1 and n % 4 == 1 and TILES * (q % 2) + n // 4 + 2 < 8:
                            mask_bias(TILES * (q % 2) + n // 4 + 2)

            def norm(q):
                pool.wait_ge(eps_added, q + 1)
                g.tensor_tensor(rstd[:, :], vareps[:, :], expo[:, :], ALU.pow).then_inc(rstd_ready, 1)

            def add_quarters(q, first, last):
                for n in range(first, last):
                    tt, part = n // 4, n % 4
                    tile = TILES * (q % 2) + tt
                    if part == 0:
                        continue
                    m = 3 * tile + part - 1
                    wait_s_read(pool, q, 4 * tt)
                    wait_s_read(pool, q, n)
                    if m > 0:
                        pool.wait_ge(acc_added, m)
                    g.tensor_tensor(acc0[:, tile % 2, :], acc0[:, tile % 2, :], mult0[:, m % 2, :],
                                    ALU.add).then_inc(acc_added, 1)

            def head(q):
                k = kind(q)
                if k == "attn":
                    run_steps(q, head_steps(q))
                elif k == "attn2":
                    normalise(q, 0)
                elif k == "moe0":
                    add_quarters(q, 0, 2)

            def tail(q):
                if kind(q) == "attn":
                    run_steps(q, tail_steps(q))

            def rest(q):
                if kind(q) == "attn":
                    run_steps(q, rest_steps(q))
                elif kind(q) == "moe0":
                    if q == 2:
                        pool.wait_ge(o_full, O_USE[1, 1] + 1)
                        g.memset(vm[1][:, :, :, :], 0.0)
                        g.memset(vm[3][:, :, :, :], 0.0).then_inc(zeroed, 1)
                    add_quarters(q, 2, 16)

            walk(head, tail, norm, rest)


def kernel(**inputs):
    import numpy as np
    import concourse.bacc as bacc
    from concourse.bass_utils import run_bass_kernel_spmd

    i = {k: np.asarray(v) for k, v in inputs.items()}

    def heads(w):
        return w.reshape(128, 8, 128)

    ctx_pad = np.zeros((128, B, KP), np.float32)
    ctx_pad[:, :, :SK] = i["ctx_1024"].transpose(2, 0, 1)
    const = np.concatenate([
        np.eye(128), (np.arange(128)[:, None] % 32 // 8 == np.arange(4)[None, :]),
        np.tile(np.arange(E0), (128, TILES)), np.tile(np.arange(E3), (128, TILES)), np.ones((128, 128)),
        np.arange(128)[:, None] % 4 == np.arange(4)[None, :]],
        axis=1).astype(np.float32)
    pair_sel = (np.arange(E3)[:, None, None] == 2 * np.arange(E3 // 2)[None, :, None]
                + np.arange(128)[None, None, :] // 64).astype(np.float32)

    def hidden_major(w, shared):
        both = np.concatenate([shared[None], w.reshape(E3 // 2, 128, 128)])
        return both.transpose(2, 0, 1)

    arrays = {
        "const": const, "pair_sel": pair_sel, "ctxT": ctx_pad,
        "x": i["x"].reshape(B * S, D),
        "wk0": heads(i["L0_xattn_Wk"]), "wv0": heads(i["L0_xattn_Wv"]),
        "wq0T": heads(i["L0_xattn_Wq"]).transpose(2, 1, 0),
        "wo0": i["L0_xattn_Wo"].reshape(8, 128, D).transpose(1, 0, 2),
        "routerT": i["L0_ffn_router_w"].T, "w_exp0": i["L0_ffn_expert_weights"].transpose(1, 0, 2),
        "sq": np.stack([i["L1_xattn_Wq"], i["L1_xattn_Wk"], i["L1_xattn_Wv"], i["L1_xattn_Wo"],
                        i["L2_xattn_Wq"].T, i["L2_xattn_Wk"].T, i["L2_xattn_Wv"].T, i["L2_ffn_weight"].T,
                        i["L3_xattn_q_w"].T, i["L3_xattn_k_w"].T, i["L3_xattn_v_w"].T], axis=1),
        "fside4": i["fside_Bx16xSxS2_0"], "phi": i["fside_BxSxS2_0"].reshape(B * S, SK),
        "mask1": i["mask_BxS2_bk0"].reshape(1, B * SK),
        "mask3": i["mask_BxS2_ik0"].reshape(1, B * SK),
        "cols": np.concatenate([
            np.stack([i[n] for n in ("L0_xattn_bo", "L1_xattn_bq", "L1_xattn_bk", "L2_xattn_bq", "L2_xattn_bk",
                                     "L3_xattn_q_b", "L3_xattn_k_b", "L3_ffn_sb1", "L3_ffn_sb3", "L3_ffn_sb2")],
                     axis=1),
            i["L1_ffn_b1"].reshape(4, 128).T, i["L3_ffn_b1"].reshape(8, 128).T, i["L3_ffn_b3"].reshape(8, 128).T],
            axis=1),
        "rows": np.concatenate([i[n] for n in ("L1_xattn_bv", "L1_xattn_bo", "L2_xattn_bv", "L3_xattn_v_b")])[None],
        "wide": np.concatenate([i["L2_ffn_bias"], i["L3_ffn_expert_bias"], i["g_xattn"], i["g_ffn"],
                                i["L2_xattn_beta_risk"].reshape(1), i["L2_xattn_beta_prio"].reshape(1),
                                i["L2_xattn_beta_impl"].reshape(1)])[None],
        "u1": i["L1_ffn_U1"], "v1": i["L1_ffn_V1"],
        "u2": i["L1_ffn_U2"].reshape(4, 128, 32).transpose(1, 0, 2),
        "v2b": np.concatenate([i["L1_ffn_V2"], i["L1_ffn_b2"][None]]),
        "gate3T": i["L3_ffn_gate_w"].T,
        "w1T": hidden_major(i["L3_ffn_w1"], i["L3_ffn_sw1"]),
        "w3T": hidden_major(i["L3_ffn_w3"], i["L3_ffn_sw3"]),
        "w2T": np.concatenate([i["L3_ffn_sw2"].T[None],
                               i["L3_ffn_w2"].transpose(0, 2, 1).reshape(E3 // 2, 128, D)]).transpose(1, 0, 2),
        "b2_exp": i["L3_ffn_b2"],
    }
    arrays = {f"in_{k}": np.ascontiguousarray(v) for k, v in arrays.items()}
    nc = bacc.Bacc("TRN2", target_bir_lowering=False, num_devices=1)
    t = {k[3:]: nc.dram_tensor(k, v.shape, mybir.dt.from_np(v.dtype), kind="ExternalInput").ap()
         for k, v in arrays.items()}
    out = nc.dram_tensor("out_x", (B, S, D), F32, kind="ExternalOutput").ap()
    build(nc, t, out)
    r = run_bass_kernel_spmd(nc, [arrays], core_ids=[0])
    return r.results[0]["out_x"]
```

```python
from contextlib import ExitStack

import concourse.bass as bass
from concourse import mybir

F32 = mybir.dt.float32
BF16 = mybir.dt.bfloat16
I32 = mybir.dt.int32
U32 = mybir.dt.uint32
U8 = mybir.dt.uint8
ALU = mybir.AluOpType
ACT = mybir.ActivationFunctionType
AX = mybir.AxisListType

B, S, D, SK = 2, 512, 128, 154
KM, KR = 128, SK - 128
RR = 4 * KR
KP = 160
TILES = S // 128
HALVES = 16
HT = S
BR = 3
NP = 6
E0, E3 = 32, 16
F3N = 1 + E3 // 2
NEG = -1.0e30
KINDS = ["attn", "moe0", "attn", "lowrank", "attn2", "fp8", "attn", "moe3"]
UNITS = {0: 8, 2: 16, 6: 16}
LAGS = {0: 3, 2: 2, 6: 2}
PARTS = [(0, 0), (0, 1), (1, 0), (1, 1), (0, 2), (2, 0), (1, 2)]
CR = 16 * len(PARTS) + 1


def kind(q):
    return KINDS[q // 2]


def layer(q):
    return q // 4


def steps(q, first, last):
    n_units, lag = UNITS[q // 2], LAGS[q // 2]
    pair0 = n_units // 2 - 1
    for k in range(first, last):
        if k < n_units:
            yield "scores", k
        if q // 2 == 0 and 2 <= k <= n_units + 1:
            yield "normalise", k - 2
        if k >= lag:
            yield "transpose", k - lag
        if q // 2 > 0 and k in (pair0 + 2, n_units + 1):
            yield "sums", int(k == n_units + 1)
        if q // 2 > 0 and k == pair0 + 3:
            yield "expand", 0
        if k == pair0 + 5:
            yield "values", 0
        if k == pair0 + 7:
            yield "finish", 0
    if last == n_units + lag:
        if q // 2 > 0:
            yield "expand", 1
        yield "values", 1
        yield "finish", 1


def head_steps(q):
    return steps(q, 0, 2)


def rest_steps(q, part):
    d = 2 if layer(q) == 0 else 3
    return steps(q, 2 + part * d, 2 + part * d + d if part < 2 else UNITS[q // 2])


def tail_steps(q):
    return steps(q, UNITS[q // 2], UNITS[q // 2] + LAGS[q // 2])


def rest_units(part):
    return (range(2, 5), range(5, 8), range(8, 16))[part]


def walk(head, tail, stats, turn, project, rest):
    for part in (stats, turn, project):
        part(0)
    for q in range(HALVES):
        head(q)
        if q > 0:
            tail(q - 1)
        for i, part in enumerate((stats, turn, project)):
            if q + 1 < HALVES:
                part(q + 1)
            rest(q, i)
    tail(HALVES - 1)


PREP = [("k", 1), ("v", 1, 0), ("v", 1, 1), ("k", 3), ("v", 3, 0), ("v", 3, 1), ("k", 2), ("v", 2, 0), ("v", 2, 1)]


def moe3_units(part):
    return (range(1, 3), range(3, 5), range(5, F3N - 1))[part]


def t_uses():
    keys = []
    for h in range(8):
        keys += [("k0", h), ("v0", h)]
    keys += [("a0", h) for h in range(8)]
    keys += [("vo", b, i) for b in range(B) for i in range(2)] + [("vr", b) for b in range(B)]

    def of_steps(q, events):
        for what, n in events:
            if what == "transpose":
                keys.append(("t", q, n))
            if what == "expand":
                keys.extend([("rt", q, n), ("rx", q, n)])
            if what == "finish":
                keys.append(("fin", q, n))

    def head(q):
        if kind(q) == "attn":
            of_steps(q, head_steps(q))

    def tail(q):
        if kind(q) == "attn":
            of_steps(q, tail_steps(q))
        elif kind(q) != "moe0":
            keys.append(("fin", q))

    def turn(q):
        keys.append(("ln", q))

    def project(q):
        if kind(q) in ("attn", "attn2") and q >= 2:
            keys.append(("q", q))
        elif kind(q) in ("moe0", "moe3"):
            keys.append(("logits", q))
        elif kind(q) == "lowrank":
            keys.append(("p1", q))

    def rest(q, part):
        if kind(q) == "attn":
            of_steps(q, rest_steps(q, part))
        elif q == 2:
            keys.extend(PREP[3 * part:3 * part + 3])
        elif kind(q) == "lowrank" and part == 0:
            keys.append(("q1", q))
        elif kind(q) == "attn2" and part == 0:
            keys.extend([("main", q), ("rem", q)])
        elif q == 10 and part == 2:
            keys.extend([("amax_t", q), ("amax_b", q)])
        elif kind(q) == "moe3":
            if part == 0:
                keys.extend([("gates", q), ("gb", q, 1)])
            keys.extend([("gb", q, n + 1) for n in moe3_units(part)])

    walk(head, tail, lambda q: None, turn, project, rest)
    return keys


def s_uses():
    keys = []
    for q in range(HALVES):
        n = {"attn": UNITS.get(q // 2), "moe0": 16, "lowrank": 2, "attn2": 1, "fp8": 0, "moe3": F3N}[kind(q)]
        keys += [(q, i) for i in range(n)]
    return keys


def build(nc, t, out):
    T_USE = {key: (i % 2, i // 2) for i, key in enumerate(t_uses())}
    S_USE = {key: (i % 2, i // 2) for i, key in enumerate(s_uses())}
    P_KEYS = [(q, n) for q in range(HALVES) for n in range(UNITS[q // 2] if kind(q) == "attn" else
                                                           1 if kind(q) == "attn2" else 0)]
    P_USE = {key: i for i, key in enumerate(P_KEYS)}
    M_USE = {key: i for i, key in enumerate((q, tt) for q in range(HALVES) if kind(q) == "attn" for tt in range(TILES))}
    O_KEYS = [(q, p) for q in range(HALVES) if kind(q) == "attn" for p in range(2)] + [(q, 0) for q in (14, 15)]
    O_USE = {key: i for i, key in enumerate(O_KEYS)}
    PAIR_USE = {key: i for i, key in enumerate((q, p) for q in (4, 5, 12, 13) for p in range(2))}
    P_READY = {8: 17, 9: 18}
    BIAS_USE = {key: i for i, key in enumerate((q, n) for q in (4, 5) for n in range(16))}

    with ExitStack() as ctx:
        def sb(name, shape, dt=F32):
            return ctx.enter_context(nc.sbuf_tensor(name, shape, dt))

        def ps(name, cols):
            return ctx.enter_context(nc.psum_tensor(name, [128, cols], F32))

        def sem(name):
            return ctx.enter_context(nc.semaphore(name))

        const = sb("const", [128, 584])
        head_sel = const[0:16, 456:584]
        rmask = const[:, 452:456]
        ident, dmask, iota32, iota16, ones = (const[:, 0:128], const[:, 128:132], const[:, 132:260],
                                              const[:, 260:324], const[:, 324:452])
        x = sb("x", [128, 8, D])
        ctxT = sb("ctxT", [128, B, KP])
        ctx_all = ctxT[:, :, :].rearrange("p b k -> p (b k)")
        cols = sb("cols", [128, 30])
        (bo0, bq1, bk1, bq2, bk2, bq3, bk3, sb1, sb3, sb2) = (cols[:, i:i + 1] for i in range(10))
        fb1 = cols[:, 10:14]
        eb1, eb3 = cols[:, 14:22], cols[:, 22:30]
        rows = sb("rows", [1, 4 * 128])
        bv1, bo1, bv2, bv3 = (rows[0:1, 128 * i:128 * i + 128] for i in range(4))
        wide = sb("wide", [128, 155])
        b_fp8, ebias, gates_in, betas = wide[:, 0:128], wide[:, 128:144], wide[:, 144:152], wide[:, 152:155]
        mask_b = {i: sb(f"mask_b{i}", [128, B * SK], BF16) for i in (1, 3)}
        scores_sb = sb("scores_sb", [128, 2, 4, SK])
        masks = scores_sb[:, :, :, :].rearrange("p i g k -> p (i g k)").rearrange("p (n k) -> p n k", n=4)
        mask3_i32, mask3f, mask1 = masks[:, 0, :].bitcast(I32), masks[:, 1, :], masks[:, 2, :].rearrange(
            "p (b k) -> p b k", b=B)
        mask1_u8 = masks[:, 3, 0:B * SK // 4].bitcast(U8)
        early = sb("early", [128, 4, 8, 128])
        wq0T, wk0, wv0, wo0 = (early[:, i] for i in range(4))
        routerT = sb("routerT", [128, E0])
        experts = sb("experts", [128, E0 * D])
        w_exp0 = experts[:, :].rearrange("p (e d) -> p e d", e=E0)
        w1T, w3T, w2T = (experts[:, 1152 * i:1152 * i + 1152].rearrange("p (n c) -> p n c", n=F3N) for i in range(3))
        gT = experts[0:E3, 3456:3456 + HT]
        sq = sb("sq", [128, 12, D])
        wq1, wk1, wv1, wo1, wq2, wk2, wv2, w_fp8, wq3, wk3, wv3 = (sq[:, i, :] for i in range(11))
        u1 = sb("u1", [128, 32])
        v1 = sb("v1", [32, 512])
        u2 = sb("u2", [128, 4, 32])
        v2b = sb("v2b", [33, D])
        gate3T = sb("gate3T", [128, E3])
        b2_exp = sb("b2_exp", [E3, D])
        bias1 = sb("bias1", [128, BR, 16, SK])
        phi = sb("phi", [128, 8, SK])
        phi_flat = phi[:, :, :].rearrange("p t k -> p (t k)")
        pair_sel = phi_flat[0:E3, 0:E3 // 2 * 128].rearrange("p (n c) -> p n c", n=E3 // 2)

        keyed = sb("keyed", [128, 4 * 8 * KP])
        a0 = keyed[:, 0:2560].rearrange("p (h b k) -> p h b k", h=8, b=B)
        vo_main = keyed[:, 2560:4608].rearrange("p (b h d) -> p b h d", b=B, h=8)
        vo_rem = keyed[:, 4608:5120].rearrange("p (b u d) -> p b u d", b=B, u=2)
        vm = {i: keyed[:, 640 * (i - 1):640 * (i - 1) + 1280].rearrange("p (b g c) -> p b g c", b=B, g=4)
              for i in (1, 3)}
        vr = {i: sb(f"vr{i}", [RR, B, 128]) for i in (1, 3)}
        ctx_rem = sb("ctx_rem", [128, B, RR])
        ks = {1: sb("ks1", [128, 8, 2, B * SK], BF16),
              3: keyed[:, 2560:2560 + 2464].bitcast(BF16).rearrange("p (a h k) -> p a h k", a=8, h=2)}
        kT2 = sb("kT2", [128, B, KP])
        v2m = sb("v2m", [128, B, D])
        v2r = sb("v2r", [KR, B, D])
        tg = sb("tg", [128, 8])
        tg_bias = sb("tg_bias", [128, D])
        coef = sb("coef", [128, 2])
        all_masked = sb("all_masked", [128, 2])
        expo = sb("expo", [128, 4])

        xnT = [sb(f"xnT{b}", [128, HT]) for b in range(B)]
        qT = sb("qT", [128, HT])
        parts = sb("parts", [128, 3, HT], BF16)
        left = sb("left", [128, HT])
        xn = sb("xn", [128, TILES, D])
        stats = sb("stats", [128, TILES, 6])
        meanvar = sb("meanvar", [128, TILES, 2])
        vareps = sb("vareps", [128, TILES])
        rstd = sb("rstd", [128, TILES])
        probs = sb("probs", [128, NP, SK, 4])
        negmax = sb("negmax", [128, NP, 4])
        sums = sb("sums", [128, NP, 4])
        pair_sums = sb("pair_sums", [128, 2, 2, 16])
        pair_rsums = sb("pair_rsums", [128, 2, 2, 16])
        rT = sb("rT", [16, 256])
        rexp = sb("rexp", [128, 2, 256])
        rsums = sb("rsums", [128, NP, 4])
        pT = sb("pT", [128, 2, 20, 256])
        oT = sb("oT", [128, 2, 256])
        spare = sb("spare", [128, 4])
        kT0 = pT[:, 0, 0:10, :].rearrange("p a c -> p (a c)").rearrange("p (h k) -> p h k", h=8)
        vT0 = pT[:, 0, 10:20, :].rearrange("p a c -> p (a c)").rearrange("p (h b k) -> p h b k", h=8, b=B)
        vT0_rem = pT[:, 1, 0:8, 0:B * RR].rearrange("p h (b c) -> p h b c", b=B)
        qs = [early[:, 2 * i:2 * i + 2].rearrange("p i h c -> p (i h c)").bitcast(BF16).rearrange(
            "p (a c) -> p a c", a=8) for i in range(2)]
        mult0, acc0 = (early[:, 2 * i:2 * i + 2].rearrange("p i h c -> p i (h c)") for i in range(2))
        red0 = sb("red0", [128, D])
        lg = sb("lg", [128, TILES, 32])
        lsel = sb("lsel", [128, TILES, 32])
        ex = sb("ex", [128, TILES, 32])
        hit = sb("hit", [128, 2, TILES, 32])
        gate = sb("gate", [128, 2, TILES, 32])
        top8 = sb("top8", [128, TILES, 8])
        idx8 = sb("idx8", [128, TILES, 8], U32)
        idxf = sb("idxf", [128, TILES, 2])
        gsum = sb("gsum", [128, 2, TILES])
        work = bias1[:, :, :, :].rearrange("p i h k -> p (i h k)")
        hidden = work[:, 0:2048].rearrange("p (n c) -> p n c", n=4)
        fq = work[:, 5120:6144].rearrange("p (n c) -> p n c", n=2)
        p1 = fq[0:32, 0, :]
        q1 = fq[0:33, 1, :]
        a1, h3, hg = (work[:, c:c + 1024].rearrange("p (n c) -> p n c", n=2) for c in (3072, 4096, 5120))
        oT3 = work[:, 6144:6656]
        x8 = work[:, 2048:2560].bitcast(BF16).rearrange("p (b c) -> p b c", b=B)
        am = sb("am", [128, 2])
        am2 = sb("am2", [2, 4])
        fsc = sb("fsc", [128, 8])
        w8 = sb("w8", [128, 128], BF16)

        psS = ps("psS", 2048)
        slot_view = psS[:, :].rearrange("p (s g c) -> p s g c", s=2, g=4)
        psT = [ps("psT0", 512), ps("psT1", 512)]
        psO = ps("psO", 512)
        psM = ps("psM", 512)

        LOADS = ["const", "ctxT", "x", "wk0", "wv0", "wq0T", "wo0", "cols", "wide", "rows", "routerT", "w_exp0",
                 "masks1", "masks3", "sq", "phi", "u1", "v1", "u2", "v2b", "pair_sel", "gate3T", "w1T", "w3T",
                 "w2T", "b2_exp"]
        loaded = {n: sem(f"loaded_{n}") for n in LOADS}
        bias_loaded = [sem(f"bias_loaded{i}") for i in range(8)]
        t_full, t_free = ([sem(f"t_{w}{i}") for i in range(2)] for w in ("full", "free"))
        s_full, s_free = ([sem(f"s_{w}{i}") for i in range(2)] for w in ("full", "free"))
        m_full, m_free, o_full, o_free = (sem(n) for n in ("m_full", "m_free", "o_full", "o_free"))
        dve_done = sem("dve_done")
        pool_done = sem("pool_done")
        zeroed = sem("zeroed")
        consts_ready = sem("consts_ready")
        tanh_ready = sem("tanh_ready")
        eps_added = sem("eps_added")
        rstd_ready = sem("rstd_ready")
        xn_ready = sem("xn_ready")
        xnT_ready = sem("xnT_ready")
        max_ready = sem("max_ready")
        bias_exp_done = sem("bias_exp_done")
        rsum_ready = sem("rsum_ready")
        probs_ready = sem("probs_ready")
        split = sem("split")
        q_stacked = [sem(f"q_stacked{i}") for i in range(4)]
        k_stacked = {i: sem(f"k_stacked{i}") for i in (1, 3)}
        ones_set = sem("ones_set")
        parts_saved = sem("parts_saved")
        sums_ready = sem("sums_ready")
        rexp_ready = sem("rexp_ready")
        exp_in = sem("exp_in")
        exp_out = sem("exp_out")
        gate_ready = sem("gate_ready")
        acc_first = sem("acc_first")
        mult_ready = sem("mult_ready")
        acc_added = sem("acc_added")
        acc_read = sem("acc_read")
        hidden_ready = sem("hidden_ready")
        q1_ready = sem("q1_ready")
        silu_ready = sem("silu_ready")
        y_done = sem("y_done")
        am_ready = sem("am_ready")
        quant_ready = sem("quant_ready")
        x_final = sem("x_final")
        stored = sem("stored")

        def t_bank(key):
            return psT[T_USE[key][0]]

        def wait_t_free(eng, key):
            i, n = T_USE[key]
            if n > 0:
                eng.wait_ge(t_free[i], n)

        def wait_t_full(eng, key):
            i, n = T_USE[key]
            eng.wait_ge(t_full[i], n + 1)

        def wait_t_read(eng, key):
            i, n = T_USE[key]
            eng.wait_ge(t_free[i], n + 1)

        def slot(q, n):
            return slot_view[:, S_USE[q, n][0]]

        def wait_s_free(eng, q, n):
            i, k = S_USE[q, n]
            if k > 0:
                eng.wait_ge(s_free[i], k)

        def wait_s_full(eng, q, n):
            i, k = S_USE[q, n]
            eng.wait_ge(s_full[i], k + 1)

        def wait_s_read(eng, q, n):
            i, k = S_USE[q, n]
            eng.wait_ge(s_free[i], k + 1)

        def wait_exp_done(eng, q, n):
            if layer(q) == 1:
                eng.wait_ge(bias_exp_done, BIAS_USE[q, n] + 1)
            elif kind(q) == "attn2":
                eng.wait_ge(exp_out, EXP_OUT[q])
            else:
                wait_s_read(eng, q, n)

        EXP_IN = {2: 1, 3: 2, 14: 3, 15: 4}
        EXP_OUT = {2: 1, 3: 2, 8: 3, 9: 4, 14: 5, 15: 6}
        STACKS = {("k", 1): 0, ("k", 3): 1, 4: 2, 5: 3, 12: 4, 13: 5}
        Q_STACK = {4: 0, 5: 1, 12: 2, 13: 3}
        LAST_STACK = {("k", 3): ("k", 1), 4: ("k", 3), 5: 4, 12: 5, 13: 12}

        def wait_stacked(eng, key):
            if key in Q_STACK:
                eng.wait_ge(q_stacked[Q_STACK[key]], 16 * len(PARTS))
            else:
                eng.wait_ge(k_stacked[key[1]], 16 * (2 * len(PARTS) + 1))

        X_SCALE = {0: 0, 1: 4, 2: 1, 3: 5, 4: 2, 5: 6, 6: 3, 7: 7}

        def turned_by(q, n):
            if layer(q) == 3:
                return "scalar" if n % 4 == 0 else "vector"
            return "scalar" if n % 2 == 0 else "vector"

        def rem_turned_by(q):
            return "vector" if layer(q) == 3 else "scalar"

        def tile_of(q, n):
            return n // (UNITS[q // 2] // TILES), n % (UNITS[q // 2] // TILES)

        def copy_turned(eng, copy, q, n):
            tt, u = tile_of(q, n)
            nu = UNITS[q // 2] // TILES
            p, cols_of = tt // 2, slice(tt % 2 * 128, tt % 2 * 128 + 128)
            me = "scalar" if eng is nc.scalar else "vector"
            use = O_USE[q, p]
            if turned_by(q, n) == me:
                if use >= 2:
                    eng.wait_ge(o_full, use - 1)
                wait_t_full(eng, ("t", q, n))
                copy(pT[:, use % 2, 4 * u:4 * u + 4, cols_of],
                     t_bank(("t", q, n))[:, :].rearrange("p (g c) -> p g c", g=4)).then_inc(
                    t_free[T_USE["t", q, n][0]], 1)
            if u == nu - 1 and rem_turned_by(q) == me:
                if use >= 2:
                    eng.wait_ge(o_full, use - 1)
                eng.wait_ge(m_full, M_USE[q, tt] + 1)
                copy(pT[0:RR, use % 2, 4 * nu:5 * nu, cols_of],
                     psM[0:RR, 0:128 * nu].rearrange("p (u c) -> p u c", u=nu)).then_inc(m_free, 1)

        block = ctx.enter_context(nc.Block())

        @block.sync
        def _(sp):
            def load(name, dst, src):
                sp.dma_start(dst, src).then_inc(loaded[name], 16)

            load("const", const[:, :], t["const"])
            load("ctxT", ctxT[:, :, :], t["ctxT"])
            load("wk0", wk0[:, :, :], t["wk0"])
            load("wv0", wv0[:, :, :], t["wv0"])
            load("wq0T", wq0T[:, :, :], t["wq0T"])
            load("wo0", wo0[:, :, :], t["wo0"])
            load("routerT", routerT[:, :], t["routerT"])
            load("w_exp0", w_exp0[:, :, :], t["w_exp0"])
            load("sq", sq[:, 0:11, :], t["sq"])

            def load_bias(i):
                b, tt = i // TILES, i % TILES
                src = t["fside4"][b, :, 128 * tt:128 * tt + 128, :].rearrange("h p k -> p h k")
                sp.dma_start(bias1[:, i % BR, :, :], src).then_inc(bias_loaded[i], 16)

            for i in range(BR):
                load_bias(i)
            load("phi", phi[:, :, :], t["phi"].rearrange("(t p) k -> p t k", p=128))
            for name, dst in (("u1", u1), ("v1", v1), ("u2", u2), ("v2b", v2b), ("gate3T", gate3T),
                              ("b2_exp", b2_exp)):
                load(name, dst[:], t[name])

            def save_parts(key, n):
                sp.wait_ge(split, STACKS[key] + 1)
                if STACKS[key] > 0:
                    wait_stacked(sp, LAST_STACK[key])
                sp.dma_start(t["parts"][:, :, 0:n], parts[:, :, 0:n]).then_inc(parts_saved, 16)
                sp.wait_ge(parts_saved, 16 * (STACKS[key] + 1))

            def stack_keys(i):
                save_parts(("k", i), B * SK)
                src = t["parts"][:, :, 0:B * SK].rearrange("(a h d) n k -> h d a n k", h=2, d=8)
                for c, (_, part) in enumerate(PARTS):
                    for h in range(2):
                        r0 = 16 * c + 8 * h
                        sp.dma_start(ks[i][r0:r0 + 8, :, h, :], src[h, :, :, part, :]).then_inc(k_stacked[i], 16)
                sp.dma_start(ks[i][CR - 1:CR, :, :, :].rearrange("p a h k -> p (a h) k"),
                             mask_b[i][0:1, :].unsqueeze(1).broadcast_to([1, 16, B * SK])).then_inc(k_stacked[i], 16)

            def stack_queries(q):
                save_parts(q, HT)
                if layer(q) == 1:
                    sp.wait_ge(ones_set, q - 3)
                if q >= 12:
                    wait_s_full(sp, q - 8, UNITS[6] - 1)
                src = t["parts"][:, :, :].rearrange("(a r) n c -> r a n c", r=16)
                for c, (part, _) in enumerate(PARTS):
                    sp.dma_start(qs[q % 2][16 * c:16 * c + 16, :, :], src[:, :, part, :]).then_inc(
                        q_stacked[Q_STACK[q]], 16)

            sp.wait_ge(consts_ready, 1)
            stack_keys(1)
            stack_keys(3)
            wait_s_full(sp, 3, 15)
            for name, dst in (("w1T", w1T), ("w3T", w3T), ("w2T", w2T)):
                load(name, dst, t[name])
            stack_queries(4)
            for i in range(BR, 8):
                if i == BR + 2:
                    stack_queries(5)
                old = i - BR
                wait_s_read(sp, 4 + old // TILES, 4 * (old % TILES) + 3)
                load_bias(i)
            sp.wait_ge(am_ready, 1)
            load("pair_sel", pair_sel, t["pair_sel"])
            stack_queries(12)
            stack_queries(13)
            for b in range(B):
                sp.wait_ge(x_final, b + 1)
                sp.dma_start(out[b].rearrange("(t p) d -> p t d", p=128),
                             x[:, TILES * b:TILES * b + TILES, :]).then_inc(stored, 16)
            sp.wait_ge(stored, 32)

        @block.tensor
        def _(pe):
            mm = nc.tensor.matmul

            def begin_t(key):
                wait_t_free(pe, key)
                return t_bank(key)

            def end_t(ins, key):
                ins.then_inc(t_full[T_USE[key][0]], 1)

            def prepare0():
                pe.wait_ge(loaded["const"], 16)
                pe.wait_ge(loaded["ctxT"], 16)
                pe.wait_ge(loaded["wk0"], 16)
                pe.wait_ge(loaded["wv0"], 16)
                for h in range(8):
                    for key, w in ((("k0", h), wk0), (("v0", h), wv0)):
                        bank = begin_t(key)
                        end_t(mm(bank[:, 0:B * KP], w[:, h, :], ctx_all, start=True, stop=True), key)
                pe.wait_ge(loaded["wq0T"], 16)
                for h in range(8):
                    key = ("a0", h)
                    bank = begin_t(key)
                    wait_t_read(pe, ("k0", h))
                    end_t(mm(bank[:, 0:B * KP], wq0T[:, h, :], kT0[:, h, :], start=True, stop=True), key)
                pe.wait_ge(loaded["wo0"], 16)
                for b in range(B):
                    for i in range(2):
                        key = ("vo", b, i)
                        bank = begin_t(key)
                        for g in range(4):
                            h = 4 * i + g
                            wait_t_read(pe, ("v0", h))
                            last = mm(bank[:, 128 * g:128 * g + 128], vT0[:, h, b, 0:KM], wo0[:, h, :],
                                      start=True, stop=True)
                        end_t(last, key)
                for b in range(B):
                    key = ("vr", b)
                    bank = begin_t(key)
                    for u in range(2):
                        for g in range(4):
                            h = 4 * u + g
                            last = mm(bank[0:RR, 128 * u:128 * u + 128], vT0_rem[:, h, b, :], wo0[:, h, :],
                                      start=g == 0, stop=g == 3)
                    end_t(last, key)

            def prepare(key):
                bank = begin_t(key)
                i = key[1]
                wk, wv, bv = {1: (wk1, wv1, bv1), 2: (wk2, wv2, bv2), 3: (wk3, wv3, bv3)}[i]
                if key[0] == "k":
                    last = mm(bank[:, 0:B * KP], wk, ctx_all, start=True, stop=True)
                else:
                    b = key[2]
                    mm(bank[:, 0:128], ctxT[:, b, 0:KM], wv, start=True, stop=False)
                    mm(bank[:, 0:128], ones[0:1, :], bv, start=False, stop=True)
                    lhs = ctxT[:, b, KM:SK] if i == 2 else ctx_rem[:, b, :]
                    o = bank[0:lhs.shape[1], 128:256]
                    mm(o, lhs, wv, start=True, stop=False)
                    last = mm(o, ones[0:1, 0:lhs.shape[1]], bv, start=False, stop=True)
                end_t(last, key)

            def scores(q, n):
                b, i = q % 2, layer(q)
                tt, u = tile_of(q, n)
                wait_s_free(pe, q, n)
                sl = slot(q, n)
                tok = slice(128 * tt, 128 * tt + 128)
                if i == 0:
                    for g in range(4):
                        last = mm(sl[:, g, 0:SK], xnT[b][:, tok], a0[:, 4 * u + g, b, 0:SK], start=True, stop=True)
                else:
                    for g in range(2):
                        last = mm(sl[:, 2 * g:2 * g + 2, 0:SK], qs[b][0:CR, 2 * u + g, tok],
                                  ks[i][0:CR, 2 * u + g, :, SK * b:SK * b + SK], start=True, stop=True)
                last.then_inc(s_full[S_USE[q, n][0]], 1)

            def expand(q, p):
                use = O_USE[q, p]
                key = ("rt", q, p)
                bank = begin_t(key)
                pe.wait_ge(sums_ready, PAIR_USE[q, p] + 1)
                for c in range(2):
                    last = nc.tensor.transpose(bank[0:16, 128 * c:128 * c + 128], pair_rsums[:, use % 2, c, :], ident)
                end_t(last, key)
                wait_t_read(pe, key)
                key = ("rx", q, p)
                bank = begin_t(key)
                end_t(mm(bank[:, 0:256], head_sel, rT[:, :], start=True, stop=True), key)

            def turn_probs(q, n):
                tt, u = tile_of(q, n)
                key = ("t", q, n)
                if layer(q) == 0:
                    pe.wait_ge(probs_ready, P_USE[q, n] + 1)
                else:
                    wait_exp_done(pe, q, n)
                if u == 0 and M_USE[q, tt] > 0:
                    pe.wait_ge(m_free, M_USE[q, tt])
                p = probs[:, P_USE[q, n] % NP]
                last = nc.tensor.transpose(psM[0:RR, 128 * u:128 * u + 128],
                                           p[:, KM:SK, :].rearrange("p k g -> p (k g)"), ident)
                if u == UNITS[q // 2] // TILES - 1:
                    last.then_inc(m_full, 1)
                bank = begin_t(key)
                for g in range(4):
                    last = nc.tensor.transpose(bank[:, 128 * g:128 * g + 128], p[:, 0:KM, g], ident)
                end_t(last, key)

            def values(q, p):
                b, i, nu = q % 2, layer(q), UNITS[q // 2] // TILES
                use = O_USE[q, p]
                for n in range(p * 2 * nu, (p + 1) * 2 * nu):
                    if n >= (p + 1) * 2 * nu - 4:
                        wait_t_read(pe, ("t", q, n))
                pe.wait_ge(m_free, M_USE[q, 2 * p + 1] + 1)
                if use > 0:
                    pe.wait_ge(o_free, use)
                src = pT[:, use % 2]
                if i == 0:
                    for c in range(8):
                        mm(psO[:, 0:256], vo_main[:, b, c, :], src[:, c, :], start=c == 0, stop=False)
                    for u in range(2):
                        last = mm(psO[:, 0:256], vo_rem[0:RR, b, u, :], src[0:RR, 8 + u, :], start=False, stop=u == 1)
                else:
                    for g in range(4):
                        for u in range(nu):
                            mm(psO[32 * u:32 * u + 32, 0:256], vm[i][:, b, u, 32 * g:32 * g + 32],
                               src[:, 4 * u + g, :], start=g == 0, stop=False, skip_group_check=True)
                    for u in range(nu):
                        last = mm(psO[32 * u:32 * u + 32, 0:256], vr[i][:, b, 32 * u:32 * u + 32],
                                  src[0:RR, 4 * nu + u, :], start=False, stop=True, skip_group_check=True)
                last.then_inc(o_full, 1)

            def finish(q, p):
                key = ("fin", q, p)
                use = O_USE[q, p]
                bank = begin_t(key)
                pe.wait_ge(o_free, use + 1)
                for c in range(2):
                    part = oT[:, use % 2, 128 * c:128 * c + 128]
                    o = bank[:, 128 * c:128 * c + 128]
                    if layer(q) == 1:
                        mm(o, part, wo1, start=True, stop=False)
                        last = mm(o, ones[0:1, :], bo1, start=False, stop=True)
                    else:
                        last = nc.tensor.transpose(o, part, ident)
                end_t(last, key)

            def run_steps(q, events):
                for what, n in events:
                    if what == "scores":
                        scores(q, n)
                    elif what == "transpose":
                        turn_probs(q, n)
                    elif what == "expand":
                        expand(q, n)
                    elif what == "values":
                        values(q, n)
                    elif what == "finish":
                        finish(q, n)

            def tokens_major(key, lhs_of, rhs):
                bank = begin_t(key)
                w = rhs.shape[1]
                for tt in range(TILES):
                    last = mm(bank[:, w * tt:w * tt + w], lhs_of(tt), rhs, start=True, stop=True)
                end_t(last, key)

            def expert_unit(q, n):
                tt, part = n // 4, n % 4
                wait_s_free(pe, q, n)
                sl = slot(q, n)
                for g in range(2):
                    e = 8 * part + 4 * g
                    last = mm(sl[:, 2 * g:2 * g + 2, :].rearrange("p g c -> p (g c)"),
                              xnT[q % 2][:, 128 * tt:128 * tt + 128],
                              w_exp0[:, e:e + 4, :].rearrange("p e d -> p (e d)"), start=True, stop=True)
                last.then_inc(s_full[S_USE[q, n][0]], 1)

            def lowrank_unit(q, n):
                wait_s_free(pe, q, n)
                sl = slot(q, n)
                for g in range(2):
                    c = 2 * n + g
                    last = mm(sl[:, 2 * g:2 * g + 2, :].rearrange("p g c -> p (g c)"), v1[:, 128 * c:128 * c + 128],
                              p1, start=True, stop=True)
                last.then_inc(s_full[S_USE[q, n][0]], 1)

            def moe3_unit(q, n):
                wait_s_free(pe, q, n)
                sl = slot(q, n)
                for g, w in enumerate((w1T, w3T)):
                    last = mm(sl[:, 2 * g:2 * g + 2, :].rearrange("p g c -> p (g c)"), w[:, n, :], xnT[q % 2][:, :],
                              start=True, stop=True)
                last.then_inc(s_full[S_USE[q, n][0]], 1)

            def gate_spread(q, n):
                key = ("gb", q, n)
                bank = begin_t(key)
                end_t(mm(bank[:, :], pair_sel[:, n - 1, :], gT, start=True, stop=True), key)

            def moe3_out(q, n):
                if n == 0:
                    wait_s_read(pe, q, 0)
                    pe.wait_ge(o_free, O_USE[q, 0])
                else:
                    wait_t_read(pe, ("gb", q, n))
                src = h3[:, 0, :] if n == 0 else hg[:, n % 2, :]
                last = mm(psO[:, :], w2T[:, n, :], src, start=n == 0, stop=n == F3N - 1)
                last.then_inc(o_full if n == F3N - 1 else y_done, 1)

            def project(q):
                b, k = q % 2, kind(q)
                pe.wait_ge(xnT_ready, q + 1)
                if k in ("attn", "attn2") and q >= 2:
                    key = ("q", q)
                    bank = begin_t(key)
                    w = {1: wq1, 2: wq2, 3: wq3}[layer(q)]
                    end_t(mm(bank[:, :], w, xnT[b][:, :], start=True, stop=True), key)
                elif k in ("moe0", "moe3"):
                    if q == 2:
                        pe.wait_ge(loaded["routerT"], 16)
                    if q == 14:
                        pe.wait_ge(loaded["gate3T"], 16)
                    tokens_major(("logits", q), lambda tt: xnT[b][:, 128 * tt:128 * tt + 128],
                                 (routerT if k == "moe0" else gate3T)[:, :])
                elif k == "lowrank":
                    if q == 6:
                        for n in ("u1", "v1", "u2", "v2b"):
                            pe.wait_ge(loaded[n], 16)
                    key = ("p1", q)
                    bank = begin_t(key)
                    end_t(mm(bank[0:32, :], u1[:, :], xnT[b][:, :], start=True, stop=True), key)

            def head(q):
                b, k = q % 2, kind(q)
                if k == "attn":
                    if layer(q) > 0:
                        wait_stacked(pe, q)
                    if layer(q) > 0 and b == 0:
                        wait_stacked(pe, ("k", layer(q)))
                    run_steps(q, head_steps(q))
                elif k == "moe0":
                    if q == 2:
                        pe.wait_ge(loaded["w_exp0"], 16)
                    expert_unit(q, 0)
                    expert_unit(q, 1)
                elif k == "moe3":
                    if q == 14:
                        for n in ("w1T", "w3T", "w2T", "b2_exp", "pair_sel"):
                            pe.wait_ge(loaded[n], 16)
                    moe3_unit(q, 0)
                    moe3_unit(q, 1)
                elif k == "lowrank":
                    wait_t_read(pe, ("p1", q))
                    lowrank_unit(q, 0)
                    lowrank_unit(q, 1)
                elif k == "attn2":
                    wait_t_read(pe, ("q", q))
                    wait_s_free(pe, q, 0)
                    for tt in range(TILES):
                        last = mm(slot(q, 0)[:, tt, 0:SK], qT[:, 128 * tt:128 * tt + 128], kT2[:, b, 0:SK],
                                  start=True, stop=True)
                    last.then_inc(s_full[S_USE[q, 0][0]], 1)

            def turn(q):
                key = ("ln", q)
                bank = begin_t(key)
                pe.wait_ge(xn_ready, q + 1)
                for tt in range(TILES):
                    last = nc.tensor.transpose(bank[:, 128 * tt:128 * tt + 128], xn[:, tt, :], ident)
                end_t(last, key)

            def rest(q, part):
                k = kind(q)
                if k == "attn":
                    run_steps(q, rest_steps(q, part))
                elif k == "moe0":
                    todo = PREP[3 * part:3 * part + 3] if q == 2 else []
                    if q == 2 and part == 0:
                        pe.wait_ge(loaded["sq"], 16)
                        pe.wait_ge(loaded["rows"], 16)
                    for n in rest_units(part):
                        expert_unit(q, n)
                        if todo:
                            prepare(todo.pop(0))
                elif k == "lowrank" and part == 0:
                    key = ("q1", q)
                    bank = begin_t(key)
                    for c in range(4):
                        pe.wait_ge(hidden_ready, (q - 6) * 4 + c + 1)
                        last = mm(bank[0:32, :], u2[:, c, :], hidden[:, c, :], start=c == 0, stop=c == 3)
                    end_t(last, key)
                elif k == "attn2" and part == 0:
                    pe.wait_ge(probs_ready, P_READY[q])
                    p = probs[:, P_USE[q, 0] % NP]
                    for key, keys in ((("main", q), slice(0, KM)), (("rem", q), slice(KM, SK))):
                        bank = begin_t(key)
                        for tt in range(TILES):
                            last = nc.tensor.transpose(bank[0:keys.stop - keys.start, 128 * tt:128 * tt + 128],
                                                       p[:, keys, tt], ident)
                        end_t(last, key)
                elif q == 10 and part == 2:
                    key = ("amax_t", q)
                    bank = begin_t(key)
                    pe.wait_ge(am_ready, 1)
                    end_t(nc.tensor.transpose(bank[0:2, 0:128], am[:, :], ident), key)
                    key = ("amax_b", q)
                    bank = begin_t(key)
                    pe.wait_ge(am_ready, 2)
                    end_t(mm(bank[:, 0:2], ones[0:2, :], am2[:, 2:4], start=True, stop=True), key)
                elif k == "moe3":
                    if part == 0:
                        moe3_out(q, 0)
                        key = ("gates", q)
                        bank = begin_t(key)
                        pe.wait_ge(gate_ready, q - 14 + 3)
                        for tt in range(TILES):
                            last = nc.tensor.transpose(bank[0:E3, 128 * tt:128 * tt + 128], gate[:, q % 2, tt, 0:E3],
                                                       ident)
                        end_t(last, key)
                        wait_t_read(pe, key)
                        mm(psO[:, :], b2_exp[:, :], gT, start=False, stop=False)
                        gate_spread(q, 1)
                    for n in moe3_units(part):
                        moe3_unit(q, n + 1)
                        gate_spread(q, n + 1)
                        moe3_out(q, n)

            def tail(q):
                b, k = q % 2, kind(q)
                if k == "attn":
                    run_steps(q, tail_steps(q))
                elif k == "lowrank":
                    wait_t_read(pe, ("q1", q))
                    tokens_major(("fin", q), lambda tt: q1[:, 128 * tt:128 * tt + 128], v2b[:, :])
                elif k == "attn2":
                    wait_t_read(pe, ("main", q))
                    wait_t_read(pe, ("rem", q))
                    key = ("fin", q)
                    bank = begin_t(key)
                    for tt in range(TILES):
                        tok = slice(128 * tt, 128 * tt + 128)
                        mm(bank[:, tok], pT[:, 0, 0:2, :].rearrange("p a c -> p (a c)")[:, tok], v2m[:, b, :],
                           start=True, stop=False)
                        last = mm(bank[:, tok], pT[0:KR, 1, 0:2, :].rearrange("p a c -> p (a c)")[:, tok],
                                  v2r[:, b, :], start=False, stop=True)
                    end_t(last, key)
                elif k == "fp8":
                    pe.wait_ge(quant_ready, b + 2)
                    tokens_major(("fin", q), lambda tt: x8[:, b, 128 * tt:128 * tt + 128], w8[:, :])
                elif k == "moe3":
                    moe3_out(q, F3N - 1)
                    key = ("fin", q)
                    bank = begin_t(key)
                    pe.wait_ge(o_free, O_USE[q, 0] + 1)
                    for tt in range(TILES):
                        last = nc.tensor.transpose(bank[:, 128 * tt:128 * tt + 128], oT3[:, 128 * tt:128 * tt + 128],
                                                   ident)
                    end_t(last, key)

            prepare0()
            walk(head, tail, lambda q: None, turn, project, rest)

        @block.vector
        def _(dve):
            v = nc.vector
            chain = [0]

            def tick(ins):
                chain[0] += 1
                ins.then_inc(dve_done, 1)

            def settle():
                dve.wait_ge(dve_done, chain[0])

            def link(ins):
                tick(ins)
                settle()

            def copy(dst, src):
                return v.tensor_copy(dst, src)

            def free_t(ins, key):
                ins.then_inc(t_free[T_USE[key][0]], 1)

            def constants():
                for n in ("const", "cols", "wide", "masks1", "masks3"):
                    dve.wait_ge(loaded[n], 16)
                tick(v.tensor_tensor(coef[:, 0:1], betas[:, 0:1], betas[:, 1:2], ALU.add))
                tick(v.tensor_copy(mask1[:, :, :].rearrange("p b k -> p (b k)"), mask1_u8))
                tick(v.tensor_copy(mask3f, mask3_i32))
                settle()
                tick(v.tensor_tensor(coef[:, 1:2], coef[:, 0:1], betas[:, 2:3], ALU.subtract))
                tick(v.tensor_reduce(all_masked[:, :], mask1[:, :, :], AX.X, ALU.min))
                tick(v.tensor_scalar(mask_b[3][:, :], mask3f, 0.0, NEG, ALU.is_gt, ALU.mult))
                settle()
                link(v.tensor_scalar(all_masked[:, :], all_masked[:, :], -1.0, 1.0, ALU.mult, ALU.add))
                link(v.tensor_tensor(mask1[:, :, 0], mask1[:, :, 0], all_masked[:, :], ALU.mult))
                link(v.tensor_scalar(mask_b[1][:, :], mask1[:, :, :].rearrange("p b k -> p (b k)"), NEG, None,
                                     ALU.mult))
                dve.wait_ge(tanh_ready, 1)
                v.tensor_scalar(tg_bias[:, :], b_fp8, tg[:, X_SCALE[5]:X_SCALE[5] + 1], None,
                                ALU.mult).then_inc(consts_ready, 1)
                dve.wait_ge(consts_ready, 1)

            def prepare0():
                dve.wait_ge(loaded["ctxT"], 16)
                dve.wait_ge(zeroed, 1)
                v.tensor_copy(ctx_rem[:, :, :].rearrange("p b (k g) -> p b k g", g=4),
                              ctxT[:, :, KM:SK].unsqueeze(3).broadcast_to([128, B, KR, 4]))
                for h in range(8):
                    key = ("v0", h)
                    wait_t_full(dve, key)
                    src = t_bank(key)[:, 0:B * KP].rearrange("p (b k) -> p b k", b=B)
                    v.tensor_copy(vT0[:, h, :, 0:KM], src[:, :, 0:KM])
                    free_t(v.tensor_copy(vT0_rem[:, h, :, :].rearrange("p b (k g) -> p b k g", g=4)[:, :, :, h % 4],
                                         src[:, :, KM:SK]), key)
                for h in range(0, 8, 2):
                    key = ("a0", h)
                    wait_t_full(dve, key)
                    free_t(v.tensor_scalar(a0[:, h, :, :], t_bank(key)[:, 0:B * KP].rearrange("p (b k) -> p b k", b=B),
                                           64.0 ** -0.5, None, ALU.mult), key)
                for b in range(B):
                    key = ("vo", b, 0)
                    wait_t_full(dve, key)
                    free_t(v.tensor_copy(vo_main[:, b, 0:4, :].rearrange("p h d -> p (h d)"), t_bank(key)[:, :]), key)

            def stats_of(q):
                b = q % 2
                if q < 2:
                    dve.wait_ge(loaded["x"], 16)
                settle()
                xs = x[:, TILES * b:TILES * b + TILES, :]
                for tt in range(TILES):
                    tick(v.bn_stats(stats[:, tt, :], xs[:, tt, :]))
                settle()
                for tt in range(TILES):
                    tick(v.bn_aggr(meanvar[:, tt, :], stats[:, tt, :]))
                settle()
                v.tensor_scalar(vareps[:, :], meanvar[:, :, 1], 1e-5, None, ALU.add).then_inc(eps_added, 1)
                dve.wait_ge(rstd_ready, q + 1)
                if q > 0:
                    wait_t_full(dve, ("ln", q - 1))
                for tt in range(TILES):
                    last = v.tensor_scalar(xn[:, tt, :], xs[:, tt, :], meanvar[:, tt, 0:1], rstd[:, tt:tt + 1],
                                           ALU.subtract, ALU.mult)
                last.then_inc(xn_ready, 1)

            def add_to_x(q, key, tiles, width):
                wait_t_full(dve, key)
                s = q // 2
                xs = x[:, tiles.start:tiles.stop, :].rearrange("p t d -> p (t d)")
                v.scalar_tensor_tensor(xs, t_bank(key)[:, 0:width], tg[:, X_SCALE[s]:X_SCALE[s] + 1], xs,
                                       ALU.mult, ALU.add).then_inc(t_free[T_USE[key][0]], 1)
                wait_t_read(dve, key)

            def maxima(q, n):
                b = q % 2
                ring = P_USE[q, n] % NP
                wait_s_full(dve, q, n)
                src = slot(q, n)[:, :, 0:SK]
                if layer(q) == 1:
                    tt, u = tile_of(q, n)
                    if u == 0:
                        dve.wait_ge(bias_loaded[TILES * b + tt], 16)
                    use = BIAS_USE[q, n]
                    if use >= 2:
                        dve.wait_ge(bias_exp_done, use - 1)
                    part = bias1[:, (TILES * b + tt) % BR, 4 * u:4 * u + 4, :]
                    v.tensor_tensor(scores_sb[:, use % 2, :, :], src, part, ALU.add).then_inc(
                        s_free[S_USE[q, n][0]], 1)
                    src = scores_sb[:, use % 2, :, :]
                    wait_s_read(dve, q, n)
                v.tensor_reduce(negmax[:, ring, :], src, AX.X, ALU.max, negate=True).then_inc(max_ready, 1)

            def reciprocals(q, n):
                ring = P_USE[q, n] % NP
                wait_exp_done(dve, q, n)
                v.reciprocal(rsums[:, ring, :], sums[:, ring, :]).then_inc(rsum_ready, 1)

            def pair_reciprocals(q, p):
                nu = UNITS[q // 2] // TILES
                wait_exp_done(dve, q, (p + 1) * 2 * nu - 1)
                use = O_USE[q, p]
                v.reciprocal(pair_rsums[:, use % 2], pair_sums[:, use % 2]).then_inc(sums_ready, 1)

            def scale_values(q, p):
                use = O_USE[q, p]
                dve.wait_ge(o_full, use + 1)
                dve.wait_ge(rexp_ready, PAIR_USE[q, p] + 1)
                v.tensor_tensor(oT[:, use % 2, :], psO[:, 0:256], rexp[:, use % 2, :], ALU.mult).then_inc(o_free, 1)

            def run_steps(q, events):
                for what, n in events:
                    if what == "scores":
                        maxima(q, n)
                    elif what == "normalise":
                        reciprocals(q, n)
                    elif what == "sums":
                        pair_reciprocals(q, n)
                    elif what == "values" and layer(q) > 0:
                        scale_values(q, n)
                    elif what == "transpose":
                        copy_turned(nc.vector, copy, q, n)
                    elif what == "finish":
                        t0 = TILES * (q % 2) + 2 * n
                        add_to_x(q, ("fin", q, n), range(t0, t0 + 2), 256)

            def gating(q):
                first = kind(q) == "moe0"
                ne = E0 if first else E3
                io = (iota32 if first else iota16).rearrange("p (t e) -> p t e", t=TILES)
                key = ("logits", q)
                wait_t_full(dve, key)
                bank = t_bank(key)[:, 0:TILES * ne].rearrange("p (t e) -> p t e", t=TILES)
                l, sel, e = lg[:, :, 0:ne], lsel[:, :, 0:ne], ex[:, :, 0:ne]
                free_t(v.tensor_copy(l, bank), key)
                wait_t_read(dve, key)
                if not first:
                    v.tensor_copy(sel, l).then_inc(exp_in, 1)
                    dve.wait_ge(exp_in, EXP_IN[q])
                    link(v.tensor_tensor(sel, l, ebias.unsqueeze(1).broadcast_to([128, TILES, ne]), ALU.add))
                    l = sel
                for tt in range(TILES):
                    tick(v.max(top8[:, tt, :], l[:, tt, :]))
                settle()
                for tt in range(TILES):
                    tick(v.max_index(idx8[:, tt, :], top8[:, tt, :], l[:, tt, :]))
                if first:
                    v.tensor_tensor(sel, l, top8[:, :, 0:1].broadcast_to([128, TILES, ne]),
                                    ALU.subtract).then_inc(exp_in, 1)
                settle()
                link(v.tensor_copy(idxf[:, :, :], idx8[:, :, 0:2]))
                for i in range(2):
                    tick(v.tensor_tensor(hit[:, i, :, 0:ne], io, idxf[:, :, i:i + 1].broadcast_to([128, TILES, ne]),
                                         ALU.is_equal))
                settle()
                link(v.tensor_tensor(hit[:, 0, :, 0:ne], hit[:, 0, :, 0:ne], hit[:, 1, :, 0:ne], ALU.add))
                dve.wait_ge(exp_out, EXP_OUT[q])
                g = gate[:, q % 2, :, 0:ne]
                if first:
                    link(v.tensor_reduce(gsum[:, 0, :], e, AX.X, ALU.add))
                else:
                    link(v.tensor_scalar(e, e, 1.0, None, ALU.add))
                    link(v.reciprocal(e, e))
                link(v.tensor_tensor(e, e, hit[:, 0, :, 0:ne], ALU.mult))
                if not first:
                    link(v.tensor_reduce(gsum[:, 0, :], e, AX.X, ALU.add))
                    link(v.tensor_scalar(gsum[:, 0, :], gsum[:, 0, :], 1e-10, None, ALU.add))
                link(v.reciprocal(gsum[:, 1, :], gsum[:, 0, :]))
                v.tensor_tensor(g, e, gsum[:, 1, :].unsqueeze(2).broadcast_to([128, TILES, ne]),
                                ALU.mult).then_inc(gate_ready, 1)
                dve.wait_ge(gate_ready, {2: 1, 3: 2, 14: 3, 15: 4}[q])

            def weigh(q, n):
                tt, part = n // 4, n % 4
                tile = TILES * (q % 2) + tt
                wait_s_full(dve, q, n)
                w = gate[:, q % 2, tt, 8 * part:8 * part + 8].rearrange("p (g e) -> p g e", g=4)
                src = slot(q, n).rearrange("p g (e d) -> p g e d", e=2)
                w = w.unsqueeze(3).broadcast_to([128, 4, 2, 128])
                if part == 0:
                    if tile >= 2:
                        dve.wait_ge(acc_read, tile - 1)
                    dst, done = acc0[:, tile % 2, :], s_free[S_USE[q, n][0]]
                else:
                    m = 3 * tile + part - 1
                    if m >= 2:
                        dve.wait_ge(acc_added, m - 1)
                    dst, done = mult0[:, m % 2, :], s_free[S_USE[q, n][0]]
                v.tensor_tensor(dst.rearrange("p (g e d) -> p g e d", g=4, e=2), src, w, ALU.mult).then_inc(done, 1)

            def sum_experts(q, tt):
                tile = TILES * (q % 2) + tt
                dve.wait_ge(acc_added, 3 * tile + 3)
                settle()
                v.tensor_reduce(red0[:, :], acc0[:, tile % 2, :].rearrange("p (e d) -> p d e", e=8), AX.X,
                                ALU.add).then_inc(acc_read, 1)
                dve.wait_ge(acc_read, tile + 1)
                s = X_SCALE[q // 2]
                tick(v.scalar_tensor_tensor(x[:, tile, :], red0[:, :], tg[:, s:s + 1], x[:, tile, :],
                                            ALU.mult, ALU.add))

            def quantise(src, scale, tmp, dst, sig):
                link(v.tensor_scalar(tmp[0], src, scale, None, ALU.mult))
                link(v.tensor_scalar(tmp[1].bitcast(U32), tmp[0].bitcast(U32), 0x7F800000, None, ALU.bitwise_and))
                link(v.tensor_scalar(tmp[1], tmp[1], 2.0 ** -6, 1.5 * 2.0 ** 20, ALU.max, ALU.mult))
                link(v.tensor_tensor(tmp[0], tmp[0], tmp[1], ALU.add))
                v.tensor_tensor(dst, tmp[0], tmp[1], ALU.subtract).then_inc(sig, 1)

            def project(q):
                k = kind(q)
                if k in ("attn", "attn2") and q >= 2:
                    key = ("q", q)
                    wait_t_full(dve, key)
                    if q in (5, 13):
                        dve.wait_ge(split, STACKS[q])
                    bias, dim = {1: (bq1, 8.0), 2: (bq2, 128.0), 3: (bq3, 8.0)}[layer(q)]
                    free_t(v.tensor_scalar(qT[:, :], t_bank(key)[:, :], bias, dim ** -0.5, ALU.add, ALU.mult), key)
                elif k in ("moe0", "moe3"):
                    gating(q)

            def head(q):
                b, k = q % 2, kind(q)
                if k == "attn":
                    run_steps(q, head_steps(q))
                elif k == "moe0":
                    weigh(q, 0)
                    weigh(q, 1)
                elif k == "attn2":
                    wait_s_full(dve, q, 0)
                    if q == 8:
                        dve.wait_ge(loaded["phi"], 16)
                    sc = scores_sb[:, q % 2, :, :]
                    v.scalar_tensor_tensor(sc, phi[:, TILES * b:TILES * b + TILES, :], coef[:, 1:2],
                                           slot(q, 0)[:, :, 0:SK], ALU.mult, ALU.add).then_inc(
                        s_free[S_USE[q, 0][0]], 1)
                    wait_s_read(dve, q, 0)
                    v.tensor_reduce(negmax[:, P_USE[q, 0] % NP, :], sc, AX.X, ALU.max,
                                    negate=True).then_inc(max_ready, 1)
                    reciprocals(q, 0)

            def moe3_hidden(q, n):
                use = (q - 14) * F3N + n
                wait_s_full(dve, q, n)
                dve.wait_ge(silu_ready, use + 1)
                b3 = sb3 if n == 0 else eb3[:, n - 1:n]
                dst = h3[:, 0 if n == 0 else 1, :]
                if n == 0 and q == 15:
                    dve.wait_ge(y_done, F3N - 1)
                if n >= 2:
                    wait_t_read(dve, ("gb", q, n - 1))
                v.scalar_tensor_tensor(dst.rearrange("p (g c) -> p g c", g=2), slot(q, n)[:, 2:4, :], b3,
                                       a1[:, use % 2, :].rearrange("p (g c) -> p g c", g=2),
                                       ALU.add, ALU.mult).then_inc(s_free[S_USE[q, n][0]], 1)
                if n == 0:
                    return
                wait_s_read(dve, q, n)
                key = ("gb", q, n)
                wait_t_full(dve, key)
                if n >= 3:
                    dve.wait_ge(y_done, (q - 14) * (F3N - 1) + n - 1)
                elif n == 2 and q == 15:
                    dve.wait_ge(o_full, O_USE[14, 0] + 1)
                free_t(v.tensor_tensor(hg[:, n % 2, :], dst, t_bank(key)[:, :], ALU.mult), key)

            def rest(q, part):
                b, k = q % 2, kind(q)
                if k == "attn":
                    run_steps(q, rest_steps(q, part))
                elif k == "moe0":
                    for n in rest_units(part):
                        weigh(q, n)
                        if n % 4 == 2 and n > 4:
                            sum_experts(q, n // 4 - 1)
                elif k == "attn2" and part == 0:
                    key = ("main", q)
                    wait_t_full(dve, key)
                    free_t(v.tensor_copy(pT[:, 0, 0:2, :].rearrange("p a c -> p (a c)"), t_bank(key)[:, :]), key)
                elif q == 10 and part == 2:
                    dve.wait_ge(xnT_ready, 12)
                    for i in range(B):
                        tick(v.tensor_reduce(fsc[:, i:i + 1], xnT[i][:, :], AX.X, ALU.max, apply_absolute_value=True))
                    tick(v.tensor_reduce(am[:, 1:2], w_fp8, AX.X, ALU.max, apply_absolute_value=True))
                    settle()
                    v.tensor_tensor(am[:, 0:1], fsc[:, 0:1], fsc[:, 1:2], ALU.max).then_inc(am_ready, 1)
                    key = ("amax_t", q)
                    wait_t_full(dve, key)
                    free_t(v.tensor_reduce(am2[:, 0:1], t_bank(key)[0:2, 0:128], AX.X, ALU.max), key)
                    wait_t_read(dve, key)
                    v.tensor_scalar(am2[:, 2:4], ident[0:2, 0:2], am2[:, 0:1], None, ALU.mult).then_inc(am_ready, 1)
                    key = ("amax_b", q)
                    wait_t_full(dve, key)
                    free_t(v.tensor_scalar(fsc[:, 2:4], t_bank(key)[:, 0:2], 1e-12, None, ALU.max), key)
                    wait_t_read(dve, key)
                    link(v.reciprocal(fsc[:, 2:4], fsc[:, 2:4]))
                    link(v.tensor_scalar(fsc[:, 4:6], fsc[:, 2:4], 448.0, None, ALU.mult))
                    link(v.tensor_tensor(fsc[:, 6:7], fsc[:, 4:5], fsc[:, 5:6], ALU.mult))
                    link(v.reciprocal(fsc[:, 7:8], fsc[:, 6:7]))
                    s = X_SCALE[5]
                    link(v.tensor_tensor(fsc[:, 6:7], fsc[:, 7:8], tg[:, s:s + 1], ALU.mult))
                    quantise(w_fp8, fsc[:, 5:6], (fq[:, 0, 0:128], fq[:, 1, 0:128]), w8[:, :], quant_ready)
                    dve.wait_ge(quant_ready, 1)
                    for i in range(B):
                        quantise(xnT[i][:, :], fsc[:, 4:5], (fq[:, 0, :], fq[:, 1, :]), x8[:, i, :], quant_ready)
                        dve.wait_ge(quant_ready, i + 2)
                elif k == "moe3":
                    for n in (0, *moe3_units(0)) if part == 0 else moe3_units(part):
                        moe3_hidden(q, n)

            def tail(q):
                b, k = q % 2, kind(q)
                half = range(TILES * b, TILES * b + TILES)
                if k == "attn":
                    run_steps(q, tail_steps(q))
                elif k == "moe0":
                    sum_experts(q, TILES - 1)
                elif k == "fp8":
                    key = ("fin", q)
                    wait_t_full(dve, key)
                    xs = x[:, half.start:half.stop, :]
                    free_t(v.scalar_tensor_tensor(xs.rearrange("p t d -> p (t d)"), t_bank(key)[:, :], fsc[:, 6:7],
                                                  xs.rearrange("p t d -> p (t d)"), ALU.mult, ALU.add), key)
                    wait_t_read(dve, key)
                    link(v.tensor_tensor(xs, xs, tg_bias[:, :].unsqueeze(1).broadcast_to([128, TILES, D]), ALU.add))
                elif k == "moe3":
                    moe3_hidden(q, F3N - 1)
                    key = ("fin", q)
                    wait_t_full(dve, key)
                    s = X_SCALE[7]
                    xs = x[:, half.start:half.stop, :].rearrange("p t d -> p (t d)")
                    v.scalar_tensor_tensor(xs, t_bank(key)[:, :], tg[:, s:s + 1], xs, ALU.mult,
                                           ALU.add).then_inc(x_final, 1)
                    if b == 0:
                        dve.wait_ge(x_final, 1)
                        free_t(v.memset(am2[0:1, 0:1], 0.0), key)
                else:
                    add_to_x(q, ("fin", q), half, 512)

            prepare0()
            constants()
            walk(head, tail, stats_of, lambda q: None, project, rest)

        @block.scalar
        def _(act):
            a = nc.scalar.activation

            def copy(dst, src):
                return a(dst, src, ACT.Copy)

            def free_t(ins, key):
                ins.then_inc(t_free[T_USE[key][0]], 1)

            def load(name, dst, src):
                act.dma_start(dst, src).then_inc(loaded[name], 16)

            load("x", x[:, :, :], t["x"].rearrange("(t p) d -> p t d", p=128))
            load("wide", wide[:, :], t["wide"].broadcast_to([128, 155]))
            load("cols", cols[:, :], t["cols"])
            load("masks1", mask1_u8, t["mask1"].broadcast_to([128, B * SK]))
            load("masks3", mask3_i32, t["mask3"].broadcast_to([128, B * SK]))
            load("rows", rows[:, :], t["rows"])
            act.wait_ge(loaded["wide"], 16)
            a(tg[:, :], gates_in, ACT.Tanh).then_inc(tanh_ready, 1)

            def prepare0():
                for h in range(8):
                    key = ("k0", h)
                    wait_t_full(act, key)
                    free_t(copy(kT0[:, h, :], t_bank(key)[:, 0:B * KP]), key)
                for h in range(1, 8, 2):
                    key = ("a0", h)
                    wait_t_full(act, key)
                    free_t(a(a0[:, h, :, :].rearrange("p b k -> p (b k)"), t_bank(key)[:, 0:B * KP], ACT.Copy,
                             scale=64.0 ** -0.5), key)
                for b in range(B):
                    key = ("vo", b, 1)
                    wait_t_full(act, key)
                    free_t(copy(vo_main[:, b, 4:8, :].rearrange("p h d -> p (h d)"), t_bank(key)[:, :]), key)
                for b in range(B):
                    key = ("vr", b)
                    wait_t_full(act, key)
                    free_t(copy(vo_rem[0:RR, b, :, :].rearrange("p u d -> p (u d)"), t_bank(key)[0:RR, 0:256]), key)

            def prepare(key):
                wait_t_full(act, key)
                bank, i = t_bank(key), key[1]
                if key[0] == "k":
                    if i == 2:
                        last = a(kT2[:, :, :].rearrange("p b k -> p (b k)"), bank[:, 0:B * KP], ACT.Identity, bias=bk2)
                    else:
                        if i == 3:
                            act.wait_ge(split, 1)
                        last = a(left[:, 0:B * SK].rearrange("p (b k) -> p b k", b=B),
                                 bank[:, 0:B * KP].rearrange("p (b k) -> p b k", b=B)[:, :, 0:SK],
                                 ACT.Identity, bias=bk1 if i == 1 else bk3)
                else:
                    b = key[2]
                    if i == 2:
                        copy(v2m[:, b, :], bank[:, 0:128])
                        last = copy(v2r[:, b, :], bank[0:KR, 128:256])
                    else:
                        copy(vm[i][:, b, :, :].rearrange("p g (u c) -> p g u c", u=4)[:, :, :, 0:8],
                             bank[:, 0:128].rearrange("p (g u d) -> p g u d", g=4, u=4))
                        for g in range(4):
                            last = a(vr[i][:, b, :].rearrange("p (u c) -> p u c", u=4)[:, :, 8 * g:8 * g + 8],
                                     bank[0:RR, 128:256].rearrange("p (u c) -> p u c", u=4)[:, :, 8 * g:8 * g + 8],
                                     ACT.Copy, scale=rmask[0:RR, g:g + 1])
                free_t(last, key)

            def turn(q):
                key = ("ln", q)
                wait_t_full(act, key)
                copy(xnT[q % 2][:, :], t_bank(key)[:, :]).then_inc(xnT_ready, 1)
                act.wait_ge(xnT_ready, q + 1)
                free_t(copy(spare[:, 0:1], t_bank(key)[:, 0:1]), key)

            def exps(q, n):
                ring = P_USE[q, n] % NP
                if P_USE[q, n] >= NP:
                    old = P_KEYS[P_USE[q, n] - NP]
                    wait_t_full(act, ("t", *old) if kind(old[0]) == "attn" else ("rem", old[0]))
                act.wait_ge(max_ready, P_USE[q, n] + 1)
                if layer(q) == 1:
                    src = scores_sb[:, BIAS_USE[q, n] % 2, :, :]
                elif kind(q) == "attn2":
                    src = scores_sb[:, q % 2, :, :]
                else:
                    src = slot(q, n)
                if kind(q) == "attn" and layer(q) > 0:
                    tt, u = tile_of(q, n)
                    totals = pair_sums[:, O_USE[q, tt // 2] % 2, tt % 2, 4 * u:4 * u + 4]
                else:
                    totals = sums[:, ring, :]
                for g in range(4):
                    last = a(probs[:, ring, :, g], src[:, g, 0:SK], ACT.Exp, bias=negmax[:, ring, g:g + 1],
                             accum_out=totals[:, g:g + 1])
                if layer(q) == 1:
                    last.then_inc(bias_exp_done, 1)
                elif kind(q) == "attn2":
                    last.then_inc(exp_out, 1)
                else:
                    last.then_inc(s_free[S_USE[q, n][0]], 1)

            def run_steps(q, events):
                for what, n in events:
                    if what == "scores":
                        exps(q, n)
                    elif what == "transpose":
                        copy_turned(nc.scalar, copy, q, n)
                    elif what == "expand":
                        key = ("rt", q, n)
                        wait_t_full(act, key)
                        free_t(copy(rT[:, :], t_bank(key)[0:16, 0:256]), key)
                        key = ("rx", q, n)
                        wait_t_full(act, key)
                        copy(rexp[:, O_USE[q, n] % 2, :], t_bank(key)[:, 0:256]).then_inc(rexp_ready, 1)
                        act.wait_ge(rexp_ready, PAIR_USE[q, n] + 1)
                        free_t(copy(spare[:, 3:4], t_bank(key)[:, 0:1]), key)
                    elif what == "values" and layer(q) == 0:
                        use = O_USE[q, n]
                        act.wait_ge(o_full, use + 1)
                        a(oT[:, use % 2, :], psO[:, 0:256], ACT.Identity, bias=bo0).then_inc(o_free, 1)

            def gate_exp(q):
                act.wait_ge(exp_in, EXP_IN[q])
                ne = E0 if q < 4 else E3
                a(ex[:, :, 0:ne], lsel[:, :, 0:ne] if q < 4 else lg[:, :, 0:ne], ACT.Exp,
                  scale=1.0 if q < 4 else -1.0).then_inc(exp_out, 1)

            def silu(q, n):
                use = (q - 14) * F3N + n
                wait_s_full(act, q, n)
                if use >= 2:
                    wait_s_read(act, q if n >= 2 else q - 1, n - 2 if n >= 2 else n - 2 + F3N)
                b1 = sb1 if n == 0 else eb1[:, n - 1:n]
                a(a1[:, use % 2, :].rearrange("p (g c) -> p g c", g=2), slot(q, n)[:, 0:2, :], ACT.Silu,
                  bias=b1).then_inc(silu_ready, 1)

            def project(q):
                if kind(q) in ("moe0", "moe3"):
                    gate_exp(q)
                elif kind(q) == "lowrank":
                    key = ("p1", q)
                    wait_t_full(act, key)
                    free_t(copy(p1, t_bank(key)[0:32, :]), key)

            def head(q):
                k = kind(q)
                if k == "attn":
                    run_steps(q, head_steps(q))
                elif k == "attn2":
                    exps(q, 0)
                elif q == 6:
                    a(q1[32:33, :], xnT[0][32:33, :], ACT.Identity, scale=0.0, bias=1.0)

            def tail(q):
                k = kind(q)
                if k == "attn":
                    run_steps(q, tail_steps(q))
                elif k == "moe3":
                    silu(q, F3N - 1)
                    act.wait_ge(o_full, O_USE[q, 0] + 1)
                    a(oT3, psO[:, :], ACT.Identity, bias=sb2).then_inc(o_free, 1)

            def rest(q, part):
                k = kind(q)
                if k == "attn":
                    run_steps(q, rest_steps(q, part))
                elif q == 2:
                    if part == 0:
                        act.wait_ge(consts_ready, 1)
                        act.wait_ge(zeroed, 2)
                    for key in PREP[3 * part:3 * part + 3]:
                        prepare(key)
                elif k == "lowrank" and part == 0:
                    for n in range(2):
                        wait_s_full(act, q, n)
                        for c in range(2):
                            ins = a(hidden[:, 2 * n + c, :].rearrange("p (g c) -> p g c", g=2),
                                    slot(q, n)[:, 2 * c:2 * c + 2, :], ACT.Gelu_apprx_tanh,
                                    bias=fb1[:, 2 * n + c:2 * n + c + 1])
                            ins.then_inc(hidden_ready, 1)
                        act.wait_ge(hidden_ready, (q - 6) * 4 + 2 * n + 2)
                        copy(spare[:, 2:3], slot(q, n)[:, 0, 0:1]).then_inc(s_free[S_USE[q, n][0]], 1)
                    key = ("q1", q)
                    wait_t_full(act, key)
                    free_t(copy(q1[0:32, :], t_bank(key)[0:32, :]), key)
                elif k == "attn2" and part == 0:
                    key = ("rem", q)
                    wait_t_full(act, key)
                    free_t(copy(pT[0:KR, 1, 0:2, :].rearrange("p a c -> p (a c)"), t_bank(key)[0:KR, :]), key)
                elif k == "moe3":
                    if part == 0:
                        silu(q, 0)
                        key = ("gates", q)
                        wait_t_full(act, key)
                        free_t(copy(gT, t_bank(key)[0:E3, :]), key)
                    for n in moe3_units(part):
                        silu(q, n)

            prepare0()
            walk(head, tail, lambda q: None, turn, project, rest)

        @block.gpsimd
        def _(pool):
            g = nc.gpsimd
            g.memset(expo[:, :], -0.5)
            g.memset(vT0_rem, 0.0).then_inc(zeroed, 1)
            g.memset(ks[1][:, :, :, :], 0.0)

            chain = [0]

            def link(ins):
                chain[0] += 1
                ins.then_inc(pool_done, 1)
                pool.wait_ge(pool_done, chain[0])

            def split_parts(src, n, key):
                rem = left[:, 0:n]
                if STACKS[key] > 0:
                    pool.wait_ge(parts_saved, 16 * STACKS[key])
                link(g.tensor_copy(parts[:, 0, 0:n], src))
                for i in range(1, 3):
                    link(g.tensor_tensor(rem, src if i == 1 else rem, parts[:, i - 1, 0:n], ALU.subtract))
                    ins = g.tensor_copy(parts[:, i, 0:n], rem)
                    if i == 1:
                        link(ins)
                ins.then_inc(split, 1)

            def normalise(q, n):
                i = P_USE[q, n]
                pool.wait_ge(rsum_ready, P_READY.get(q, i + 1))
                p = probs[:, i % NP, :, :]
                g.tensor_tensor(p, p, rsums[:, i % NP, :].unsqueeze(1).broadcast_to([128, SK, 4]),
                                ALU.mult).then_inc(probs_ready, 1)

            def run_steps(q, events):
                for what, n in events:
                    if what == "normalise":
                        normalise(q, n)

            def stats_of(q):
                pool.wait_ge(eps_added, q + 1)
                g.tensor_tensor(rstd[:, :], vareps[:, :], expo[:, :], ALU.pow).then_inc(rstd_ready, 1)

            def add_quarters(q, first, last):
                for n in range(first, last):
                    tt, part = n // 4, n % 4
                    tile = TILES * (q % 2) + tt
                    if part == 0:
                        continue
                    m = 3 * tile + part - 1
                    wait_s_read(pool, q, 4 * tt)
                    wait_s_read(pool, q, n)
                    if m > 0:
                        pool.wait_ge(acc_added, m)
                    g.tensor_tensor(acc0[:, tile % 2, :], acc0[:, tile % 2, :], mult0[:, m % 2, :],
                                    ALU.add).then_inc(acc_added, 1)

            def head(q):
                k = kind(q)
                if k == "attn":
                    run_steps(q, head_steps(q))
                elif k == "attn2":
                    normalise(q, 0)
                elif k == "moe0":
                    add_quarters(q, 0, 2)

            def tail(q):
                if kind(q) == "attn":
                    run_steps(q, tail_steps(q))
                elif q == 3:
                    pool.wait_ge(acc_read, 2 * TILES)
                    g.memset(qs[1][96:128, :, :], 1.0).then_inc(ones_set, 1)
                    pool.wait_ge(ones_set, 2)

            def project(q):
                if q in STACKS:
                    wait_t_read(pool, ("q", q))
                    split_parts(qT[:, :], HT, q)

            def rest(q, part):
                if kind(q) == "attn":
                    run_steps(q, rest_steps(q, part))
                elif kind(q) == "moe0":
                    if q == 2 and part == 0:
                        pool.wait_ge(o_full, O_USE[1, 1] + 1)
                        g.memset(vm[1][:, :, :, :], 0.0)
                        g.memset(ks[3][:, :, :, :], 0.0)
                        g.memset(vm[3][:, :, :, :], 0.0).then_inc(zeroed, 1)
                    units = rest_units(part)
                    add_quarters(q, units.start, units.stop)
                    if q == 2 and part < 2:
                        i = 2 * part + 1
                        wait_t_read(pool, ("k", i))
                        split_parts(left[:, 0:B * SK], B * SK, ("k", i))
                    if q == 3 and part == 2:
                        pool.wait_ge(acc_added, 24)
                        g.memset(qs[0][96:128, :, :], 1.0).then_inc(ones_set, 1)
                        pool.wait_ge(ones_set, 1)

            walk(head, tail, stats_of, lambda q: None, project, rest)


def kernel(**inputs):
    import numpy as np
    import concourse.bacc as bacc
    from concourse.bass_utils import run_bass_kernel_spmd

    i = {k: np.asarray(v) for k, v in inputs.items()}

    def heads(w):
        return w.reshape(128, 8, 128)

    ctx_pad = np.zeros((128, B, KP), np.float32)
    ctx_pad[:, :, :SK] = i["ctx_1024"].transpose(2, 0, 1)
    const = np.concatenate([
        np.eye(128), (np.arange(128)[:, None] % 32 // 8 == np.arange(4)[None, :]),
        np.tile(np.arange(E0), (128, TILES)), np.tile(np.arange(E3), (128, TILES)), np.ones((128, 128)),
        np.arange(128)[:, None] % 4 == np.arange(4)[None, :],
        np.arange(128)[:, None] == np.arange(128)[None, :] // 8],
        axis=1).astype(np.float32)
    pair_sel = (np.arange(E3)[:, None, None] == 2 * np.arange(E3 // 2)[None, :, None]
                + np.arange(128)[None, None, :] // 64).astype(np.float32)

    def hidden_major(w, shared):
        both = np.concatenate([shared[None], w.reshape(E3 // 2, 128, 128)])
        return both.transpose(2, 0, 1)

    arrays = {
        "const": const, "pair_sel": pair_sel, "ctxT": ctx_pad,
        "x": i["x"].reshape(B * S, D),
        "wk0": heads(i["L0_xattn_Wk"]), "wv0": heads(i["L0_xattn_Wv"]),
        "wq0T": heads(i["L0_xattn_Wq"]).transpose(2, 1, 0),
        "wo0": i["L0_xattn_Wo"].reshape(8, 128, D).transpose(1, 0, 2),
        "routerT": i["L0_ffn_router_w"].T, "w_exp0": i["L0_ffn_expert_weights"].transpose(1, 0, 2),
        "sq": np.stack([i["L1_xattn_Wq"], i["L1_xattn_Wk"], i["L1_xattn_Wv"], i["L1_xattn_Wo"],
                        i["L2_xattn_Wq"].T, i["L2_xattn_Wk"].T, i["L2_xattn_Wv"].T, i["L2_ffn_weight"].T,
                        i["L3_xattn_q_w"].T, i["L3_xattn_k_w"].T, i["L3_xattn_v_w"].T], axis=1),
        "fside4": i["fside_Bx16xSxS2_0"], "phi": i["fside_BxSxS2_0"].reshape(B * S, SK),
        "mask1": i["mask_BxS2_bk0"].reshape(1, B * SK),
        "mask3": i["mask_BxS2_ik0"].reshape(1, B * SK),
        "cols": np.concatenate([
            np.stack([i[n] for n in ("L0_xattn_bo", "L1_xattn_bq", "L1_xattn_bk", "L2_xattn_bq", "L2_xattn_bk",
                                     "L3_xattn_q_b", "L3_xattn_k_b", "L3_ffn_sb1", "L3_ffn_sb3", "L3_ffn_sb2")],
                     axis=1),
            i["L1_ffn_b1"].reshape(4, 128).T, i["L3_ffn_b1"].reshape(8, 128).T, i["L3_ffn_b3"].reshape(8, 128).T],
            axis=1),
        "rows": np.concatenate([i[n] for n in ("L1_xattn_bv", "L1_xattn_bo", "L2_xattn_bv", "L3_xattn_v_b")])[None],
        "wide": np.concatenate([i["L2_ffn_bias"], i["L3_ffn_expert_bias"], i["g_xattn"], i["g_ffn"],
                                i["L2_xattn_beta_risk"].reshape(1), i["L2_xattn_beta_prio"].reshape(1),
                                i["L2_xattn_beta_impl"].reshape(1)])[None],
        "u1": i["L1_ffn_U1"], "v1": i["L1_ffn_V1"],
        "u2": i["L1_ffn_U2"].reshape(4, 128, 32).transpose(1, 0, 2),
        "v2b": np.concatenate([i["L1_ffn_V2"], i["L1_ffn_b2"][None]]),
        "gate3T": i["L3_ffn_gate_w"].T,
        "w1T": hidden_major(i["L3_ffn_w1"], i["L3_ffn_sw1"]),
        "w3T": hidden_major(i["L3_ffn_w3"], i["L3_ffn_sw3"]),
        "w2T": np.concatenate([i["L3_ffn_sw2"].T[None],
                               i["L3_ffn_w2"].transpose(0, 2, 1).reshape(E3 // 2, 128, D)]).transpose(1, 0, 2),
        "b2_exp": i["L3_ffn_b2"],
    }
    arrays = {f"in_{k}": np.ascontiguousarray(v) for k, v in arrays.items()}
    nc = bacc.Bacc("TRN2", target_bir_lowering=False, num_devices=1)
    t = {k[3:]: nc.dram_tensor(k, v.shape, mybir.dt.from_np(v.dtype), kind="ExternalInput").ap()
         for k, v in arrays.items()}
    t["parts"] = nc.dram_tensor("parts_scratch", (128, 3, HT), BF16, kind="Internal").ap()
    out = nc.dram_tensor("out_x", (B, S, D), F32, kind="ExternalOutput").ap()
    build(nc, t, out)
    r = run_bass_kernel_spmd(nc, [arrays], core_ids=[0])
    return r.results[0]["out_x"]
```

```python
from contextlib import ExitStack

import concourse.bass as bass
from concourse import mybir

F32 = mybir.dt.float32
BF16 = mybir.dt.bfloat16
I32 = mybir.dt.int32
U32 = mybir.dt.uint32
U16 = mybir.dt.uint16
U8 = mybir.dt.uint8
ALU = mybir.AluOpType
ACT = mybir.ActivationFunctionType
AX = mybir.AxisListType

B, S, D, SK = 2, 512, 128, 154
KM, KR = 128, SK - 128
RR = 4 * KR
KP = 160
TILES = S // 128
HALVES = 16
HT = S
BR = 3
NP = 5
E0, E3 = 32, 16
F3N = 1 + E3 // 2
NB = 3
NEG = -1.0e30
KINDS = ["attn", "moe0", "attn", "lowrank", "attn2", "fp8", "attn", "moe3"]
UNITS = {0: 8, 2: 16, 6: 16}
LAGS = {0: (3, 5, 6, 8), 2: (3, 5, 8, 10), 6: (3, 5, 8, 10)}
PARTS = [(0, 0), (0, 1), (1, 0), (1, 1), (0, 2), (2, 0), (1, 2)]
CR = 16 * len(PARTS) + 1


def kind(q):
    return KINDS[q // 2]


def layer(q):
    return q // 4


def steps(s, first, last):
    n, (lag, v_first, v_last, end) = UNITS[s], LAGS[s]
    for k in range(first, last):
        if lag < k <= 2 * n + lag and k > first:
            yield "collect", *unit(s, k - lag - 1)
        ahead = s == 2
        if k == 0 and ahead:
            yield "feed", *unit(s, 0)
        if k + ahead < 2 * n:
            yield "feed", *unit(s, k + ahead)
        if k < 2 * n:
            yield "scores", *unit(s, k)
        if s == 0 and 2 <= k < 2 * n + 2:
            yield "normalise", *unit(s, k - 2)
        if lag <= k < 2 * n + lag:
            yield "transpose", *unit(s, k - lag)
        for pair in range(4):
            since = k - ((pair + 1) * n // 2 - 1)
            q, p = 2 * s + pair // 2, pair % 2
            if s > 0 and since == 2:
                yield "sums", q, p
            if s > 0 and since == 4:
                yield "turn sums", q, p
            if s > 0 and since == 6:
                yield "expand", q, p
            if v_first <= since <= v_last:
                yield "values", q, (p, since - v_first)
            if since == v_last:
                yield "evacuate", q, p
            if since == end:
                yield "finish", q, p
    if last > first and lag < last <= 2 * n + lag:
        yield "collect", *unit(s, last - lag - 1)


def unit(s, k):
    return 2 * s + k // UNITS[s], k % UNITS[s]


def tail_end(s):
    return UNITS[s] + LAGS[s][3]


def second_tail(s):
    return 21 if s == 0 else 2 * UNITS[s] + 2


def head_steps(q):
    k0 = q % 2 * UNITS[q // 2]
    return steps(q // 2, k0, k0 + 2)


def rest_steps(q, part):
    s, n = q // 2, UNITS[q // 2]
    if q % 2 == 0:
        cuts = (2, 4, 6, n) if s == 0 else (2, 5, 8, n)
    else:
        first = tail_end(s)
        cuts = (first, first + 2, first + 4, second_tail(s))
    return steps(s, cuts[part], cuts[part + 1])


def tail_steps(q):
    s, n = q // 2, UNITS[q // 2]
    return steps(s, n + 2, tail_end(s)) if q % 2 == 0 else steps(s, second_tail(s), n + tail_end(s))


def rest_units(part):
    return (range(2, 5), range(5, 8), range(8, 16))[part]


def walk(head, tail, stats, turn, project, rest):
    turn(0)
    project(0)
    for q in range(HALVES):
        head(q)
        if q > 0:
            tail(q - 1)
        for i, part in enumerate((stats, turn, project)):
            if q + 1 < HALVES:
                part(q + 1)
            rest(q, i)
    tail(HALVES - 1)


PREP = [("k", 1), ("v", 1, 0), ("v", 1, 1), ("k", 3), ("v", 3, 0), ("v", 3, 1), ("k", 2), ("v", 2, 0), ("v", 2, 1)]


def moe3_units(part):
    return (range(1, 3), range(3, 5), range(5, F3N - 1))[part]


def t_uses():
    keys = []
    for h in range(8):
        keys += [("k0", h), ("v0", h)]
    keys += [("a0", h) for h in range(8)]
    keys += [("vo", b, i) for b in range(B) for i in range(2)] + [("vr", b) for b in range(B)]

    def of_steps(events):
        for what, q, n in events:
            if what == "transpose":
                keys.append(("t", q, n))
            if what == "turn sums":
                keys.append(("rt", q, n))
            if what == "expand":
                keys.append(("rx", q, n))
            if what == "finish":
                keys.append(("fin", q, n))

    def head(q):
        if kind(q) == "attn":
            of_steps(head_steps(q))

    def tail(q):
        if kind(q) == "attn":
            of_steps(tail_steps(q))
        elif kind(q) != "moe0":
            keys.append(("fin", q))

    def turn(q):
        keys.append(("ln", q))

    def project(q):
        if kind(q) in ("attn", "attn2") and q >= 2:
            keys.append(("q", q))
        elif kind(q) in ("moe0", "moe3"):
            keys.append(("logits", q))
        elif kind(q) == "lowrank":
            keys.append(("p1", q))

    def rest(q, part):
        if kind(q) == "attn":
            of_steps(rest_steps(q, part))
        elif q == 2:
            keys.extend(PREP[3 * part:3 * part + 3])
        elif kind(q) == "lowrank" and part == 0:
            keys.append(("q1", q))
        elif kind(q) == "attn2" and part == 0:
            keys.extend([("main", q), ("rem", q)])
        elif q == 10 and part == 2:
            keys.extend([("amax_t", q), ("amax_b", q)])
        elif kind(q) == "moe3":
            if part == 0:
                keys.extend([("gates", q), ("gb", q, 1)])
            keys.extend([("gb", q, n + 1) for n in moe3_units(part)])

    walk(head, tail, lambda q: None, turn, project, rest)
    return keys


def s_uses():
    keys = []
    for q in range(HALVES):
        n = {"attn": UNITS.get(q // 2), "moe0": 16, "lowrank": 2, "attn2": 1, "fp8": 0, "moe3": F3N}[kind(q)]
        keys += [(q, i) for i in range(n)]
    return keys


def build(nc, t, out):
    T_USE = {key: (i % 2, i // 2) for i, key in enumerate(t_uses())}
    S_USE = {key: (i % 2, i // 2) for i, key in enumerate(s_uses())}
    P_KEYS = [(q, n) for q in range(HALVES) for n in range(UNITS[q // 2] if kind(q) == "attn" else
                                                           1 if kind(q) == "attn2" else 0)]
    P_USE = {key: i for i, key in enumerate(P_KEYS)}
    M_USE = {key: i for i, key in enumerate((q, tt) for q in range(HALVES) if kind(q) == "attn" for tt in range(TILES))}
    O_KEYS = [(q, p) for q in range(HALVES) if kind(q) == "attn" for p in range(2)] + [(q, 0) for q in (14, 15)]
    O_USE = {key: i for i, key in enumerate(O_KEYS)}
    PAIR_USE = {key: i for i, key in enumerate((q, p) for q in (4, 5, 12, 13) for p in range(2))}
    P_READY = {8: 17, 9: 18}
    BIAS_USE = {key: i for i, key in enumerate((q, n) for q in (4, 5) for n in range(16))}

    with ExitStack() as ctx:
        def sb(name, shape, dt=F32):
            return ctx.enter_context(nc.sbuf_tensor(name, shape, dt))

        def ps(name, cols):
            return ctx.enter_context(nc.psum_tensor(name, [128, cols], F32))

        def sem(name):
            return ctx.enter_context(nc.semaphore(name))

        const = sb("const", [128, 584])
        head_sel = const[0:16, 456:584]
        rmask = const[:, 452:456]
        ident, dmask, iota32, iota16, ones = (const[:, 0:128], const[:, 128:132], const[:, 132:260],
                                              const[:, 260:324], const[:, 324:452])
        x = sb("x", [128, 8, D])
        ctxT = sb("ctxT", [128, B, KP])
        ctx_all = ctxT[:, :, :].rearrange("p b k -> p (b k)")
        cols = sb("cols", [128, 30])
        (bo0, bq1, bk1, bq2, bk2, bq3, bk3, sb1, sb3, sb2) = (cols[:, i:i + 1] for i in range(10))
        fb1 = cols[:, 10:14]
        eb1, eb3 = cols[:, 14:22], cols[:, 22:30]
        rows = sb("rows", [1, 4 * 128])
        bv1, bo1, bv2, bv3 = (rows[0:1, 128 * i:128 * i + 128] for i in range(4))
        wide = sb("wide", [128, 155])
        b_fp8, ebias, gates_in, betas = wide[:, 0:128], wide[:, 128:144], wide[:, 144:152], wide[:, 152:155]
        mask_b = {i: sb(f"mask_b{i}", [128, B * SK], BF16) for i in (1, 3)}
        scores_sb = sb("scores_sb", [128, NB, 4, SK])
        masks = scores_sb[:, 0:2, :, :].rearrange("p i g k -> p (i g k)").rearrange("p (n k) -> p n k", n=4)
        mask3_i32, mask3f, mask1 = masks[:, 0, :].bitcast(I32), masks[:, 1, :], masks[:, 2, :].rearrange(
            "p (b k) -> p b k", b=B)
        mask1_u8 = masks[:, 3, 0:B * SK // 4].bitcast(U8)
        early = sb("early", [128, 4, 8, 128])
        wq0T, wk0, wv0, wo0 = (early[:, i] for i in range(4))
        routerT = sb("routerT", [128, E0])
        experts = sb("experts", [128, E0 * D])
        w_exp0 = experts[:, :].rearrange("p (e d) -> p e d", e=E0)
        w1T, w3T, w2T = (experts[:, 1152 * i:1152 * i + 1152].rearrange("p (n c) -> p n c", n=F3N) for i in range(3))
        gT = experts[0:3 * E3, 3456:3456 + HT]
        sq = sb("sq", [128, 11, D])
        wq1, wk1, wv1, wo1, wq2, wk2, wv2, w_fp8, wq3, wk3, wv3 = (sq[:, i, :] for i in range(11))
        u1 = sb("u1", [128, 32])
        v1 = sb("v1", [32, 512])
        u2 = sb("u2", [128, 4, 32])
        v2b = sb("v2b", [33, D])
        gate3T = sb("gate3T", [128, E3])
        b2_exp = sb("b2_exp", [3 * E3, D])
        bias1 = sb("bias1", [128, BR, 16, SK])
        phi = sb("phi", [128, 8, SK])
        phi_flat = phi[:, :, :].rearrange("p t k -> p (t k)")
        pair_sel = phi_flat[0:3 * E3, 0:E3 // 4 * 128].bitcast(BF16).rearrange("p (n c) -> p n c", n=E3 // 2)
        gT_b = phi_flat[0:3 * E3, 512:512 + HT // 2].bitcast(BF16)

        keyed = sb("keyed", [128, 4 * 8 * KP])
        a0 = keyed[:, 0:2560].rearrange("p (h b k) -> p h b k", h=8, b=B)
        vo_main = keyed[:, 2560:4608].rearrange("p (b h d) -> p b h d", b=B, h=8)
        vo_rem = keyed[:, 4608:5120].rearrange("p (b u d) -> p b u d", b=B, u=2)
        vm = {i: keyed[:, 640 * (i - 1):640 * (i - 1) + 1280].rearrange("p (b g c) -> p b g c", b=B, g=4)
              for i in (1, 3)}
        vr = {i: sb(f"vr{i}", [RR, B, 128]) for i in (1, 3)}
        ctx_rem = sb("ctx_rem", [128, B, RR])
        ks = {1: sb("ks1", [128, 8, 2, B * SK], BF16),
              3: keyed[:, 2560:2560 + 2464].bitcast(BF16).rearrange("p (a h k) -> p a h k", a=8, h=2)}
        kT2 = sb("kT2", [128, B, KP])
        v2m = sb("v2m", [128, B, D])
        v2r = sb("v2r", [KR, B, D])
        tg = sb("tg", [128, 8])
        tg_bias = sb("tg_bias", [128, D])
        coef = sb("coef", [128, 2])
        all_masked = sb("all_masked", [128, 2])
        expo = sb("expo", [128, 4])

        xnT = [sb(f"xnT{b}", [128, HT]) for b in range(B)]
        qT = sb("qT", [128, HT])
        parts = sb("parts", [128, 3, HT], BF16)
        left = sb("left", [128, HT])
        xn = sb("xn", [128, TILES, D])
        stats = sb("stats", [128, TILES, 6])
        meanvar = sb("meanvar", [128, TILES, 2])
        vareps = sb("vareps", [128, TILES])
        rstd = sb("rstd", [128, TILES])
        probs = sb("probs", [128, NP, SK, 4])
        negmax = sb("negmax", [128, NP, 4])
        sums = sb("sums", [128, NP, 4])
        pair_sums = sb("pair_sums", [128, 2, 2, 16])
        pair_rsums = sb("pair_rsums", [128, 2, 2, 16])
        rT = sb("rT", [16, 256])
        rexp = sb("rexp", [128, 2, 256])
        rsums = sb("rsums", [128, NP, 4])
        pT = sb("pT", [128, 2, 20, 256])
        oT = sb("oT", [128, 2, 256])
        spare = sb("spare", [128, 4])
        kT0 = pT[:, 0, 0:10, :].rearrange("p a c -> p (a c)").rearrange("p (h k) -> p h k", h=8)
        vT0 = pT[:, 0, 10:20, :].rearrange("p a c -> p (a c)").rearrange("p (h b k) -> p h b k", h=8, b=B)
        vT0_rem = pT[:, 1, 0:8, 0:B * RR].rearrange("p h (b c) -> p h b c", b=B)
        qs = [early[:, 2 * i:2 * i + 2].rearrange("p i h c -> p (i h c)").bitcast(BF16).rearrange(
            "p (a c) -> p a c", a=8) for i in range(2)]
        mult0, acc0 = (pT[:, i, 10:18, :].rearrange("p a c -> p (a c)").rearrange("p (i c) -> p i c", i=2)
                       for i in range(2))
        red0 = sb("red0", [128, D])
        lg = sb("lg", [128, TILES, 32])
        lsel = sb("lsel", [128, TILES, 32])
        ex = sb("ex", [128, TILES, 32])
        hit = sb("hit", [128, 2, TILES, 32])
        gate = sb("gate", [128, 2, TILES, 32])
        gate_parts = sb("gate_parts", [128, 2, TILES, 3 * E3])
        part_b = sb("part_b", [128, TILES, E3], BF16)
        top8 = sb("top8", [128, TILES, 8])
        idx8 = sb("idx8", [128, TILES, 8], U32)
        idxf = sb("idxf", [128, TILES, 2])
        gsum = sb("gsum", [128, 2, TILES])
        work = bias1[:, :, :, :].rearrange("p i h k -> p (i h k)")
        hidden = work[:, 0:2048].rearrange("p (n c) -> p n c", n=4)
        fq = work[:, 5120:6144].rearrange("p (n c) -> p n c", n=2)
        p1 = fq[0:32, 0, :]
        q1 = fq[0:33, 1, :]
        a1, h3, hg = (work[:, c:c + 1024].rearrange("p (n c) -> p n c", n=2) for c in (3072, 4096, 5120))
        oT3 = work[:, 6144:6656]
        x8 = work[:, 2048:2560].bitcast(BF16).rearrange("p (b c) -> p b c", b=B)
        am = sb("am", [128, 2])
        am2 = sb("am2", [2, 4])
        fsc = sb("fsc", [128, 8])
        w8 = sb("w8", [128, 128], BF16)

        psS = ps("psS", 2048)
        slot_view = psS[:, :].rearrange("p (s g c) -> p s g c", s=2, g=4)
        psT = [ps("psT0", 512), ps("psT1", 512)]
        psO = ps("psO", 512)
        psM = ps("psM", 512)

        LOADS = ["const", "ctxT", "x", "wk0_0", "wv0_0", "wk0_4", "wv0_4", "wq0T", "wo0", "cols", "wide", "rows", "routerT", "w_exp0",
                 "masks1", "masks3", "sq", "phi", "u1", "v1", "u2", "v2b", "pair_sel", "gate3T", "w1T", "w3T",
                 "w2T", "b2_exp"]
        loaded = {n: sem(f"loaded_{n}") for n in LOADS}
        bias_loaded = [sem(f"bias_loaded{i}") for i in range(8)]
        t_full, t_free = ([sem(f"t_{w}{i}") for i in range(2)] for w in ("full", "free"))
        s_full, s_free = ([sem(f"s_{w}{i}") for i in range(2)] for w in ("full", "free"))
        m_full, m_free, o_full, o_free = (sem(n) for n in ("m_full", "m_free", "o_full", "o_free"))
        dve_done = sem("dve_done")
        pool_done = sem("pool_done")
        zeroed = sem("zeroed")
        consts_ready = sem("consts_ready")
        tanh_ready = sem("tanh_ready")
        eps_added = sem("eps_added")
        rstd_ready = sem("rstd_ready")
        xn_ready = sem("xn_ready")
        xnT_ready = sem("xnT_ready")
        max_ready = sem("max_ready")
        bias_exp_done = sem("bias_exp_done")
        rsum_ready = sem("rsum_ready")
        probs_ready = sem("probs_ready")
        split = sem("split")
        q_stacked = [sem(f"q_stacked{i}") for i in range(4)]
        k_stacked = {i: sem(f"k_stacked{i}") for i in (1, 3)}
        exponent_set = sem("exponent_set")
        ones_set = sem("ones_set")
        parts_saved = [sem(f"parts_saved{i}") for i in range(3)]
        sums_ready = sem("sums_ready")
        rexp_ready = sem("rexp_ready")
        exp_in = sem("exp_in")
        exp_out = sem("exp_out")
        gate_ready = sem("gate_ready")
        acc_first = sem("acc_first")
        mult_ready = sem("mult_ready")
        acc_added = sem("acc_added")
        acc_read = sem("acc_read")
        hidden_ready = sem("hidden_ready")
        q1_ready = sem("q1_ready")
        silu_ready = sem("silu_ready")
        y_done = sem("y_done")
        am_ready = sem("am_ready")
        quant_ready = sem("quant_ready")
        x_final = sem("x_final")
        stored = sem("stored")

        def t_bank(key):
            return psT[T_USE[key][0]]

        def wait_t_free(eng, key):
            i, n = T_USE[key]
            if n > 0:
                eng.wait_ge(t_free[i], n)

        def wait_t_full(eng, key):
            i, n = T_USE[key]
            eng.wait_ge(t_full[i], n + 1)

        def wait_t_read(eng, key):
            i, n = T_USE[key]
            eng.wait_ge(t_free[i], n + 1)

        def slot(q, n):
            return slot_view[:, S_USE[q, n][0]]

        def wait_s_free(eng, q, n):
            i, k = S_USE[q, n]
            if k > 0:
                eng.wait_ge(s_free[i], k)

        def wait_s_full(eng, q, n):
            i, k = S_USE[q, n]
            eng.wait_ge(s_full[i], k + 1)

        def wait_s_read(eng, q, n):
            i, k = S_USE[q, n]
            eng.wait_ge(s_free[i], k + 1)

        def wait_exp_done(eng, q, n):
            if layer(q) == 1:
                eng.wait_ge(bias_exp_done, BIAS_USE[q, n] + 1)
            elif kind(q) == "attn2":
                eng.wait_ge(exp_out, EXP_OUT[q])
            else:
                wait_s_read(eng, q, n)

        EXP_IN = {2: 1, 3: 2, 14: 3, 15: 4}
        EXP_OUT = {2: 1, 3: 2, 8: 3, 9: 4, 14: 5, 15: 6}
        STACKS = {("k", 1): 0, ("k", 3): 1, 4: 2, 5: 3, 12: 4, 13: 5}
        Q_STACK = {4: 0, 5: 1, 12: 2, 13: 3}
        LAST_STACK = {("k", 3): ("k", 1), 4: ("k", 3), 5: 4, 12: 5, 13: 12}

        def wait_stacked(eng, key):
            if key in Q_STACK:
                eng.wait_ge(q_stacked[Q_STACK[key]], 16 * len(PARTS))
            else:
                eng.wait_ge(k_stacked[key[1]], 16 * (2 * len(PARTS) + 1))

        X_SCALE = {0: 0, 1: 4, 2: 1, 3: 5, 4: 2, 5: 6, 6: 3, 7: 7}

        def turned_by(q, n):
            if layer(q) == 3:
                return "scalar" if n % 4 == 0 else "vector"
            if layer(q) == 1:
                return "vector" if n % 4 == 3 else "scalar"
            return "scalar" if n % 2 == 0 else "vector"

        def rem_turned_by(q):
            return "vector" if layer(q) == 3 else "scalar"

        def tile_of(q, n):
            return n // (UNITS[q // 2] // TILES), n % (UNITS[q // 2] // TILES)

        def copy_turned(eng, copy, q, n):
            tt, u = tile_of(q, n)
            nu = UNITS[q // 2] // TILES
            p, cols_of = tt // 2, slice(tt % 2 * 128, tt % 2 * 128 + 128)
            me = "scalar" if eng is nc.scalar else "vector"
            use = O_USE[q, p]
            if turned_by(q, n) == me:
                if use >= 2:
                    eng.wait_ge(o_full, use - 1)
                wait_t_full(eng, ("t", q, n))
                copy(pT[:, use % 2, 4 * u:4 * u + 4, cols_of],
                     t_bank(("t", q, n))[:, :].rearrange("p (g c) -> p g c", g=4)).then_inc(
                    t_free[T_USE["t", q, n][0]], 1)
            if u == nu - 1 and rem_turned_by(q) == me:
                if use >= 2:
                    eng.wait_ge(o_full, use - 1)
                eng.wait_ge(m_full, M_USE[q, tt] + 1)
                copy(pT[0:RR, use % 2, 4 * nu:5 * nu, cols_of],
                     psM[0:RR, 0:128 * nu].rearrange("p (u c) -> p u c", u=nu)).then_inc(m_free, 1)

        block = ctx.enter_context(nc.Block())

        @block.sync
        def _(sp):
            def load(name, dst, src):
                sp.dma_start(dst, src).then_inc(loaded[name], 16)

            load("ctxT", ctxT[:, :, :], t["ctxT"])
            for h in range(0, 8, 4):
                load(f"wk0_{h}", wk0[:, h:h + 4, :], t["wk0"][:, h:h + 4, :])
                load(f"wv0_{h}", wv0[:, h:h + 4, :], t["wv0"][:, h:h + 4, :])
            load("const", const[:, :], t["const"])
            load("wq0T", wq0T[:, :, :], t["wq0T"])
            load("wo0", wo0[:, :, :], t["wo0"])
            load("routerT", routerT[:, :], t["routerT"])
            load("w_exp0", w_exp0[:, :, :], t["w_exp0"])
            load("sq", sq[:, :, :], t["sq"])

            def load_bias(i):
                b, tt = i // TILES, i % TILES
                src = t["fside4"][b, :, 128 * tt:128 * tt + 128, :].rearrange("h p k -> p h k")
                sp.dma_start(bias1[:, i % BR, :, :], src).then_inc(bias_loaded[i], 16)

            for i in range(BR):
                load_bias(i)
            load("phi", phi[:, :, :], t["phi"].rearrange("(t p) k -> p t k", p=128))
            for name, dst in (("u1", u1), ("v1", v1), ("u2", u2), ("v2b", v2b), ("gate3T", gate3T),
                              ("b2_exp", b2_exp)):
                load(name, dst[:], t[name])

            def stack(key, n, rows):
                signal = k_stacked[key[1]] if key in (("k", 1), ("k", 3)) else q_stacked[Q_STACK[key]]
                for part in range(3):
                    sp.wait_ge(split, 3 * STACKS[key] + part + 1)
                    if part == 0 and STACKS[key] > 0:
                        wait_stacked(sp, LAST_STACK[key])
                    sp.dma_start(t["parts"][:, part, 0:n], parts[:, part, 0:n]).then_inc(parts_saved[part], 16)
                    if part > 0:
                        read_parts(key, part - 1, rows, signal)
                read_parts(key, 2, rows, signal)

            def read_parts(key, part, rows, signal):
                sp.wait_ge(parts_saved[part], 16 * (STACKS[key] + 1))
                for dst, src in rows(part):
                    sp.dma_start(dst, src).then_inc(signal, 16)

            def stack_keys(i):
                src = t["parts"][:, :, 0:B * SK].rearrange("(a h d) n k -> h d a n k", h=2, d=8)
                stack(("k", i), B * SK, lambda part: [
                    (ks[i][16 * c + 8 * h:16 * c + 8 * h + 8, :, h, :], src[h, :, :, part, :])
                    for c, of in enumerate(PARTS) if of[1] == part for h in range(2)])
                sp.dma_start(ks[i][CR - 1:CR, :, :, :].rearrange("p a h k -> p (a h) k"),
                             mask_b[i][0:1, :].unsqueeze(1).broadcast_to([1, 16, B * SK])).then_inc(k_stacked[i], 16)

            def stack_queries(q):
                if q == 4:
                    sp.wait_ge(ones_set, 2)
                if q >= 12:
                    wait_s_full(sp, q - 8, UNITS[6] - 1)
                src = t["parts"][:, :, :].rearrange("(a r) n c -> r a n c", r=16)
                stack(q, HT, lambda part: [(qs[q % 2][16 * c:16 * c + 16, :, :], src[:, :, part, :])
                                           for c, of in enumerate(PARTS) if of[0] == part])

            sp.wait_ge(consts_ready, 1)
            stack_keys(1)
            stack_keys(3)
            stack_queries(4)
            wait_s_full(sp, 3, 15)
            for name, dst in (("w1T", w1T), ("w3T", w3T), ("w2T", w2T)):
                load(name, dst, t[name])
            for i in range(BR, 8):
                if i == BR + 2:
                    stack_queries(5)
                old = i - BR
                wait_s_read(sp, 4 + old // TILES, 4 * (old % TILES) + 3)
                load_bias(i)
            sp.wait_ge(am_ready, 1)
            load("pair_sel", pair_sel.bitcast(U16), t["pair_sel"])
            stack_queries(12)
            stack_queries(13)
            for b in range(B):
                sp.wait_ge(x_final, b + 1)
                sp.dma_start(out[b].rearrange("(t p) d -> p t d", p=128),
                             x[:, TILES * b:TILES * b + TILES, :]).then_inc(stored, 16)
            sp.wait_ge(stored, 32)

        @block.tensor
        def _(pe):
            mm = nc.tensor.matmul

            def begin_t(key):
                wait_t_free(pe, key)
                return t_bank(key)

            def end_t(ins, key):
                ins.then_inc(t_full[T_USE[key][0]], 1)

            def prepare0():
                pe.wait_ge(loaded["ctxT"], 16)
                for h in range(8):
                    if h % 4 == 0:
                        pe.wait_ge(loaded[f"wk0_{h}"], 16)
                        pe.wait_ge(loaded[f"wv0_{h}"], 16)
                    for key, w in ((("k0", h), wk0), (("v0", h), wv0)):
                        bank = begin_t(key)
                        end_t(mm(bank[:, 0:B * KP], w[:, h, :], ctx_all, start=True, stop=True), key)
                pe.wait_ge(loaded["wq0T"], 16)
                for h in range(8):
                    key = ("a0", h)
                    bank = begin_t(key)
                    wait_t_read(pe, ("k0", h))
                    end_t(mm(bank[:, 0:B * KP], wq0T[:, h, :], kT0[:, h, :], start=True, stop=True), key)
                pe.wait_ge(loaded["wo0"], 16)
                for b in range(B):
                    for i in range(2):
                        key = ("vo", b, i)
                        bank = begin_t(key)
                        for g in range(4):
                            h = 4 * i + g
                            wait_t_read(pe, ("v0", h))
                            last = mm(bank[:, 128 * g:128 * g + 128], vT0[:, h, b, 0:KM], wo0[:, h, :],
                                      start=True, stop=True)
                        end_t(last, key)
                for b in range(B):
                    key = ("vr", b)
                    bank = begin_t(key)
                    for u in range(2):
                        for g in range(4):
                            h = 4 * u + g
                            last = mm(bank[0:RR, 128 * u:128 * u + 128], vT0_rem[:, h, b, :], wo0[:, h, :],
                                      start=g == 0, stop=g == 3)
                    end_t(last, key)

                pe.wait_ge(loaded["const"], 16)

            def prepare(key):
                bank = begin_t(key)
                i = key[1]
                wk, wv, bv = {1: (wk1, wv1, bv1), 2: (wk2, wv2, bv2), 3: (wk3, wv3, bv3)}[i]
                if key[0] == "k":
                    last = mm(bank[:, 0:B * KP], wk, ctx_all, start=True, stop=True)
                else:
                    b = key[2]
                    mm(bank[:, 0:128], ctxT[:, b, 0:KM], wv, start=True, stop=False)
                    mm(bank[:, 0:128], ones[0:1, :], bv, start=False, stop=True)
                    lhs = ctxT[:, b, KM:SK] if i == 2 else ctx_rem[:, b, :]
                    o = bank[0:lhs.shape[1], 128:256]
                    mm(o, lhs, wv, start=True, stop=False)
                    last = mm(o, ones[0:1, 0:lhs.shape[1]], bv, start=False, stop=True)
                end_t(last, key)

            def scores(q, n):
                b, i = q % 2, layer(q)
                tt, u = tile_of(q, n)
                wait_s_free(pe, q, n)
                sl = slot(q, n)
                tok = slice(128 * tt, 128 * tt + 128)
                if i == 0:
                    for g in range(4):
                        last = mm(sl[:, g, 0:SK], xnT[b][:, tok], a0[:, 4 * u + g, b, 0:SK], start=True, stop=True)
                else:
                    for g in range(2):
                        last = mm(sl[:, 2 * g:2 * g + 2, 0:SK], qs[b][0:CR, 2 * u + g, tok],
                                  ks[i][0:CR, 2 * u + g, :, SK * b:SK * b + SK], start=True, stop=True)
                last.then_inc(s_full[S_USE[q, n][0]], 1)

            def turn_probs(q, n):
                tt, u = tile_of(q, n)
                key = ("t", q, n)
                if layer(q) == 0:
                    pe.wait_ge(probs_ready, P_USE[q, n] + 1)
                else:
                    wait_exp_done(pe, q, n)
                if u == 0 and M_USE[q, tt] > 0:
                    pe.wait_ge(m_free, M_USE[q, tt])
                p = probs[:, P_USE[q, n] % NP]
                last = nc.tensor.transpose(psM[0:RR, 128 * u:128 * u + 128],
                                           p[:, KM:SK, :].rearrange("p k g -> p (k g)"), ident)
                if u == UNITS[q // 2] // TILES - 1:
                    last.then_inc(m_full, 1)
                bank = begin_t(key)
                for g in range(4):
                    last = nc.tensor.transpose(bank[:, 128 * g:128 * g + 128], p[:, 0:KM, g], ident)
                end_t(last, key)

            def values(q, p, piece):
                b, i, nu = q % 2, layer(q), UNITS[q // 2] // TILES
                use = O_USE[q, p]
                pieces = LAGS[q // 2][2] - LAGS[q // 2][1] + 1
                if piece == 0:
                    for n in range(p * 2 * nu, (p + 1) * 2 * nu):
                        if n >= (p + 1) * 2 * nu - 4:
                            wait_t_read(pe, ("t", q, n))
                    if use > 0:
                        pe.wait_ge(o_free, use)
                src = pT[:, use % 2]
                if i == 0:
                    for c in range(4 * piece, 4 * piece + 4):
                        mm(psO[:, 0:256], vo_main[:, b, c, :], src[:, c, :], start=c == 0, stop=False)
                else:
                    g = piece
                    for u in range(nu):
                        mm(psO[32 * u:32 * u + 32, 0:256], vm[i][:, b, u, 32 * g:32 * g + 32],
                           src[:, 4 * u + g, :], start=g == 0, stop=False, skip_group_check=True)
                if piece < pieces - 1:
                    return
                pe.wait_ge(m_free, M_USE[q, 2 * p + 1] + 1)
                for u in range(nu):
                    if i == 0:
                        last = mm(psO[:, 0:256], vo_rem[0:RR, b, u, :], src[0:RR, 8 + u, :], start=False, stop=u == 1)
                    else:
                        last = mm(psO[32 * u:32 * u + 32, 0:256], vr[i][:, b, 32 * u:32 * u + 32],
                                  src[0:RR, 4 * nu + u, :], start=False, stop=True, skip_group_check=True)
                last.then_inc(o_full, 1)

            def turn_sums(q, p):
                key = ("rt", q, p)
                bank = begin_t(key)
                pe.wait_ge(sums_ready, PAIR_USE[q, p] + 1)
                for c in range(2):
                    last = nc.tensor.transpose(bank[0:16, 128 * c:128 * c + 128],
                                               pair_rsums[:, O_USE[q, p] % 2, c, :], ident)
                end_t(last, key)

            def expand(q, p):
                wait_t_read(pe, ("rt", q, p))
                key = ("rx", q, p)
                bank = begin_t(key)
                end_t(mm(bank[:, 0:256], head_sel, rT[:, :], start=True, stop=True), key)

            def finish(q, p):
                key = ("fin", q, p)
                use = O_USE[q, p]
                bank = begin_t(key)
                pe.wait_ge(o_free, use + 1)
                for c in range(2):
                    part = oT[:, use % 2, 128 * c:128 * c + 128]
                    o = bank[:, 128 * c:128 * c + 128]
                    if layer(q) == 1:
                        mm(o, part, wo1, start=True, stop=False)
                        last = mm(o, ones[0:1, :], bo1, start=False, stop=True)
                    else:
                        last = nc.tensor.transpose(o, part, ident)
                end_t(last, key)

            def run_steps(events):
                for what, q, n in events:
                    if what == "feed":
                        if n == 0 and layer(q) > 0:
                            wait_stacked(pe, q)
                        if n == 0 and layer(q) > 0 and q % 2 == 0:
                            wait_stacked(pe, ("k", layer(q)))
                        scores(q, n)
                    elif what == "transpose":
                        turn_probs(q, n)
                    elif what == "turn sums":
                        turn_sums(q, n)
                    elif what == "expand":
                        expand(q, n)
                    elif what == "values":
                        values(q, *n)
                    elif what == "finish":
                        finish(q, n)

            def tokens_major(key, lhs_of, rhs):
                bank = begin_t(key)
                w = rhs.shape[1]
                for tt in range(TILES):
                    last = mm(bank[:, w * tt:w * tt + w], lhs_of(tt), rhs, start=True, stop=True)
                end_t(last, key)

            def expert_unit(q, n):
                tt, part = n // 4, n % 4
                wait_s_free(pe, q, n)
                sl = slot(q, n)
                for g in range(2):
                    e = 8 * part + 4 * g
                    last = mm(sl[:, 2 * g:2 * g + 2, :].rearrange("p g c -> p (g c)"),
                              xnT[q % 2][:, 128 * tt:128 * tt + 128],
                              w_exp0[:, e:e + 4, :].rearrange("p e d -> p (e d)"), start=True, stop=True)
                last.then_inc(s_full[S_USE[q, n][0]], 1)

            def lowrank_unit(q, n):
                wait_s_free(pe, q, n)
                sl = slot(q, n)
                for g in range(2):
                    c = 2 * n + g
                    last = mm(sl[:, 2 * g:2 * g + 2, :].rearrange("p g c -> p (g c)"), v1[:, 128 * c:128 * c + 128],
                              p1, start=True, stop=True)
                last.then_inc(s_full[S_USE[q, n][0]], 1)

            def moe3_unit(q, n):
                wait_s_free(pe, q, n)
                sl = slot(q, n)
                for g, w in enumerate((w1T, w3T)):
                    last = mm(sl[:, 2 * g:2 * g + 2, :].rearrange("p g c -> p (g c)"), w[:, n, :], xnT[q % 2][:, :],
                              start=True, stop=True)
                last.then_inc(s_full[S_USE[q, n][0]], 1)

            def gate_spread(q, n):
                key = ("gb", q, n)
                bank = begin_t(key)
                end_t(mm(bank[:, :], pair_sel[:, n - 1, :], gT_b, start=True, stop=True), key)

            def moe3_out(q, n):
                if n == 0:
                    wait_s_read(pe, q, 0)
                    pe.wait_ge(o_free, O_USE[q, 0])
                else:
                    wait_t_read(pe, ("gb", q, n))
                src = h3[:, 0, :] if n == 0 else hg[:, n % 2, :]
                last = mm(psO[:, :], w2T[:, n, :], src, start=n == 0, stop=n == F3N - 1)
                last.then_inc(o_full if n == F3N - 1 else y_done, 1)

            def project(q):
                b, k = q % 2, kind(q)
                pe.wait_ge(xnT_ready, q + 1)
                if k in ("attn", "attn2") and q >= 2:
                    key = ("q", q)
                    bank = begin_t(key)
                    w = {1: wq1, 2: wq2, 3: wq3}[layer(q)]
                    end_t(mm(bank[:, :], w, xnT[b][:, :], start=True, stop=True), key)
                elif k in ("moe0", "moe3"):
                    if q == 2:
                        pe.wait_ge(loaded["routerT"], 16)
                    if q == 14:
                        pe.wait_ge(loaded["gate3T"], 16)
                    tokens_major(("logits", q), lambda tt: xnT[b][:, 128 * tt:128 * tt + 128],
                                 (routerT if k == "moe0" else gate3T)[:, :])
                elif k == "lowrank":
                    if q == 6:
                        for n in ("u1", "v1", "u2", "v2b"):
                            pe.wait_ge(loaded[n], 16)
                    key = ("p1", q)
                    bank = begin_t(key)
                    end_t(mm(bank[0:32, :], u1[:, :], xnT[b][:, :], start=True, stop=True), key)

            def head(q):
                b, k = q % 2, kind(q)
                if k == "attn":
                    run_steps(head_steps(q))
                elif k == "moe0":
                    if q == 2:
                        pe.wait_ge(loaded["w_exp0"], 16)
                    expert_unit(q, 0)
                    expert_unit(q, 1)
                elif k == "moe3":
                    if q == 14:
                        for n in ("w1T", "w3T", "w2T", "b2_exp", "pair_sel"):
                            pe.wait_ge(loaded[n], 16)
                    moe3_unit(q, 0)
                    moe3_unit(q, 1)
                elif k == "lowrank":
                    wait_t_read(pe, ("p1", q))
                    lowrank_unit(q, 0)
                    lowrank_unit(q, 1)
                elif k == "attn2":
                    wait_t_read(pe, ("q", q))
                    wait_s_free(pe, q, 0)
                    for tt in range(TILES):
                        last = mm(slot(q, 0)[:, tt, 0:SK], qT[:, 128 * tt:128 * tt + 128], kT2[:, b, 0:SK],
                                  start=True, stop=True)
                    last.then_inc(s_full[S_USE[q, 0][0]], 1)

            def turn(q):
                key = ("ln", q)
                bank = begin_t(key)
                pe.wait_ge(xn_ready, q + 1)
                for tt in range(TILES):
                    last = nc.tensor.transpose(bank[:, 128 * tt:128 * tt + 128], xn[:, tt, :], ident)
                end_t(last, key)

            def rest(q, part):
                k = kind(q)
                if k == "attn":
                    run_steps(rest_steps(q, part))
                elif k == "moe0":
                    todo = PREP[3 * part:3 * part + 3] if q == 2 else []
                    if q == 2 and part == 0:
                        pe.wait_ge(loaded["sq"], 16)
                        pe.wait_ge(loaded["rows"], 16)
                    for n in rest_units(part):
                        expert_unit(q, n)
                        if todo:
                            prepare(todo.pop(0))
                elif k == "lowrank" and part == 0:
                    key = ("q1", q)
                    bank = begin_t(key)
                    for c in range(4):
                        pe.wait_ge(hidden_ready, (q - 6) * 4 + c + 1)
                        last = mm(bank[0:32, :], u2[:, c, :], hidden[:, c, :], start=c == 0, stop=c == 3)
                    end_t(last, key)
                elif k == "attn2" and part == 0:
                    pe.wait_ge(probs_ready, P_READY[q])
                    p = probs[:, P_USE[q, 0] % NP]
                    for key, keys in ((("main", q), slice(0, KM)), (("rem", q), slice(KM, SK))):
                        bank = begin_t(key)
                        for tt in range(TILES):
                            last = nc.tensor.transpose(bank[0:keys.stop - keys.start, 128 * tt:128 * tt + 128],
                                                       p[:, keys, tt], ident)
                        end_t(last, key)
                elif q == 10 and part == 2:
                    key = ("amax_t", q)
                    bank = begin_t(key)
                    pe.wait_ge(am_ready, 1)
                    end_t(nc.tensor.transpose(bank[0:2, 0:128], am[:, :], ident), key)
                    key = ("amax_b", q)
                    bank = begin_t(key)
                    pe.wait_ge(am_ready, 2)
                    end_t(mm(bank[:, 0:2], ones[0:2, :], am2[:, 2:4], start=True, stop=True), key)
                elif k == "moe3":
                    if part == 0:
                        moe3_out(q, 0)
                        key = ("gates", q)
                        bank = begin_t(key)
                        pe.wait_ge(gate_ready, q - 14 + 3)
                        for tt in range(TILES):
                            last = nc.tensor.transpose(bank[0:3 * E3, 128 * tt:128 * tt + 128],
                                                       gate_parts[:, q % 2, tt, :], ident)
                        end_t(last, key)
                        wait_t_read(pe, key)
                        mm(psO[:, :], b2_exp[:, :], gT, start=False, stop=False)
                        gate_spread(q, 1)
                    for n in moe3_units(part):
                        moe3_unit(q, n + 1)
                        gate_spread(q, n + 1)
                        if n > 1:
                            moe3_out(q, n - 1)

            def tail(q):
                b, k = q % 2, kind(q)
                if k == "attn":
                    run_steps(tail_steps(q))
                elif k == "lowrank":
                    wait_t_read(pe, ("q1", q))
                    tokens_major(("fin", q), lambda tt: q1[:, 128 * tt:128 * tt + 128], v2b[:, :])
                elif k == "attn2":
                    wait_t_read(pe, ("main", q))
                    wait_t_read(pe, ("rem", q))
                    key = ("fin", q)
                    bank = begin_t(key)
                    for tt in range(TILES):
                        tok = slice(128 * tt, 128 * tt + 128)
                        mm(bank[:, tok], pT[:, 0, 0:2, :].rearrange("p a c -> p (a c)")[:, tok], v2m[:, b, :],
                           start=True, stop=False)
                        last = mm(bank[:, tok], pT[0:KR, 1, 0:2, :].rearrange("p a c -> p (a c)")[:, tok],
                                  v2r[:, b, :], start=False, stop=True)
                    end_t(last, key)
                elif k == "fp8":
                    pe.wait_ge(quant_ready, b + 2)
                    tokens_major(("fin", q), lambda tt: x8[:, b, 128 * tt:128 * tt + 128], w8[:, :])
                elif k == "moe3":
                    moe3_out(q, F3N - 2)
                    moe3_out(q, F3N - 1)
                    key = ("fin", q)
                    bank = begin_t(key)
                    pe.wait_ge(o_free, O_USE[q, 0] + 1)
                    for tt in range(TILES):
                        last = nc.tensor.transpose(bank[:, 128 * tt:128 * tt + 128], oT3[:, 128 * tt:128 * tt + 128],
                                                   ident)
                    end_t(last, key)

            prepare0()
            walk(head, tail, lambda q: None, turn, project, rest)

        @block.vector
        def _(dve):
            v = nc.vector
            chain = [0]

            def tick(ins):
                chain[0] += 1
                ins.then_inc(dve_done, 1)

            def settle():
                dve.wait_ge(dve_done, chain[0])

            def link(ins):
                tick(ins)
                settle()

            def copy(dst, src):
                return v.tensor_copy(dst, src)

            def free_t(ins, key):
                ins.then_inc(t_free[T_USE[key][0]], 1)

            def constants():
                for n in ("const", "cols", "wide", "masks1", "masks3"):
                    dve.wait_ge(loaded[n], 16)
                tick(v.tensor_tensor(coef[:, 0:1], betas[:, 0:1], betas[:, 1:2], ALU.add))
                tick(v.tensor_copy(mask1[:, :, :].rearrange("p b k -> p (b k)"), mask1_u8))
                tick(v.tensor_copy(mask3f, mask3_i32))
                settle()
                tick(v.tensor_tensor(coef[:, 1:2], coef[:, 0:1], betas[:, 2:3], ALU.subtract))
                tick(v.tensor_reduce(all_masked[:, :], mask1[:, :, :], AX.X, ALU.min))
                tick(v.tensor_scalar(mask_b[3][:, :], mask3f, 0.0, NEG, ALU.is_gt, ALU.mult))
                settle()
                link(v.tensor_scalar(all_masked[:, :], all_masked[:, :], -1.0, 1.0, ALU.mult, ALU.add))
                link(v.tensor_tensor(mask1[:, :, 0], mask1[:, :, 0], all_masked[:, :], ALU.mult))
                link(v.tensor_scalar(mask_b[1][:, :], mask1[:, :, :].rearrange("p b k -> p (b k)"), NEG, None,
                                     ALU.mult))
                dve.wait_ge(tanh_ready, 1)
                v.tensor_scalar(tg_bias[:, :], b_fp8, tg[:, X_SCALE[5]:X_SCALE[5] + 1], None,
                                ALU.mult).then_inc(consts_ready, 1)
                dve.wait_ge(consts_ready, 1)

            def prepare0():
                dve.wait_ge(loaded["ctxT"], 16)
                dve.wait_ge(zeroed, 1)
                v.tensor_copy(ctx_rem[:, :, :].rearrange("p b (k g) -> p b k g", g=4),
                              ctxT[:, :, KM:SK].unsqueeze(3).broadcast_to([128, B, KR, 4]))
                for h in range(8):
                    key = ("v0", h)
                    wait_t_full(dve, key)
                    src = t_bank(key)[:, 0:B * KP].rearrange("p (b k) -> p b k", b=B)
                    v.tensor_copy(vT0[:, h, :, 0:KM], src[:, :, 0:KM])
                    free_t(v.tensor_copy(vT0_rem[:, h, :, :].rearrange("p b (k g) -> p b k g", g=4)[:, :, :, h % 4],
                                         src[:, :, KM:SK]), key)
                for h in range(0, 8, 2):
                    key = ("a0", h)
                    wait_t_full(dve, key)
                    free_t(v.tensor_scalar(a0[:, h, :, :], t_bank(key)[:, 0:B * KP].rearrange("p (b k) -> p b k", b=B),
                                           64.0 ** -0.5, None, ALU.mult), key)
                for b in range(B):
                    key = ("vo", b, 0)
                    wait_t_full(dve, key)
                    free_t(v.tensor_copy(vo_main[:, b, 0:4, :].rearrange("p h d -> p (h d)"), t_bank(key)[:, :]), key)

            def stats_of(q):
                b = q % 2
                if q < 2:
                    dve.wait_ge(loaded["x"], 16)
                settle()
                xs = x[:, TILES * b:TILES * b + TILES, :]
                for tt in range(TILES):
                    tick(v.bn_stats(stats[:, tt, :], xs[:, tt, :]))
                settle()
                for tt in range(TILES):
                    tick(v.bn_aggr(meanvar[:, tt, :], stats[:, tt, :]))
                settle()
                v.tensor_scalar(vareps[:, :], meanvar[:, :, 1], 1e-5, None, ALU.add).then_inc(eps_added, 1)
                dve.wait_ge(rstd_ready, q + 1)
                if q > 0:
                    wait_t_full(dve, ("ln", q - 1))
                for tt in range(TILES):
                    last = v.tensor_scalar(xn[:, tt, :], xs[:, tt, :], meanvar[:, tt, 0:1], rstd[:, tt:tt + 1],
                                           ALU.subtract, ALU.mult)
                last.then_inc(xn_ready, 1)

            def add_to_x(q, key, tiles, width):
                wait_t_full(dve, key)
                s = q // 2
                xs = x[:, tiles.start:tiles.stop, :].rearrange("p t d -> p (t d)")
                v.scalar_tensor_tensor(xs, t_bank(key)[:, 0:width], tg[:, X_SCALE[s]:X_SCALE[s] + 1], xs,
                                       ALU.mult, ALU.add).then_inc(t_free[T_USE[key][0]], 1)
                wait_t_read(dve, key)

            def maxima(q, n):
                b = q % 2
                ring = P_USE[q, n] % NP
                wait_s_full(dve, q, n)
                src = slot(q, n)[:, :, 0:SK]
                if layer(q) == 1:
                    tt, u = tile_of(q, n)
                    if u == 0:
                        dve.wait_ge(bias_loaded[TILES * b + tt], 16)
                    use = BIAS_USE[q, n]
                    if use >= NB:
                        dve.wait_ge(bias_exp_done, use - NB + 1)
                    part = bias1[:, (TILES * b + tt) % BR, 4 * u:4 * u + 4, :]
                    v.tensor_tensor(scores_sb[:, use % NB, :, :], src, part, ALU.add).then_inc(
                        s_free[S_USE[q, n][0]], 1)
                    src = scores_sb[:, use % NB, :, :]
                    wait_s_read(dve, q, n)
                v.tensor_reduce(negmax[:, ring, :], src, AX.X, ALU.max, negate=True).then_inc(max_ready, 1)

            def reciprocals(q, n):
                ring = P_USE[q, n] % NP
                wait_exp_done(dve, q, n)
                v.reciprocal(rsums[:, ring, :], sums[:, ring, :]).then_inc(rsum_ready, 1)

            def pair_reciprocals(q, p):
                nu = UNITS[q // 2] // TILES
                wait_exp_done(dve, q, (p + 1) * 2 * nu - 1)
                use = O_USE[q, p]
                v.reciprocal(pair_rsums[:, use % 2], pair_sums[:, use % 2]).then_inc(sums_ready, 1)

            def scale_values(q, p):
                use = O_USE[q, p]
                dve.wait_ge(o_full, use + 1)
                dve.wait_ge(rexp_ready, PAIR_USE[q, p] + 1)
                v.tensor_tensor(oT[:, use % 2, :], psO[:, 0:256], rexp[:, use % 2, :], ALU.mult).then_inc(o_free, 1)

            def run_steps(events):
                for what, q, n in events:
                    if what == "scores":
                        maxima(q, n)
                    elif what == "normalise":
                        reciprocals(q, n)
                    elif what == "sums":
                        pair_reciprocals(q, n)
                    elif what == "evacuate" and layer(q) > 0:
                        scale_values(q, n)
                    elif what == "collect":
                        copy_turned(nc.vector, copy, q, n)
                    elif what == "finish":
                        t0 = TILES * (q % 2) + 2 * n
                        add_to_x(q, ("fin", q, n), range(t0, t0 + 2), 256)

            def gating(q):
                first = kind(q) == "moe0"
                ne = E0 if first else E3
                io = (iota32 if first else iota16).rearrange("p (t e) -> p t e", t=TILES)
                key = ("logits", q)
                wait_t_full(dve, key)
                bank = t_bank(key)[:, 0:TILES * ne].rearrange("p (t e) -> p t e", t=TILES)
                l, sel, e = lg[:, :, 0:ne], lsel[:, :, 0:ne], ex[:, :, 0:ne]
                free_t(v.tensor_copy(l, bank), key)
                wait_t_read(dve, key)
                if not first:
                    v.tensor_copy(sel, l).then_inc(exp_in, 1)
                    dve.wait_ge(exp_in, EXP_IN[q])
                    link(v.tensor_tensor(sel, l, ebias.unsqueeze(1).broadcast_to([128, TILES, ne]), ALU.add))
                    l = sel
                for tt in range(TILES):
                    tick(v.max(top8[:, tt, :], l[:, tt, :]))
                settle()
                for tt in range(TILES):
                    tick(v.max_index(idx8[:, tt, :], top8[:, tt, :], l[:, tt, :]))
                if first:
                    v.tensor_tensor(sel, l, top8[:, :, 0:1].broadcast_to([128, TILES, ne]),
                                    ALU.subtract).then_inc(exp_in, 1)
                settle()
                link(v.tensor_copy(idxf[:, :, :], idx8[:, :, 0:2]))
                for i in range(2):
                    tick(v.tensor_tensor(hit[:, i, :, 0:ne], io, idxf[:, :, i:i + 1].broadcast_to([128, TILES, ne]),
                                         ALU.is_equal))
                settle()
                link(v.tensor_tensor(hit[:, 0, :, 0:ne], hit[:, 0, :, 0:ne], hit[:, 1, :, 0:ne], ALU.add))
                dve.wait_ge(exp_out, EXP_OUT[q])
                g = gate[:, q % 2, :, 0:ne]
                if first:
                    link(v.tensor_reduce(gsum[:, 0, :], e, AX.X, ALU.add))
                else:
                    link(v.tensor_scalar(e, e, 1.0, None, ALU.add))
                    link(v.reciprocal(e, e))
                link(v.tensor_tensor(e, e, hit[:, 0, :, 0:ne], ALU.mult))
                if not first:
                    link(v.tensor_reduce(gsum[:, 0, :], e, AX.X, ALU.add))
                    link(v.tensor_scalar(gsum[:, 0, :], gsum[:, 0, :], 1e-10, None, ALU.add))
                link(v.reciprocal(gsum[:, 1, :], gsum[:, 0, :]))
                last = v.tensor_tensor(g, e, gsum[:, 1, :].unsqueeze(2).broadcast_to([128, TILES, ne]), ALU.mult)
                if not first:
                    link(last)
                    parts_of = gate_parts[:, q % 2].rearrange("p t (i e) -> p t i e", i=3)
                    for i in range(2):
                        link(v.tensor_copy(part_b[:, :, :], g))
                        tick(v.tensor_copy(parts_of[:, :, i, :], part_b[:, :, :]))
                        rest_of = parts_of[:, :, 2, :] if i == 1 else g
                        last = v.tensor_tensor(rest_of, g, part_b[:, :, :], ALU.subtract)
                        if i == 0:
                            link(last)
                last.then_inc(gate_ready, 1)
                dve.wait_ge(gate_ready, {2: 1, 3: 2, 14: 3, 15: 4}[q])

            def weigh(q, n):
                tt, part = n // 4, n % 4
                tile = TILES * (q % 2) + tt
                wait_s_full(dve, q, n)
                w = gate[:, q % 2, tt, 8 * part:8 * part + 8].rearrange("p (g e) -> p g e", g=4)
                src = slot(q, n).rearrange("p g (e d) -> p g e d", e=2)
                w = w.unsqueeze(3).broadcast_to([128, 4, 2, 128])
                if part == 0:
                    if tile >= 2:
                        dve.wait_ge(acc_read, tile - 1)
                    dst, done = acc0[:, tile % 2, :], s_free[S_USE[q, n][0]]
                else:
                    m = 3 * tile + part - 1
                    if m >= 2:
                        dve.wait_ge(acc_added, m - 1)
                    dst, done = mult0[:, m % 2, :], s_free[S_USE[q, n][0]]
                v.tensor_tensor(dst.rearrange("p (g e d) -> p g e d", g=4, e=2), src, w, ALU.mult).then_inc(done, 1)

            def add_last(q, tt):
                tile = TILES * (q % 2) + tt
                m = 3 * tile + 2
                dve.wait_ge(acc_added, m)
                wait_s_read(dve, q, 4 * tt + 3)
                v.tensor_tensor(acc0[:, tile % 2, :], acc0[:, tile % 2, :], mult0[:, m % 2, :],
                                ALU.add).then_inc(acc_added, 1)

            def sum_experts(q, tt):
                tile = TILES * (q % 2) + tt
                dve.wait_ge(acc_added, 3 * tile + 3)
                settle()
                v.tensor_reduce(red0[:, :], acc0[:, tile % 2, :].rearrange("p (e d) -> p d e", e=8), AX.X,
                                ALU.add).then_inc(acc_read, 1)
                dve.wait_ge(acc_read, tile + 1)
                s = X_SCALE[q // 2]
                tick(v.scalar_tensor_tensor(x[:, tile, :], red0[:, :], tg[:, s:s + 1], x[:, tile, :],
                                            ALU.mult, ALU.add))

            def quantise(src, scale, tmp, dst, sig):
                link(v.tensor_scalar(tmp[0], src, scale, None, ALU.mult))
                link(v.tensor_scalar(tmp[1].bitcast(U32), tmp[0].bitcast(U32), 0x7F800000, None, ALU.bitwise_and))
                link(v.tensor_scalar(tmp[1], tmp[1], 2.0 ** -6, 1.5 * 2.0 ** 20, ALU.max, ALU.mult))
                link(v.tensor_tensor(tmp[0], tmp[0], tmp[1], ALU.add))
                v.tensor_tensor(dst, tmp[0], tmp[1], ALU.subtract).then_inc(sig, 1)

            def quantise_x(i):
                quantise(xnT[i][:, :], fsc[:, 4:5], (fq[:, 0, :], fq[:, 1, :]), x8[:, i, :], quant_ready)
                dve.wait_ge(quant_ready, i + 2)

            def project(q):
                k = kind(q)
                if k == "fp8":
                    dve.wait_ge(xn_ready, q + 1)
                    xs = x[:, TILES * (q % 2):TILES * (q % 2) + TILES, :]
                    tick(v.tensor_tensor(xs, xs, tg_bias[:, :].unsqueeze(1).broadcast_to([128, TILES, D]), ALU.add))
                if k in ("attn", "attn2") and q >= 2:
                    key = ("q", q)
                    wait_t_full(dve, key)
                    bias, dim = {1: (bq1, 8.0), 2: (bq2, 128.0), 3: (bq3, 8.0)}[layer(q)]
                    free_t(v.tensor_scalar(qT[:, :], t_bank(key)[:, :], bias, dim ** -0.5, ALU.add, ALU.mult), key)
                    if q in STACKS:
                        wait_t_read(dve, key)
                        for saved in parts_saved:
                            dve.wait_ge(saved, 16 * STACKS[q])
                        v.tensor_copy(parts[:, 0, :], qT[:, :]).then_inc(split, 1)
                        dve.wait_ge(split, 3 * STACKS[q] + 1)
                        link(v.tensor_tensor(left[:, :], qT[:, :], parts[:, 0, :], ALU.subtract))
                        v.tensor_copy(parts[:, 1, :], left[:, :]).then_inc(split, 1)
                        dve.wait_ge(split, 3 * STACKS[q] + 2)
                        v.tensor_tensor(parts[:, 2, :], left[:, :], parts[:, 1, :],
                                        ALU.subtract).then_inc(split, 1)
                elif k in ("moe0", "moe3"):
                    gating(q)

            def head(q):
                b, k = q % 2, kind(q)
                if k == "attn":
                    run_steps(head_steps(q))
                elif k == "moe0":
                    weigh(q, 0)
                elif k == "attn2":
                    wait_s_full(dve, q, 0)
                    if q == 8:
                        dve.wait_ge(loaded["phi"], 16)
                    sc = scores_sb[:, q % 2, :, :]
                    v.scalar_tensor_tensor(sc, phi[:, TILES * b:TILES * b + TILES, :], coef[:, 1:2],
                                           slot(q, 0)[:, :, 0:SK], ALU.mult, ALU.add).then_inc(
                        s_free[S_USE[q, 0][0]], 1)
                    wait_s_read(dve, q, 0)
                    v.tensor_reduce(negmax[:, P_USE[q, 0] % NP, :], sc, AX.X, ALU.max,
                                    negate=True).then_inc(max_ready, 1)
                    reciprocals(q, 0)

            def moe3_hidden(q, n):
                use = (q - 14) * F3N + n
                wait_s_full(dve, q, n)
                dve.wait_ge(silu_ready, use + 1)
                b3 = sb3 if n == 0 else eb3[:, n - 1:n]
                dst = h3[:, 0 if n == 0 else 1, :]
                if n == 0 and q == 15:
                    dve.wait_ge(y_done, F3N - 1)
                if n >= 2:
                    wait_t_read(dve, ("gb", q, n - 1))
                v.scalar_tensor_tensor(dst.rearrange("p (g c) -> p g c", g=2), slot(q, n)[:, 2:4, :], b3,
                                       a1[:, use % 2, :].rearrange("p (g c) -> p g c", g=2),
                                       ALU.add, ALU.mult).then_inc(s_free[S_USE[q, n][0]], 1)
                if n == 0:
                    return
                wait_s_read(dve, q, n)
                key = ("gb", q, n)
                wait_t_full(dve, key)
                if n >= 3:
                    dve.wait_ge(y_done, (q - 14) * (F3N - 1) + n - 1)
                elif n == 2 and q == 15:
                    dve.wait_ge(o_full, O_USE[14, 0] + 1)
                free_t(v.tensor_tensor(hg[:, n % 2, :], dst, t_bank(key)[:, :], ALU.mult), key)

            def rest(q, part):
                b, k = q % 2, kind(q)
                if k == "attn":
                    run_steps(rest_steps(q, part))
                elif k == "moe0":
                    for n in rest_units(part):
                        if n % 4 != 1:
                            weigh(q, n)
                        if n % 4 == 0:
                            add_last(q, n // 4 - 1)
                        if n % 4 == 2 and n > 4:
                            sum_experts(q, n // 4 - 1)
                elif k == "attn2" and part == 0:
                    key = ("main", q)
                    wait_t_full(dve, key)
                    free_t(v.tensor_copy(pT[:, 0, 0:2, :].rearrange("p a c -> p (a c)"), t_bank(key)[:, :]), key)
                elif q == 10 and part == 2:
                    dve.wait_ge(xnT_ready, 12)
                    for i in range(B):
                        tick(v.tensor_reduce(fsc[:, i:i + 1], xnT[i][:, :], AX.X, ALU.max, apply_absolute_value=True))
                    tick(v.tensor_reduce(am[:, 1:2], w_fp8, AX.X, ALU.max, apply_absolute_value=True))
                    settle()
                    v.tensor_tensor(am[:, 0:1], fsc[:, 0:1], fsc[:, 1:2], ALU.max).then_inc(am_ready, 1)
                    key = ("amax_t", q)
                    wait_t_full(dve, key)
                    free_t(v.tensor_reduce(am2[:, 0:1], t_bank(key)[0:2, 0:128], AX.X, ALU.max), key)
                    wait_t_read(dve, key)
                    v.tensor_scalar(am2[:, 2:4], ident[0:2, 0:2], am2[:, 0:1], None, ALU.mult).then_inc(am_ready, 1)
                    key = ("amax_b", q)
                    wait_t_full(dve, key)
                    free_t(v.tensor_scalar(fsc[:, 2:4], t_bank(key)[:, 0:2], 1e-12, None, ALU.max), key)
                    wait_t_read(dve, key)
                    link(v.reciprocal(fsc[:, 2:4], fsc[:, 2:4]))
                    link(v.tensor_scalar(fsc[:, 4:6], fsc[:, 2:4], 448.0, None, ALU.mult))
                    link(v.tensor_tensor(fsc[:, 6:7], fsc[:, 4:5], fsc[:, 5:6], ALU.mult))
                    link(v.reciprocal(fsc[:, 7:8], fsc[:, 6:7]))
                    s = X_SCALE[5]
                    link(v.tensor_tensor(fsc[:, 6:7], fsc[:, 7:8], tg[:, s:s + 1], ALU.mult))
                    quantise(w_fp8, fsc[:, 5:6], (fq[:, 0, 0:128], fq[:, 1, 0:128]), w8[:, :], quant_ready)
                    dve.wait_ge(quant_ready, 1)
                    quantise_x(0)
                elif q == 11 and part == 0:
                    quantise_x(1)
                elif k == "moe3":
                    for n in (0, *moe3_units(0)) if part == 0 else moe3_units(part):
                        moe3_hidden(q, n)

            def tail(q):
                b, k = q % 2, kind(q)
                half = range(TILES * b, TILES * b + TILES)
                if k == "attn":
                    run_steps(tail_steps(q))
                elif k == "moe0":
                    add_last(q, TILES - 1)
                    sum_experts(q, TILES - 1)
                elif k == "fp8":
                    key = ("fin", q)
                    wait_t_full(dve, key)
                    settle()
                    xs = x[:, half.start:half.stop, :]
                    free_t(v.scalar_tensor_tensor(xs.rearrange("p t d -> p (t d)"), t_bank(key)[:, :], fsc[:, 6:7],
                                                  xs.rearrange("p t d -> p (t d)"), ALU.mult, ALU.add), key)
                    wait_t_read(dve, key)
                elif k == "moe3":
                    moe3_hidden(q, F3N - 1)
                    key = ("fin", q)
                    wait_t_full(dve, key)
                    s = X_SCALE[7]
                    xs = x[:, half.start:half.stop, :].rearrange("p t d -> p (t d)")
                    v.scalar_tensor_tensor(xs, t_bank(key)[:, :], tg[:, s:s + 1], xs, ALU.mult,
                                           ALU.add).then_inc(x_final, 1)
                    if b == 0:
                        dve.wait_ge(x_final, 1)
                        free_t(v.memset(am2[0:1, 0:1], 0.0), key)
                else:
                    add_to_x(q, ("fin", q), half, 512)

            stats_of(0)
            prepare0()
            constants()
            walk(head, tail, stats_of, lambda q: None, project, rest)

        @block.scalar
        def _(act):
            a = nc.scalar.activation

            def copy(dst, src):
                return a(dst, src, ACT.Copy)

            def free_t(ins, key):
                ins.then_inc(t_free[T_USE[key][0]], 1)

            def load(name, dst, src):
                act.dma_start(dst, src).then_inc(loaded[name], 16)

            load("x", x[:, :, :], t["x"].rearrange("(t p) d -> p t d", p=128))
            load("wide", wide[:, :], t["wide"].broadcast_to([128, 155]))
            load("cols", cols[:, :], t["cols"])
            load("masks1", mask1_u8, t["mask1"].broadcast_to([128, B * SK]))
            load("masks3", mask3_i32, t["mask3"].broadcast_to([128, B * SK]))
            load("rows", rows[:, :], t["rows"])
            act.wait_ge(loaded["wide"], 16)
            a(tg[:, :], gates_in, ACT.Tanh).then_inc(tanh_ready, 1)

            def prepare0():
                for h in range(8):
                    key = ("k0", h)
                    wait_t_full(act, key)
                    free_t(copy(kT0[:, h, :], t_bank(key)[:, 0:B * KP]), key)
                for h in range(1, 8, 2):
                    key = ("a0", h)
                    wait_t_full(act, key)
                    free_t(a(a0[:, h, :, :].rearrange("p b k -> p (b k)"), t_bank(key)[:, 0:B * KP], ACT.Copy,
                             scale=64.0 ** -0.5), key)
                for b in range(B):
                    key = ("vo", b, 1)
                    wait_t_full(act, key)
                    free_t(copy(vo_main[:, b, 4:8, :].rearrange("p h d -> p (h d)"), t_bank(key)[:, :]), key)
                for b in range(B):
                    key = ("vr", b)
                    wait_t_full(act, key)
                    free_t(copy(vo_rem[0:RR, b, :, :].rearrange("p u d -> p (u d)"), t_bank(key)[0:RR, 0:256]), key)

            def prepare(key):
                wait_t_full(act, key)
                bank, i = t_bank(key), key[1]
                if key[0] == "k":
                    if i == 2:
                        last = a(kT2[:, :, :].rearrange("p b k -> p (b k)"), bank[:, 0:B * KP], ACT.Identity, bias=bk2)
                    else:
                        if i == 3:
                            act.wait_ge(split, 3)
                        last = a(left[:, 0:B * SK].rearrange("p (b k) -> p b k", b=B),
                                 bank[:, 0:B * KP].rearrange("p (b k) -> p b k", b=B)[:, :, 0:SK],
                                 ACT.Identity, bias=bk1 if i == 1 else bk3)
                else:
                    b = key[2]
                    if i == 2:
                        copy(v2m[:, b, :], bank[:, 0:128])
                        last = copy(v2r[:, b, :], bank[0:KR, 128:256])
                    else:
                        copy(vm[i][:, b, :, :].rearrange("p g (u c) -> p g u c", u=4)[:, :, :, 0:8],
                             bank[:, 0:128].rearrange("p (g u d) -> p g u d", g=4, u=4))
                        for g in range(4):
                            last = a(vr[i][:, b, :].rearrange("p (u c) -> p u c", u=4)[:, :, 8 * g:8 * g + 8],
                                     bank[0:RR, 128:256].rearrange("p (u c) -> p u c", u=4)[:, :, 8 * g:8 * g + 8],
                                     ACT.Copy, scale=rmask[0:RR, g:g + 1])
                free_t(last, key)

            def turn(q):
                key = ("ln", q)
                wait_t_full(act, key)
                copy(xnT[q % 2][:, :], t_bank(key)[:, :]).then_inc(xnT_ready, 1)
                act.wait_ge(xnT_ready, q + 1)
                free_t(copy(spare[:, 0:1], t_bank(key)[:, 0:1]), key)

            def exps(q, n):
                ring = P_USE[q, n] % NP
                if P_USE[q, n] >= NP:
                    old = P_KEYS[P_USE[q, n] - NP]
                    wait_t_full(act, ("t", *old) if kind(old[0]) == "attn" else ("rem", old[0]))
                act.wait_ge(max_ready, P_USE[q, n] + 1)
                if layer(q) == 1:
                    src = scores_sb[:, BIAS_USE[q, n] % NB, :, :]
                elif kind(q) == "attn2":
                    src = scores_sb[:, q % 2, :, :]
                else:
                    src = slot(q, n)
                if kind(q) == "attn" and layer(q) > 0:
                    tt, u = tile_of(q, n)
                    totals = pair_sums[:, O_USE[q, tt // 2] % 2, tt % 2, 4 * u:4 * u + 4]
                else:
                    totals = sums[:, ring, :]
                for g in range(4):
                    last = a(probs[:, ring, :, g], src[:, g, 0:SK], ACT.Exp, bias=negmax[:, ring, g:g + 1],
                             accum_out=totals[:, g:g + 1])
                if layer(q) == 1:
                    last.then_inc(bias_exp_done, 1)
                elif kind(q) == "attn2":
                    last.then_inc(exp_out, 1)
                else:
                    last.then_inc(s_free[S_USE[q, n][0]], 1)

            def run_steps(events):
                for what, q, n in events:
                    if what == "scores":
                        exps(q, n)
                    elif what == "collect":
                        copy_turned(nc.scalar, copy, q, n)
                    elif what == "turn sums":
                        key = ("rt", q, n)
                        wait_t_full(act, key)
                        free_t(copy(rT[:, :], t_bank(key)[0:16, 0:256]), key)
                    elif what == "expand":
                        key = ("rx", q, n)
                        wait_t_full(act, key)
                        copy(rexp[:, O_USE[q, n] % 2, :], t_bank(key)[:, 0:256]).then_inc(rexp_ready, 1)
                        act.wait_ge(rexp_ready, PAIR_USE[q, n] + 1)
                        free_t(copy(spare[:, 3:4], t_bank(key)[:, 0:1]), key)
                    elif what == "evacuate" and layer(q) == 0:
                        use = O_USE[q, n]
                        act.wait_ge(o_full, use + 1)
                        a(oT[:, use % 2, :], psO[:, 0:256], ACT.Identity, bias=bo0).then_inc(o_free, 1)

            def gate_exp(q):
                act.wait_ge(exp_in, EXP_IN[q])
                ne = E0 if q < 4 else E3
                a(ex[:, :, 0:ne], lsel[:, :, 0:ne] if q < 4 else lg[:, :, 0:ne], ACT.Exp,
                  scale=1.0 if q < 4 else -1.0).then_inc(exp_out, 1)

            def weigh(q, n):
                tt = n // 4
                tile = TILES * (q % 2) + tt
                m = 3 * tile
                wait_s_full(act, q, n)
                act.wait_ge(gate_ready, q - 1)
                if m >= 2:
                    act.wait_ge(acc_added, m - 1)
                src = slot(q, n).rearrange("p g c -> p (g c)")
                for e in range(8):
                    last = a(mult0[:, m % 2, 128 * e:128 * e + 128], src[:, 128 * e:128 * e + 128], ACT.Copy,
                             scale=gate[:, q % 2, tt, 8 + e:9 + e])
                last.then_inc(s_free[S_USE[q, n][0]], 1)

            def silu(q, n):
                use = (q - 14) * F3N + n
                wait_s_full(act, q, n)
                if use >= 2:
                    wait_s_read(act, q if n >= 2 else q - 1, n - 2 if n >= 2 else n - 2 + F3N)
                b1 = sb1 if n == 0 else eb1[:, n - 1:n]
                a(a1[:, use % 2, :].rearrange("p (g c) -> p g c", g=2), slot(q, n)[:, 0:2, :], ACT.Silu,
                  bias=b1).then_inc(silu_ready, 1)

            def project(q):
                if kind(q) in ("moe0", "moe3"):
                    gate_exp(q)
                elif kind(q) == "lowrank":
                    key = ("p1", q)
                    wait_t_full(act, key)
                    free_t(copy(p1, t_bank(key)[0:32, :]), key)

            def head(q):
                k = kind(q)
                if k == "attn":
                    run_steps(head_steps(q))
                elif k == "attn2":
                    exps(q, 0)
                elif k == "moe0":
                    weigh(q, 1)
                elif q == 6:
                    a(q1[32:33, :], xnT[0][32:33, :], ACT.Identity, scale=0.0, bias=1.0)

            def tail(q):
                k = kind(q)
                if k == "attn":
                    run_steps(tail_steps(q))
                elif k == "moe3":
                    silu(q, F3N - 1)
                    act.wait_ge(o_full, O_USE[q, 0] + 1)
                    a(oT3, psO[:, :], ACT.Identity, bias=sb2).then_inc(o_free, 1)

            def rest(q, part):
                k = kind(q)
                if k == "attn":
                    run_steps(rest_steps(q, part))
                elif k == "moe0":
                    if q == 2 and part == 0:
                        act.wait_ge(consts_ready, 1)
                        act.wait_ge(zeroed, 2)
                    todo = PREP[3 * part:3 * part + 3] if q == 2 else []
                    for n in rest_units(part):
                        if n % 4 == 1:
                            weigh(q, n)
                        if todo:
                            prepare(todo.pop(0))
                elif k == "lowrank" and part == 0:
                    for n in range(2):
                        wait_s_full(act, q, n)
                        for c in range(2):
                            ins = a(hidden[:, 2 * n + c, :].rearrange("p (g c) -> p g c", g=2),
                                    slot(q, n)[:, 2 * c:2 * c + 2, :], ACT.Gelu_apprx_tanh,
                                    bias=fb1[:, 2 * n + c:2 * n + c + 1])
                            ins.then_inc(hidden_ready, 1)
                        act.wait_ge(hidden_ready, (q - 6) * 4 + 2 * n + 2)
                        copy(spare[:, 2:3], slot(q, n)[:, 0, 0:1]).then_inc(s_free[S_USE[q, n][0]], 1)
                    key = ("q1", q)
                    wait_t_full(act, key)
                    free_t(copy(q1[0:32, :], t_bank(key)[0:32, :]), key)
                elif k == "attn2" and part == 0:
                    key = ("rem", q)
                    wait_t_full(act, key)
                    free_t(copy(pT[0:KR, 1, 0:2, :].rearrange("p a c -> p (a c)"), t_bank(key)[0:KR, :]), key)
                elif k == "moe3":
                    if part == 0:
                        silu(q, 0)
                        key = ("gates", q)
                        wait_t_full(act, key)
                        copy(gT_b, t_bank(key)[0:3 * E3, :])
                        free_t(copy(gT, t_bank(key)[0:3 * E3, :]), key)
                    for n in moe3_units(part):
                        silu(q, n)

            prepare0()
            walk(head, tail, lambda q: None, turn, project, rest)

        @block.gpsimd
        def _(pool):
            g = nc.gpsimd
            g.memset(expo[:, :], -0.5).then_inc(exponent_set, 1)
            pool.wait_ge(exponent_set, 1)
            g.memset(vT0_rem, 0.0).then_inc(zeroed, 1)
            g.memset(ks[1][:, :, :, :], 0.0)

            chain = [0]

            def link(ins):
                chain[0] += 1
                ins.then_inc(pool_done, 1)
                pool.wait_ge(pool_done, chain[0])

            def split_keys(i):
                n = B * SK
                if i == 3:
                    for saved in parts_saved:
                        pool.wait_ge(saved, 16)
                rem = left[:, 0:n]
                g.tensor_copy(parts[:, 0, 0:n], rem).then_inc(split, 1)
                pool.wait_ge(split, 3 * STACKS["k", i] + 1)
                link(g.tensor_tensor(rem, rem, parts[:, 0, 0:n], ALU.subtract))
                g.tensor_copy(parts[:, 1, 0:n], rem).then_inc(split, 1)
                pool.wait_ge(split, 3 * STACKS["k", i] + 2)
                g.tensor_tensor(parts[:, 2, 0:n], rem, parts[:, 1, 0:n], ALU.subtract).then_inc(split, 1)

            def normalise(q, n):
                i = P_USE[q, n]
                pool.wait_ge(rsum_ready, P_READY.get(q, i + 1))
                p = probs[:, i % NP, :, :]
                g.tensor_tensor(p, p, rsums[:, i % NP, :].unsqueeze(1).broadcast_to([128, SK, 4]),
                                ALU.mult).then_inc(probs_ready, 1)

            def run_steps(events):
                for what, q, n in events:
                    if what == "normalise":
                        normalise(q, n)

            def stats_of(q):
                pool.wait_ge(eps_added, q + 1)
                g.tensor_tensor(rstd[:, :], vareps[:, :], expo[:, :], ALU.pow).then_inc(rstd_ready, 1)

            def add_quarters(q, first, last):
                for n in range(first, last):
                    tt, part = n // 4, n % 4
                    tile = TILES * (q % 2) + tt
                    if part in (0, 3):
                        continue
                    m = 3 * tile + part - 1
                    wait_s_read(pool, q, 4 * tt)
                    wait_s_read(pool, q, n)
                    if m > 0:
                        pool.wait_ge(acc_added, m)
                    g.tensor_tensor(acc0[:, tile % 2, :], acc0[:, tile % 2, :], mult0[:, m % 2, :],
                                    ALU.add).then_inc(acc_added, 1)

            def head(q):
                k = kind(q)
                if k == "attn":
                    run_steps(head_steps(q))
                elif k == "attn2":
                    normalise(q, 0)
                elif k == "moe0":
                    add_quarters(q, 0, 2)

            def tail(q):
                if kind(q) == "attn":
                    run_steps(tail_steps(q))

            def rest(q, part):
                if kind(q) == "attn":
                    run_steps(rest_steps(q, part))
                    if q == 1 and part == 2:
                        wait_t_full(pool, ("vr", 1))
                        pool.wait_ge(probs_ready, P_USE[1, 7] + 1)
                        pool.wait_ge(rstd_ready, 3)
                        for b in range(B):
                            g.memset(qs[b][96:128, :, :], 1.0).then_inc(ones_set, 1)
                            pool.wait_ge(ones_set, b + 1)
                elif kind(q) == "moe0":
                    if q == 2 and part == 0:
                        pool.wait_ge(o_full, O_USE[1, 1] + 1)
                        g.memset(vm[1][:, :, :, :], 0.0)
                        g.memset(ks[3][:, :, :, :], 0.0)
                        g.memset(vm[3][:, :, :, :], 0.0).then_inc(zeroed, 1)
                    units = rest_units(part)
                    add_quarters(q, units.start, units.stop)
                    if q == 2 and part < 2:
                        i = 2 * part + 1
                        wait_t_read(pool, ("k", i))
                        split_keys(i)

            stats_of(0)
            walk(head, tail, stats_of, lambda q: None, lambda q: None, rest)


def kernel(**inputs):
    import numpy as np
    import concourse.bacc as bacc
    from concourse.bass_utils import run_bass_kernel_spmd

    i = {k: np.asarray(v) for k, v in inputs.items()}

    def heads(w):
        return w.reshape(128, 8, 128)

    ctx_pad = np.zeros((128, B, KP), np.float32)
    ctx_pad[:, :, :SK] = i["ctx_1024"].transpose(2, 0, 1)
    const = np.concatenate([
        np.eye(128), (np.arange(128)[:, None] % 32 // 8 == np.arange(4)[None, :]),
        np.tile(np.arange(E0), (128, TILES)), np.tile(np.arange(E3), (128, TILES)), np.ones((128, 128)),
        np.arange(128)[:, None] % 4 == np.arange(4)[None, :],
        np.arange(128)[:, None] == np.arange(128)[None, :] // 8],
        axis=1).astype(np.float32)
    pair_sel = ((np.arange(3 * E3)[:, None, None] % E3 == 2 * np.arange(E3 // 2)[None, :, None]
                 + np.arange(128)[None, None, :] // 64) * 0x3F80).astype(np.uint16)

    def hidden_major(w, shared):
        both = np.concatenate([shared[None], w.reshape(E3 // 2, 128, 128)])
        return both.transpose(2, 0, 1)

    arrays = {
        "const": const, "pair_sel": pair_sel, "ctxT": ctx_pad,
        "x": i["x"].reshape(B * S, D),
        "wk0": heads(i["L0_xattn_Wk"]), "wv0": heads(i["L0_xattn_Wv"]),
        "wq0T": heads(i["L0_xattn_Wq"]).transpose(2, 1, 0),
        "wo0": i["L0_xattn_Wo"].reshape(8, 128, D).transpose(1, 0, 2),
        "routerT": i["L0_ffn_router_w"].T, "w_exp0": i["L0_ffn_expert_weights"].transpose(1, 0, 2),
        "sq": np.stack([i["L1_xattn_Wq"], i["L1_xattn_Wk"], i["L1_xattn_Wv"], i["L1_xattn_Wo"],
                        i["L2_xattn_Wq"].T, i["L2_xattn_Wk"].T, i["L2_xattn_Wv"].T, i["L2_ffn_weight"].T,
                        i["L3_xattn_q_w"].T, i["L3_xattn_k_w"].T, i["L3_xattn_v_w"].T], axis=1),
        "fside4": i["fside_Bx16xSxS2_0"], "phi": i["fside_BxSxS2_0"].reshape(B * S, SK),
        "mask1": i["mask_BxS2_bk0"].reshape(1, B * SK),
        "mask3": i["mask_BxS2_ik0"].reshape(1, B * SK),
        "cols": np.concatenate([
            np.stack([i[n] for n in ("L0_xattn_bo", "L1_xattn_bq", "L1_xattn_bk", "L2_xattn_bq", "L2_xattn_bk",
                                     "L3_xattn_q_b", "L3_xattn_k_b", "L3_ffn_sb1", "L3_ffn_sb3", "L3_ffn_sb2")],
                     axis=1),
            i["L1_ffn_b1"].reshape(4, 128).T, i["L3_ffn_b1"].reshape(8, 128).T, i["L3_ffn_b3"].reshape(8, 128).T],
            axis=1),
        "rows": np.concatenate([i[n] for n in ("L1_xattn_bv", "L1_xattn_bo", "L2_xattn_bv", "L3_xattn_v_b")])[None],
        "wide": np.concatenate([i["L2_ffn_bias"], i["L3_ffn_expert_bias"], i["g_xattn"], i["g_ffn"],
                                i["L2_xattn_beta_risk"].reshape(1), i["L2_xattn_beta_prio"].reshape(1),
                                i["L2_xattn_beta_impl"].reshape(1)])[None],
        "u1": i["L1_ffn_U1"], "v1": i["L1_ffn_V1"],
        "u2": i["L1_ffn_U2"].reshape(4, 128, 32).transpose(1, 0, 2),
        "v2b": np.concatenate([i["L1_ffn_V2"], i["L1_ffn_b2"][None]]),
        "gate3T": i["L3_ffn_gate_w"].T,
        "w1T": hidden_major(i["L3_ffn_w1"], i["L3_ffn_sw1"]),
        "w3T": hidden_major(i["L3_ffn_w3"], i["L3_ffn_sw3"]),
        "w2T": np.concatenate([i["L3_ffn_sw2"].T[None],
                               i["L3_ffn_w2"].transpose(0, 2, 1).reshape(E3 // 2, 128, D)]).transpose(1, 0, 2),
        "b2_exp": np.tile(i["L3_ffn_b2"], (3, 1)),
    }
    arrays = {f"in_{k}": np.ascontiguousarray(v) for k, v in arrays.items()}
    nc = bacc.Bacc("TRN2", target_bir_lowering=False, num_devices=1)
    t = {k[3:]: nc.dram_tensor(k, v.shape, mybir.dt.from_np(v.dtype), kind="ExternalInput").ap()
         for k, v in arrays.items()}
    t["parts"] = nc.dram_tensor("parts_scratch", (128, 3, HT), BF16, kind="Internal").ap()
    out = nc.dram_tensor("out_x", (B, S, D), F32, kind="ExternalOutput").ap()
    build(nc, t, out)
    r = run_bass_kernel_spmd(nc, [arrays], core_ids=[0])
    return r.results[0]["out_x"]
```
